# Optimizing a Trainium2 kernel written in Bass

```python
import numpy as np
import jax
import jax.numpy as jnp

def _softmax(x, axis=-1):
    return jax.nn.softmax(x, axis=axis)

def _gelu(x):
    return jax.nn.gelu(x, approximate=True)

def _silu(x):
    return jax.nn.silu(x)

def _sigmoid(x):
    return jax.nn.sigmoid(x)

def _layernorm(x, axis=-1, eps=1e-05):
    m = jnp.mean(x, axis=axis, keepdims=True)
    v = jnp.var(x, axis=axis, keepdims=True)
    return (x - m) / jnp.sqrt(v + eps)

def _scatter_add(tgt, idx, src, axis=0):
    return tgt.at[idx].add(src)

def _segment_sum(src, seg, n):
    return jax.ops.segment_sum(src, seg, n)
kernel_name = 'mk_perceiver_d1_seqx_r2_c684ec'

def setup_inputs(seed: int=0):
    np.random.seed(seed)
    _w = jnp.asarray

    def _rec_inputs():
        import jax
        import jax.numpy as jnp
        _rk = jax.random.key(seed)
        x = -0.0002928 + 1 * jax.random.normal(jax.random.fold_in(_rk, 1), (32, 32, 512), jnp.float32)
        _lenS = 32 - jax.random.randint(jax.random.fold_in(_rk, 7), (32,), 0, max(1, 32 // 4) + 1, jnp.int32)
        _lenS2 = 257 - jax.random.randint(jax.random.fold_in(_rk, 8), (32,), 0, max(1, 257 // 4) + 1, jnp.int32)
        _ctx_1024P = jax.random.normal(jax.random.fold_in(_rk, 11), (32, 16, 512), jnp.float32)
        _ctx_1024c = jax.random.dirichlet(jax.random.fold_in(_rk, 511), 0.3 * jnp.ones((16,), jnp.float32), (32, 257))
        _ctx_1024t = jnp.einsum('bsk,bkd->bsd', _ctx_1024c, _ctx_1024P)
        _ctx_1024t = _ctx_1024t * jax.lax.rsqrt(jnp.mean(jnp.square(_ctx_1024t)) + 1e-12) * 0.953939
        ctx_1024 = -1.39393e-06 + 0.999914 * (_ctx_1024t + 0.3 * jax.random.normal(jax.random.fold_in(_rk, 611), (32, 257, 512), jnp.float32))
        return (x, ctx_1024)
    x, ctx_1024 = _rec_inputs()

    def _L0_xattn_setup():
        import jax, jax.numpy as jnp
        import numpy as np
        D_MODEL = 512
        H = 16
        D_K = D_MODEL // H
        NEG = -1000000000.0

        def _softplus_t(x):
            return jnp.where(x > 20.0, x, jax.nn.softplus(x))
        key = jax.random.key(seed)
        ks = jax.random.split(key, 12)
        B, S = (2, 1024)
        sc = 1.0 / np.sqrt(D_MODEL)
        inp = {'query': jax.random.normal(ks[0], (B, S, D_MODEL), jnp.float32), 'key': jax.random.normal(ks[1], (B, S, D_MODEL), jnp.float32), 'value': jax.random.normal(ks[2], (B, S, D_MODEL), jnp.float32), 'Wq': jax.random.normal(ks[3], (D_MODEL, D_MODEL), jnp.float32) * sc, 'bq': jnp.zeros((D_MODEL,), jnp.float32), 'Wk': jax.random.normal(ks[4], (D_MODEL, D_MODEL), jnp.float32) * sc, 'bk': jnp.zeros((D_MODEL,), jnp.float32), 'Wv': jax.random.normal(ks[5], (D_MODEL, D_MODEL), jnp.float32) * sc, 'bv': jnp.zeros((D_MODEL,), jnp.float32), 'Wo': jax.random.normal(ks[6], (D_MODEL, D_MODEL), jnp.float32) * sc, 'bo': jnp.zeros((D_MODEL,), jnp.float32), 'raw_thresholds': jnp.full((H, 1, 1), 0.1, jnp.float32)}
        return inp
    _L0_xattn_all = _L0_xattn_setup()
    _L0_xattn_in = {k: v for k, v in _L0_xattn_all.items() if k in ('Wq', 'bq', 'Wk', 'bk', 'Wv', 'bv', 'Wo', 'bo', 'raw_thresholds')}
    del _L0_xattn_all

    def _L0_attn_setup():
        import jax, jax.numpy as jnp
        import numpy as np
        SCALE_BASE = 256
        EPS = 1e-06

        def xpos_apply(x, offset=0, downscale=False):
            L, d = (x.shape[-2], x.shape[-1])
            half = d // 2
            base = (jnp.arange(0, d, 2, dtype=jnp.float32) + 0.4 * d) / (1.4 * d)
            total = L + offset
            pos = jnp.arange(total, dtype=jnp.float32)
            scale = base[None, :] ** (pos[:, None] / SCALE_BASE)
            inv_freq = 1.0 / 10000.0 ** (jnp.arange(half, dtype=jnp.float32) / half)
            sinusoid = pos[:, None] * inv_freq[None, :]
            sin, cos = (jnp.sin(sinusoid), jnp.cos(sinusoid))
            scale, sin, cos = (scale[-L:], sin[-L:], cos[-L:])
            if downscale:
                scale = 1.0 / scale
            sin2 = jnp.repeat(sin * scale, 2, axis=-1)
            cos2 = jnp.repeat(cos * scale, 2, axis=-1)
            x1, x2 = (x[..., 0::2], x[..., 1::2])
            rot = jnp.stack([-x2, x1], axis=-1).reshape(x.shape)
            return x * cos2 + rot * sin2

        def layer_norm(x, s, b):
            mu = x.mean(-1, keepdims=True)
            var = ((x - mu) ** 2).mean(-1, keepdims=True)
            return (x - mu) / jnp.sqrt(var + EPS) * s + b

        def group_norm(h, scale, bias, n_heads):
            B, S, D = h.shape
            hg = h.reshape(B, S, n_heads, D // n_heads)
            mu = hg.mean(-1, keepdims=True)
            var = ((hg - mu) ** 2).mean(-1, keepdims=True)
            hn = ((hg - mu) / jnp.sqrt(var + EPS)).reshape(B, S, D)
            return hn * scale + bias

        def retention(xn, wq, wk, wv, gammas):
            B, S, _ = xn.shape
            q = xpos_apply(jnp.einsum('bsd,hde->bhse', xn, wq))
            k = xpos_apply(jnp.einsum('bsd,hde->bhse', xn, wk), downscale=True)
            v = jnp.einsum('bsd,hde->bhse', xn, wv)
            m = jnp.arange(S)
            diff = (m[:, None] - m[None, :]).astype(jnp.float32)
            decay = jnp.tril(gammas[:, None, None] ** diff[None])
            scores = jnp.einsum('bhse,bhte->bhst', q, k) * decay[None]
            out = jnp.einsum('bhst,bhte->bhse', scores, v)
            return out.transpose(0, 2, 1, 3).reshape(B, S, -1)
        key = jax.random.key(seed)
        L, H, D, F = (2, 8, 512, 2048)
        e = D // H
        B, S = (2, 1024)
        ks = jax.random.split(key, 8)
        f = jnp.float32
        return {'x': jax.random.normal(ks[0], (B, S, D), f), 'Wq': jax.random.normal(ks[1], (L, H, D, e), f) / D, 'Wk': jax.random.normal(ks[2], (L, H, D, e), f) / D, 'Wv': jax.random.normal(ks[3], (L, H, D, e), f) / D, 'Wg': jax.random.normal(ks[4], (L, D, D), f) / D, 'Wo': jax.random.normal(ks[5], (L, D, D), f) / D, 'gn_scale': jnp.ones((L, D), f), 'gn_bias': jnp.zeros((L, D), f), 'ln1_scale': jnp.ones((L, D), f), 'ln1_bias': jnp.zeros((L, D), f), 'ln2_scale': jnp.ones((L, D), f), 'ln2_bias': jnp.zeros((L, D), f), 'ffn_w1': jax.random.normal(ks[6], (L, D, F), f) * 0.02, 'ffn_w2': jax.random.normal(ks[7], (L, F, D), f) * 0.02}
    _L0_attn_all = _L0_attn_setup()
    _L0_attn_in = {k: v for k, v in _L0_attn_all.items() if k in ('Wq', 'Wk', 'Wv', 'Wg', 'Wo', 'gn_scale', 'gn_bias', 'ln1_scale', 'ln1_bias', 'ln2_scale', 'ln2_bias', 'ffn_w1', 'ffn_w2')}
    del _L0_attn_all

    def _L0_ffn_setup():
        import jax, jax.numpy as jnp
        import numpy as np
        from jax import lax
        DIM = 512
        HID = 1024
        E = 8
        K = 2
        B, T = (2, 256)
        key = jax.random.key(seed)
        ks = jax.random.split(key, 5)
        scale = 1.0 / np.sqrt(DIM)
        x = jax.random.normal(ks[0], (B, T, DIM), dtype=jnp.float32)
        router_w = jax.random.normal(ks[1], (E, DIM), dtype=jnp.float32) * scale
        w_gate = jax.random.normal(ks[2], (E, HID, DIM), dtype=jnp.float32) * scale
        w_up = jax.random.normal(ks[3], (E, HID, DIM), dtype=jnp.float32) * scale
        w_down = jax.random.normal(ks[4], (E, DIM, HID), dtype=jnp.float32) * (1.0 / np.sqrt(HID))
        return {'x': x, 'router_w': router_w, 'w_gate': w_gate, 'w_up': w_up, 'w_down': w_down}
    _L0_ffn_all = _L0_ffn_setup()
    _L0_ffn_in = {k: v for k, v in _L0_ffn_all.items() if k in ('router_w', 'w_gate', 'w_up', 'w_down')}
    del _L0_ffn_all
    return {'x': x, 'ctx_1024': ctx_1024, 'L0_xattn_Wq': _L0_xattn_in['Wq'], 'L0_xattn_bq': _L0_xattn_in['bq'], 'L0_xattn_Wk': _L0_xattn_in['Wk'], 'L0_xattn_bk': _L0_xattn_in['bk'], 'L0_xattn_Wv': _L0_xattn_in['Wv'], 'L0_xattn_bv': _L0_xattn_in['bv'], 'L0_xattn_Wo': _L0_xattn_in['Wo'], 'L0_xattn_bo': _L0_xattn_in['bo'], 'L0_xattn_raw_thresholds': _L0_xattn_in['raw_thresholds'], 'L0_attn_Wq': _L0_attn_in['Wq'], 'L0_attn_Wk': _L0_attn_in['Wk'], 'L0_attn_Wv': _L0_attn_in['Wv'], 'L0_attn_Wg': _L0_attn_in['Wg'], 'L0_attn_Wo': _L0_attn_in['Wo'], 'L0_attn_gn_scale': _L0_attn_in['gn_scale'], 'L0_attn_gn_bias': _L0_attn_in['gn_bias'], 'L0_attn_ln1_scale': _L0_attn_in['ln1_scale'], 'L0_attn_ln1_bias': _L0_attn_in['ln1_bias'], 'L0_attn_ln2_scale': _L0_attn_in['ln2_scale'], 'L0_attn_ln2_bias': _L0_attn_in['ln2_bias'], 'L0_attn_ffn_w1': _L0_attn_in['ffn_w1'], 'L0_attn_ffn_w2': _L0_attn_in['ffn_w2'], 'L0_ffn_router_w': _L0_ffn_in['router_w'], 'L0_ffn_w_gate': _L0_ffn_in['w_gate'], 'L0_ffn_w_up': _L0_ffn_in['w_up'], 'L0_ffn_w_down': _L0_ffn_in['w_down']}

def reference(x, ctx_1024, L0_xattn_Wq, L0_xattn_bq, L0_xattn_Wk, L0_xattn_bk, L0_xattn_Wv, L0_xattn_bv, L0_xattn_Wo, L0_xattn_bo, L0_xattn_raw_thresholds, L0_attn_Wq, L0_attn_Wk, L0_attn_Wv, L0_attn_Wg, L0_attn_Wo, L0_attn_gn_scale, L0_attn_gn_bias, L0_attn_ln1_scale, L0_attn_ln1_bias, L0_attn_ln2_scale, L0_attn_ln2_bias, L0_attn_ffn_w1, L0_attn_ffn_w2, L0_ffn_router_w, L0_ffn_w_gate, L0_ffn_w_up, L0_ffn_w_down):
    import jax
    import jax.numpy as jnp

    def _L0_xattn_ref(query, key, value, Wq, bq, Wk, bk, Wv, bv, Wo, bo, raw_thresholds):
        import jax, jax.numpy as jnp
        import numpy as np
        D_MODEL = 512
        H = 16
        D_K = D_MODEL // H
        NEG = -1000000000.0

        def _softplus_t(x):
            return jnp.where(x > 20.0, x, jax.nn.softplus(x))
        B, S, _ = query.shape

        def proj(x, W, b):
            return (x @ W.T + b).reshape(B, -1, H, D_K).transpose(0, 2, 1, 3)
        Q = proj(query, Wq, bq)
        K = proj(key, Wk, bk)
        V = proj(value, Wv, bv)
        scores = jnp.einsum('bhqd,bhkd->bhqk', Q, K) / jnp.sqrt(jnp.float32(D_K))
        thr = _softplus_t(raw_thresholds)[None]
        scores = jnp.where(scores <= thr, NEG, scores)
        attn = jax.nn.softmax(scores, axis=-1)
        x = jnp.einsum('bhqk,bhkd->bhqd', attn, V)
        x = x.transpose(0, 2, 1, 3).reshape(B, S, H * D_K)
        return x @ Wo.T + bo

    def _L0_attn_ref(x, Wq, Wk, Wv, Wg, Wo, gn_scale, gn_bias, ln1_scale, ln1_bias, ln2_scale, ln2_bias, ffn_w1, ffn_w2):
        import jax, jax.numpy as jnp
        import numpy as np
        SCALE_BASE = 256
        EPS = 1e-06

        def xpos_apply(x, offset=0, downscale=False):
            L, d = (x.shape[-2], x.shape[-1])
            half = d // 2
            base = (jnp.arange(0, d, 2, dtype=jnp.float32) + 0.4 * d) / (1.4 * d)
            total = L + offset
            pos = jnp.arange(total, dtype=jnp.float32)
            scale = base[None, :] ** (pos[:, None] / SCALE_BASE)
            inv_freq = 1.0 / 10000.0 ** (jnp.arange(half, dtype=jnp.float32) / half)
            sinusoid = pos[:, None] * inv_freq[None, :]
            sin, cos = (jnp.sin(sinusoid), jnp.cos(sinusoid))
            scale, sin, cos = (scale[-L:], sin[-L:], cos[-L:])
            if downscale:
                scale = 1.0 / scale
            sin2 = jnp.repeat(sin * scale, 2, axis=-1)
            cos2 = jnp.repeat(cos * scale, 2, axis=-1)
            x1, x2 = (x[..., 0::2], x[..., 1::2])
            rot = jnp.stack([-x2, x1], axis=-1).reshape(x.shape)
            return x * cos2 + rot * sin2

        def layer_norm(x, s, b):
            mu = x.mean(-1, keepdims=True)
            var = ((x - mu) ** 2).mean(-1, keepdims=True)
            return (x - mu) / jnp.sqrt(var + EPS) * s + b

        def group_norm(h, scale, bias, n_heads):
            B, S, D = h.shape
            hg = h.reshape(B, S, n_heads, D // n_heads)
            mu = hg.mean(-1, keepdims=True)
            var = ((hg - mu) ** 2).mean(-1, keepdims=True)
            hn = ((hg - mu) / jnp.sqrt(var + EPS)).reshape(B, S, D)
            return hn * scale + bias

        def retention(xn, wq, wk, wv, gammas):
            B, S, _ = xn.shape
            q = xpos_apply(jnp.einsum('bsd,hde->bhse', xn, wq))
            k = xpos_apply(jnp.einsum('bsd,hde->bhse', xn, wk), downscale=True)
            v = jnp.einsum('bsd,hde->bhse', xn, wv)
            m = jnp.arange(S)
            diff = (m[:, None] - m[None, :]).astype(jnp.float32)
            decay = jnp.tril(gammas[:, None, None] ** diff[None])
            scores = jnp.einsum('bhse,bhte->bhst', q, k) * decay[None]
            out = jnp.einsum('bhst,bhte->bhse', scores, v)
            return out.transpose(0, 2, 1, 3).reshape(B, S, -1)
        L, H = (Wq.shape[0], Wq.shape[1])
        gammas = 1.0 - 2.0 ** (-5.0 - jnp.arange(H, dtype=jnp.float32))
        for i in range(L):
            xn = layer_norm(x, ln1_scale[i], ln1_bias[i])
            heads = retention(xn, Wq[i], Wk[i], Wv[i], gammas)
            y = group_norm(heads, gn_scale[i], gn_bias[i], H)
            tmp = xn @ Wg[i]
            swish = tmp * jax.nn.sigmoid(tmp)
            x = swish * y @ Wo[i] + x
            xn2 = layer_norm(x, ln2_scale[i], ln2_bias[i])
            x = jax.nn.gelu(xn2 @ ffn_w1[i]) @ ffn_w2[i] + x
        return x

    def _L0_ffn_ref(x, router_w, w_gate, w_up, w_down):
        import jax, jax.numpy as jnp
        import numpy as np
        from jax import lax
        DIM = 512
        HID = 1024
        E = 8
        K = 2
        B, T = (2, 256)
        Bb, Tt, D = x.shape
        N = Bb * Tt
        xf = x.reshape(N, D)
        logits = xf @ router_w.T
        routing = jax.nn.softmax(logits, axis=-1)
        top_w, top_i = lax.top_k(routing, K)
        top_w = top_w / jnp.sum(top_w, axis=-1, keepdims=True)
        combine = jnp.zeros((N, E), dtype=x.dtype)
        combine = combine.at[jnp.arange(N)[:, None], top_i].add(top_w)
        g = jnp.einsum('nd,ehd->neh', xf, w_gate)
        u = jnp.einsum('nd,ehd->neh', xf, w_up)
        h = jax.nn.silu(g) * u
        y = jnp.einsum('neh,edh->ned', h, w_down)
        out = jnp.einsum('ned,ne->nd', y, combine)
        return out.reshape(Bb, Tt, D)
    x = x + _L0_xattn_ref(_layernorm(x, axis=-1), ctx_1024, ctx_1024, L0_xattn_Wq, L0_xattn_bq, L0_xattn_Wk, L0_xattn_bk, L0_xattn_Wv, L0_xattn_bv, L0_xattn_Wo, L0_xattn_bo, L0_xattn_raw_thresholds)
    x = x + _L0_attn_ref(_layernorm(x, axis=-1), L0_attn_Wq, L0_attn_Wk, L0_attn_Wv, L0_attn_Wg, L0_attn_Wo, L0_attn_gn_scale, L0_attn_gn_bias, L0_attn_ln1_scale, L0_attn_ln1_bias, L0_attn_ln2_scale, L0_attn_ln2_bias, L0_attn_ffn_w1, L0_attn_ffn_w2)
    x = x + _L0_ffn_ref(_layernorm(x, axis=-1), L0_ffn_router_w, L0_ffn_w_gate, L0_ffn_w_up, L0_ffn_w_down)
    return x

_drawn_inputs = setup_inputs


def setup_inputs(seed=0):
    import zlib

    import numpy as np

    out = dict(_drawn_inputs(seed))
    spreads = {'L0_xattn_bq': (0.0, 0.1),
     'L0_xattn_bk': (0.0, 0.1),
     'L0_xattn_bv': (0.0, 0.1),
     'L0_xattn_bo': (0.0, 0.1),
     'L0_xattn_raw_thresholds': (0.10000000149011612, 0.2),
     'L0_attn_gn_scale': (1.0, 0.6),
     'L0_attn_gn_bias': (0.0, 0.8),
     'L0_attn_ln1_scale': (1.0, 0.6),
     'L0_attn_ln1_bias': (0.0, 0.8),
     'L0_attn_ln2_scale': (1.0, 0.2),
     'L0_attn_ln2_bias': (0.0, 0.389)}
    factors = {'L0_attn_Wq': 8.0,
     'L0_attn_Wk': 8.0,
     'L0_attn_Wv': 7.977,
     'L0_attn_Wg': 8.0,
     'L0_attn_Wo': 8.0}
    for name, (base, spread) in spreads.items():
        noise = np.random.default_rng([zlib.crc32(name.encode()), seed]).standard_normal(out[name].shape)
        drawn = base * np.exp(spread * noise) if base else spread * noise
        out[name] = jnp.asarray(drawn.astype(out[name].dtype))
    for name, factor in factors.items():
        out[name] = (out[name] * factor).astype(out[name].dtype)
    return out
```

```python
from contextlib import ExitStack

import numpy as np
import concourse.bass as bass
from concourse import mybir

F32 = mybir.dt.float32
F32R = mybir.dt.float32r
I32 = mybir.dt.int32
U32 = mybir.dt.uint32
ALU = mybir.AluOpType
ACT = mybir.ActivationFunctionType
AX = mybir.AxisListType

P = 128
D = 512
DC = D // P
NB, S = 32, 32
TOK = NB * S
NT = TOK // P
BPT = P // S
SK = 257
SKE = SK + 1
XH = 16
XD = D // XH
HPC = P // XD
L, H, E = 2, 8, 64
F = 2048
FC = F // P
NE, HID = 8, 1024
GT = 256
NG = (2 * TOK - NE) // GT + NE
SLOTS = NG * GT
PIECES = 6
NEG_HUGE = -3.0e38
INV_SQRT_XD = float(1.0 / np.sqrt(np.float32(XD)))

PARTS = [(0, 0), (0, 1), (1, 0)]

VEC = {"bq": 0, "bk": 4, "bv": 8, "thr": 12, "head": 16}
NVEC = 20


def r(ap):
    return ap.bitcast(F32)


def wait_alone(eng, semaphore, value):
    value = eng.compute_val(value)
    eng.wait_ge(semaphore, 1)
    eng.wait_ge(semaphore, value)


def products(nc, out, terms, lhs, rhs):
    steps = [(t, a, b) for t in terms for a, b in PARTS]
    for n, (t, a, b) in enumerate(steps):
        last = nc.tensor.matmul(out, lhs(t, a), rhs(t, b), start=n == 0, stop=n == len(steps) - 1)
    return last


def build(nc, a, out, dbg=None):
    with ExitStack() as whole:
        def holder(stack):
            def sb(name, shape, dt=F32):
                return stack.enter_context(nc.sbuf_tensor(name, shape, dt))
            return sb

        taken = []

        def sem(name):
            taken.append(nc.alloc_semaphore(name))
            return taken[-1]

        def end_phase():
            nc.clear_and_free_semaphores(list(taken))
            nc.all_engine_barrier()
            taken.clear()

        keep = holder(whole)
        bank = [whole.enter_context(nc.psum_tensor(f"bank{i}", [P, 512], F32)) for i in range(8)]
        X = keep("X", [P, NT, D])
        ident = keep("ident", [P, P])
        vec = keep("vec", [P, NVEC])
        mhalf = keep("mhalf", [P, 64])
        cross_attention(nc, a, whole, holder, sem, bank, X, ident, vec, mhalf)
        end_phase()
        A = keep("A", [P, NT, D])
        if dbg != "x1":
            xg = nc.dram_tensor("xg", (SLOTS, D), F32).ap()
            yg = nc.dram_tensor("yg", (SLOTS, D), F32).ap()
            retention_layers(nc, a, whole, holder, sem, bank, X, A, ident, vec, mhalf, xg)
            end_phase()
            if dbg is None or dbg == "x3":
                mixture(nc, a, out, whole, holder, sem, bank, X, A, ident, mhalf, xg, yg)
                return
            done = sem("dbg_done")
            with nc.Block() as block:
                @block.sync
                def _(sp):
                    sp.dma_start(out.rearrange("(t p) d -> p t d", p=P), A[:, :, :]).then_inc(done, 16)
                    sp.wait_ge(done, 16)
            return
        if dbg == "x1":
            done = sem("dbg_done")
            with nc.Block() as block:
                @block.sync
                def _(sp):
                    sp.dma_start(out.rearrange("(t p) d -> p t d", p=P), X[:, :, :]).then_inc(done, 16)
                    sp.wait_ge(done, 16)
            return


def cross_attention(nc, a, whole, holder, sem, bank, X, ident, vec, mhalf):
    def col(name, c=0):
        return vec[:, VEC[name] + c:VEC[name] + c + 1]

    with ExitStack() as phase:
        sb = holder(phase)
        wk = sb("wk", [P, 2, DC, D], F32R)
        wv = sb("wv", [P, 2, DC, D], F32R)
        wo = sb("wo", [P, 2, DC, D], F32R)
        qT = sb("qT", [P, 2, DC, TOK], F32R)
        vlast = sb("vlast", [P, 2, D], F32R)
        thr = sb("thr", [P, DC])
        bo_bc = sb("bo_bc", [P, D])
        eye32 = sb("eye32", [P, NB, 32])

        with ExitStack() as inner:
            sbi = holder(inner)
            xT = sbi("xT", [P, 2, DC, TOK], F32R)
            raw = [sbi(f"raw{i}", [P, DC, D]) for i in range(3)]
            wq = sbi("wq", [P, 2, DC, D], F32R)
            craw = sbi("craw", [P, DC, P])
            cl = sbi("cl", [P, 2, DC, P], F32R)
            stats = sbi("stats", [P, NT, 6])
            mv = sbi("mv", [P, NT, 2])
            veps = sbi("veps", [P, NT])
            rstd = sbi("rstd", [P, NT])
            xh = sbi("xh", [P, 2, D])
            qf = sbi("qf", [P, 2, 512])
            th = sbi("th", [P, 5, DC])
            x_in = [sem(f"x_in{i}") for i in range(2)]
            vec_in, id_in, cl_in, misc_in = sem("vec_in"), sem("id_in"), sem("cl_in"), sem("misc_in")
            w_in = [sem(f"w_in{i}") for i in range(4)]
            half_set, x_stats, x_aggr, veps_ok, rstd_ok = sem("half_set"), sem("x_stats"), sem("x_aggr"), sem("veps_ok"), sem("rstd_ok")
            xh_ok, x_turned, xT_hi, xT_lo = sem("xh_ok"), sem("x_turned"), sem("xT_hi"), sem("xT_lo")
            w_hi, w_lo, cl_hi, cl_lo = sem("w_hi"), sem("w_lo"), sem("cl_hi"), sem("cl_lo")
            q_ps, q_f, q_hi, q_lo = sem("q_ps"), sem("q_f"), sem("q_hi"), sem("q_lo")
            vl_ps, vl_hi, vl_lo = sem("vl_ps"), sem("vl_hi"), sem("vl_lo")
            th_act, th_dve = sem("th_act"), sem("th_dve")
            weights = [(a["xwq"], wq), (a["xwv"], wv), (a["xwk"], wk), (a["xwo"], wo)]
            with nc.Block() as block:
                @block.sync
                def _(sp):
                    xv = a["x"].rearrange("(t p) d -> p t d", p=P)
                    for i in range(2):
                        sp.dma_start(X[:, 4 * i:4 * i + 4, :], xv[:, 4 * i:4 * i + 4, :]).then_inc(x_in[i], 16)
                        if i == 0:
                            sp.dma_start(ident[:, :], a["ident"]).then_inc(id_in, 16)
                            sp.dma_start(vec[:, :], a["vec"]).then_inc(vec_in, 16)
                            sp.dma_start(raw[0][:, :, :], weights[0][0]).then_inc(w_in[0], 16)
                    sp.dma_start(craw[:, :, :], a["ctx_last"]).then_inc(cl_in, 16)
                    for i in (1, 2):
                        sp.dma_start(raw[i][:, :, :], weights[i][0]).then_inc(w_in[i], 16)
                    sp.dma_start(bo_bc[:, :], a["bo_bc"]).then_inc(misc_in, 16)
                    sp.dma_start(eye32[:, :, :], a["eye32"]).then_inc(misc_in, 16)
                    sp.wait_ge(w_hi, 1)
                    sp.wait_ge(w_lo, 1)
                    sp.dma_start(raw[0][:, :, :], weights[3][0]).then_inc(w_in[3], 16)
                    sp.wait_ge(misc_in, 32)

                @block.gpsimd
                def _(pool):
                    nc.gpsimd.memset(mhalf[:, :], -0.5).then_inc(half_set, 1)
                    pool.wait_ge(half_set, 1)
                    pool.wait_ge(veps_ok, 1)
                    nc.gpsimd.tensor_tensor(rstd[:, :], veps[:, :], mhalf[:, 0:NT], ALU.pow).then_inc(rstd_ok, 1)

                @block.vector
                def _(dve):
                    for t in range(NT):
                        dve.wait_ge(x_in[t // 4], 16)
                        nc.vector.bn_stats(stats[:, t, :], X[:, t, :]).then_inc(x_stats, 1)
                    for t in range(NT):
                        dve.wait_ge(x_stats, t + 1)
                        nc.vector.bn_aggr(mv[:, t, :], stats[:, t, :]).then_inc(x_aggr, 1)
                    dve.wait_ge(x_aggr, NT)
                    nc.vector.tensor_scalar(veps[:, :], mv[:, :, 1], 1e-5, None, ALU.add).then_inc(veps_ok, 1)
                    dve.wait_ge(w_hi, 1)
                    nc.vector.tensor_tensor(wq[:, 1, :, :], raw[0][:, :, :], r(wq[:, 0, :, :]), ALU.subtract).then_inc(w_lo, 1)
                    dve.wait_ge(rstd_ok, 1)

                    def turned_lo(t):
                        dve.wait_ge(xT_hi, t + 1)
                        nc.vector.tensor_tensor(xT[:, 1, :, t * P:(t + 1) * P], bank[t % 2][:, :].rearrange("p (c n) -> p c n", c=DC),
                                                r(xT[:, 0, :, t * P:(t + 1) * P]), ALU.subtract).then_inc(xT_lo, 1)
                    for t in range(NT):
                        if t >= 2:
                            dve.wait_ge(x_turned, t - 1)
                        nc.vector.tensor_scalar(xh[:, t % 2, :], X[:, t, :], mv[:, t, 0:1], rstd[:, t:t + 1],
                                                ALU.subtract, ALU.mult).then_inc(xh_ok, 1)
                        if t >= 1:
                            turned_lo(t - 1)
                    turned_lo(NT - 1)
                    for i in (1, 2):
                        dve.wait_ge(w_hi, i + 1)
                        nc.vector.tensor_tensor(weights[i][1][:, 1, :, :], raw[i][:, :, :], r(weights[i][1][:, 0, :, :]), ALU.subtract).then_inc(w_lo, 1)
                        if i == 1:
                            dve.wait_ge(cl_hi, 1)
                            nc.vector.tensor_tensor(cl[:, 1, :, :], craw[:, :, :], r(cl[:, 0, :, :]), ALU.subtract).then_inc(cl_lo, 1)
                        for n in range(4 * i - 4, 4 * i):
                            dc, half = n // 2, n % 2
                            dve.wait_ge(q_hi, n + 1)
                            hi = qT[:, 0, dc, half * 512:(half + 1) * 512]
                            nc.vector.scalar_tensor_tensor(qT[:, 1, dc, half * 512:(half + 1) * 512], bank[2 + n % 2][:, :], col("bq", dc),
                                                           r(hi), ALU.add, ALU.subtract).then_inc(q_lo, 1)
                    dve.wait_ge(w_hi, 4)
                    nc.vector.tensor_tensor(wo[:, 1, :, :], raw[0][:, :, :], r(wo[:, 0, :, :]), ALU.subtract).then_inc(w_lo, 1)
                    dve.wait_ge(vl_hi, 1)
                    nc.vector.tensor_tensor(vlast[:, 1, :], bank[4][:, :], r(vlast[:, 0, :]), ALU.subtract).then_inc(vl_lo, 1)
                    dve.wait_ge(vec_in, 16)
                    raw_thr = vec[:, VEC["thr"]:VEC["thr"] + DC]
                    nc.vector.scalar_tensor_tensor(th[:, 0, :], raw_thr, -1.0, raw_thr, ALU.mult, ALU.max).then_inc(th_dve, 1)
                    nc.vector.tensor_scalar(th[:, 1, :], raw_thr, 0.0, None, ALU.max).then_inc(th_dve, 1)
                    dve.wait_ge(th_act, 2)
                    dve.wait_ge(th_dve, 2)
                    nc.vector.tensor_tensor(th[:, 4, :], th[:, 1, :], th[:, 3, :], ALU.add).then_inc(th_dve, 1)
                    dve.wait_ge(th_dve, 3)
                    nc.vector.tensor_scalar(thr[:, :], th[:, 4, :], float(np.sqrt(np.float32(XD))), None, ALU.mult).then_inc(th_dve, 1)

                @block.scalar
                def _(act):
                    act.wait_ge(w_in[0], 16)
                    nc.scalar.activation(wq[:, 0, :, :], raw[0][:, :, :], ACT.Copy).then_inc(w_hi, 1)
                    act.wait_ge(cl_in, 16)
                    nc.scalar.activation(cl[:, 0, :, :], craw[:, :, :], ACT.Copy).then_inc(cl_hi, 1)
                    act.wait_ge(w_in[1], 16)
                    nc.scalar.activation(wv[:, 0, :, :], raw[1][:, :, :], ACT.Copy).then_inc(w_hi, 1)
                    for t in range(NT):
                        act.wait_ge(x_turned, t + 1)
                        nc.scalar.activation(xT[:, 0, :, t * P:(t + 1) * P], bank[t % 2][:, :].rearrange("p (c n) -> p c n", c=DC),
                                             ACT.Copy).then_inc(xT_hi, 1)
                    act.wait_ge(w_in[2], 16)
                    nc.scalar.activation(wk[:, 0, :, :], raw[2][:, :, :], ACT.Copy).then_inc(w_hi, 1)
                    act.wait_ge(vec_in, 16)
                    for n in range(8):
                        dc, half = n // 2, n % 2
                        act.wait_ge(q_ps, n + 1)
                        nc.scalar.activation(qT[:, 0, dc, half * 512:(half + 1) * 512], bank[2 + n % 2][:, :], ACT.Identity,
                                             bias=col("bq", dc)).then_inc(q_hi, 1)
                    act.wait_ge(w_in[3], 16)
                    nc.scalar.activation(wo[:, 0, :, :], raw[0][:, :, :], ACT.Copy).then_inc(w_hi, 1)
                    act.wait_ge(vl_ps, 1)
                    nc.scalar.activation(vlast[:, 0, :], bank[4][:, :], ACT.Copy).then_inc(vl_hi, 1)
                    act.wait_ge(th_dve, 1)
                    nc.scalar.activation(th[:, 2, :], th[:, 0, :], ACT.Exp, scale=-1.0).then_inc(th_act, 1)
                    act.wait_ge(th_act, 1)
                    nc.scalar.activation(th[:, 3, :], th[:, 2, :], ACT.Ln, bias=1.0).then_inc(th_act, 1)

                @block.tensor
                def _(pe):
                    pe.wait_ge(id_in, 16)
                    for t in range(NT):
                        pe.wait_ge(xh_ok, t + 1)
                        if t >= 2:
                            pe.wait_ge(xT_hi, t - 1)
                            pe.wait_ge(xT_lo, t - 1)
                        for c in range(DC):
                            last = nc.tensor.transpose(bank[t % 2][:, c * P:(c + 1) * P], xh[:, t % 2, c * P:(c + 1) * P], ident[:, :])
                        last.then_inc(x_turned, 1)
                    pe.wait_ge(w_lo, 1)
                    pe.wait_ge(xT_lo, NT)
                    for n in range(8):
                        dc, half = n // 2, n % 2
                        if n >= 2:
                            pe.wait_ge(q_lo, n - 1)
                        products(nc, bank[2 + n % 2][:, :], range(DC), lambda c, h: wq[:, h, c, dc * P:(dc + 1) * P],
                                 lambda c, h: xT[:, h, c, half * 512:(half + 1) * 512]).then_inc(q_ps, 1)
                    pe.wait_ge(w_lo, 2)
                    pe.wait_ge(cl_lo, 1)
                    products(nc, bank[4][:, :], range(DC), lambda c, h: cl[:, h, c, :], lambda c, h: wv[:, h, c, :]).then_inc(vl_ps, 1)

        with ExitStack() as inner:
            sbi = holder(inner)
            craw = [sbi(f"ctxraw{i}", [P, DC, SK]) for i in range(2)]
            ctx = [sbi(f"ctx{i}", [P, 2, DC, SKE], F32R) for i in range(2)]
            kT = sbi("kT", [P, 2, DC, SKE], F32R)
            v = [sbi(f"v{i}", [P, 2, 2, D], F32R) for i in range(2)]
            qbd = sbi("qbd", [P, 2, DC, P], F32R)
            u = sbi("u", [P, DC, SKE])
            ex = sbi("ex", [P, DC, SKE])
            pr = sbi("pr", [P, DC, SKE])
            umax = sbi("umax", [P, DC])
            keepany = sbi("keepany", [P, DC])
            sc = sbi("sc", [P, DC])
            nb = sbi("nb", [P, DC])
            floor = sbi("floor", [P, DC])
            psums = sbi("psums", [P, DC])
            rsum = sbi("rsum", [P, DC])
            plast = sbi("plast", [P, DC, 32])
            pT = sbi("pT", [P, 2, 2, DC, P], F32R)
            pTl = sbi("pTl", [32, 2, DC, P], F32R)
            oT = sbi("oT", [P, DC, P])
            oT_hl = sbi("oT_hl", [P, 2, DC, P], F32R)
            ctx_in = [sem("ctx_in0"), sem("ctx_in1")]
            zeroed, ctx_hi, ctx_lo = sem("zeroed"), sem("ctx_hi"), sem("ctx_lo")
            k_ps, v_ps, s_ps, p_turned, pv_ps, o_ps = (sem(n) for n in ("k_ps", "v_ps", "s_ps", "p_turned", "pv_ps", "o_ps"))
            k_hi, k_lo, v_hi, v_lo = (sem(n) for n in ("k_hi", "k_lo", "v_hi", "v_lo"))
            u_ok, soft_ok, ex_ok, pr_ok, rsum_ok, pn_ok, plast_ok = (
                sem(n) for n in ("u_ok", "soft_ok", "ex_ok", "pr_ok", "rsum_ok", "pn_ok", "plast_ok"))
            pT_hi, pT_lo, oT_ok, oT_hi, oT_lo, x1_sum, x1_ok = (
                sem(n) for n in ("pT_hi", "pT_lo", "oT_ok", "oT_hi", "oT_lo", "x1_sum", "x1_ok"))
            qbd_ok = sem("qbd_ok")
            ctx_view = a["ctx"]

            with nc.Block() as block:
                @block.sync
                def _(sp):
                    def load(it, k):
                        b = BPT * it + k
                        sp.dma_start(craw[k % 2][:, :, :], ctx_view[bass.ds(b, 1), :, :].rearrange("o p (c n) -> p (o c) n", c=DC)).then_inc(ctx_in[k % 2], 16)
                    for k in range(BPT):
                        if k >= 2:
                            sp.wait_ge(ctx_hi, k - 1)
                            sp.wait_ge(ctx_lo, k - 1)
                        load(0, k)
                    with sp.Fori(1, NT) as it:
                        for k in range(BPT):
                            sp.wait_ge(ctx_hi, BPT * it + k - 1)
                            sp.wait_ge(ctx_lo, BPT * it + k - 1)
                            load(it, k)

                @block.gpsimd
                def _(pool):
                    for i in range(2):
                        nc.gpsimd.memset(r(ctx[i][:, :, :, SK:SKE]), 0.0).then_inc(zeroed, 1)

                    def context_lo(it, k, b):
                        pool.wait_ge(ctx_hi, b + 1)
                        nc.gpsimd.tensor_tensor(ctx[k % 2][:, 1, :, 0:SK], craw[k % 2][:, :, :], r(ctx[k % 2][:, 0, :, 0:SK]),
                                                ALU.subtract).then_inc(ctx_lo, 1)

                    def spread_q(b):
                        src = r(qT[:, :, :, :]).rearrange("p h c n -> p (h c) n")[:, :, bass.ds(b * S, S)]
                        nc.gpsimd.tensor_tensor(qbd[:, :, :, :].rearrange("p h c (g n) -> p (h c) g n", g=HPC),
                                                src.unsqueeze(2).broadcast_to([P, 2 * DC, HPC, S]),
                                                vec[:, VEC["head"]:VEC["head"] + HPC].unsqueeze(1).unsqueeze(3).broadcast_to([P, 2 * DC, HPC, S]),
                                                ALU.mult).then_inc(qbd_ok, 1)

                    def normalise(it, k):
                        b = BPT * it + k
                        pool.wait_ge(rsum_ok, b + 1)
                        nc.gpsimd.tensor_tensor(pr[:, :, 0:SK], pr[:, :, 0:SK], rsum[:, :].unsqueeze(2).broadcast_to([P, DC, SK]),
                                                ALU.mult).then_inc(pn_ok, 1)
                        pool.wait_ge(pn_ok, b + 1)
                        nc.gpsimd.tensor_tensor(plast[:, :, :], pr[:, :, SK - 1:SK].broadcast_to([P, DC, 32]),
                                                eye32[:, bass.ds(b, 1), :].broadcast_to([P, DC, 32]), ALU.mult).then_inc(plast_ok, 1)

                    def body(it, first, last):
                        for k in range(BPT):
                            b = BPT * it + k
                            if not (first and k == 0):
                                normalise(it, k - 1)
                                pool.wait_ge(s_ps, DC * b)
                            spread_q(b)
                            if not (last and k == BPT - 1):
                                if not (first and k == 0):
                                    pool.wait_ge(v_ps, 2 * b)
                                context_lo(it, k + 1, b + 1)
                            if k == 2 and not first:
                                add_bias(it - 1)

                    def add_bias(t):
                        pool.wait_ge(x1_sum, t + 1)
                        xt = X[:, bass.ds(t, 1), :].rearrange("p o d -> p (o d)")
                        nc.gpsimd.tensor_tensor(xt, xt, bo_bc[:, :], ALU.add).then_inc(x1_ok, 1)
                    context_lo(0, 0, 0)
                    body(0, True, False)
                    with pool.Fori(1, NT - 1) as it:
                        body(it, False, False)
                    body(NT - 1, False, True)
                    normalise(NT - 1, BPT - 1)
                    add_bias(NT - 1)

                @block.scalar
                def _(act):
                    def context_hi(k, use, b):
                        act.wait_ge(ctx_in[k % 2], 16 * use)
                        nc.scalar.activation(ctx[k % 2][:, 0, :, 0:SK], craw[k % 2][:, :, :], ACT.Copy).then_inc(ctx_hi, 1)

                    def exps(b, cs):
                        for c in cs:
                            act.wait_ge(soft_ok, 5 * b + 5)
                            nc.scalar.activation(ex[:, c, 0:SK], u[:, c, 0:SK], ACT.Exp, bias=nb[:, c:c + 1], scale=sc[:, c:c + 1]).then_inc(ex_ok, 1)

                    def turned(b):
                        for kt in range(2):
                            act.wait_ge(p_turned, 3 * b + kt + 1)
                            nc.scalar.activation(pT[:, 0, kt, :, :], bank[4 + kt][:, :].rearrange("p (c n) -> p c n", c=DC), ACT.Copy).then_inc(pT_hi, 1)
                        act.wait_ge(p_turned, 3 * b + 3)
                        nc.scalar.activation(pTl[:, 0, :, :], bank[6][0:32, :].rearrange("p (c n) -> p c n", c=DC), ACT.Copy).then_inc(pT_hi, 1)

                    def heads_hi(t):
                        act.wait_ge(oT_ok, HPC * BPT * (t + 1))
                        nc.scalar.activation(oT_hl[:, 0, :, :], oT[:, :, :], ACT.Copy).then_inc(oT_hi, 1)

                    def body(it, first, last):
                        for k in range(BPT):
                            b = BPT * it + k
                            begin = first and k == 0
                            if not begin:
                                exps(b - 1, (0, 1))
                            else:
                                act.wait_ge(zeroed, 2)
                            for dc in range(DC):
                                act.wait_ge(k_ps, DC * b + dc + 1)
                                nc.scalar.activation(kT[:, 0, dc, :], bank[dc % 2][:, 0:SKE], ACT.Identity, bias=col("bk", dc)).then_inc(k_hi, 1)
                                if dc == 0 and not begin:
                                    exps(b - 1, (2, 3))
                            if not begin:
                                turned(b - 1)
                            if not (last and k == BPT - 1):
                                context_hi(k + 1, 2 * it + (k + 1) // 2 + 1, b + 1)
                            for kt in range(2):
                                act.wait_ge(v_ps, 2 * b + kt + 1)
                                nc.scalar.activation(v[k % 2][:, 0, kt, :], bank[kt][:, :], ACT.Copy).then_inc(v_hi, 1)
                            if k == 0 and not first:
                                heads_hi(it - 1)
                    context_hi(0, 1, 0)
                    body(0, True, False)
                    with act.Fori(1, NT - 1) as it:
                        body(it, False, False)
                    body(NT - 1, False, True)
                    exps(NB - 1, range(DC))
                    turned(NB - 1)
                    heads_hi(NT - 1)

                @block.vector
                def _(dve):
                    def weigh(b, cs):
                        for c in cs:
                            dve.wait_ge(ex_ok, DC * b + c + 1)
                            nc.vector.scalar_tensor_tensor(pr[:, c, 0:SK], u[:, c, 0:SK], floor[:, c:c + 1], ex[:, c, 0:SK],
                                                           ALU.is_gt, ALU.mult, accum_out=psums[:, c:c + 1]).then_inc(pr_ok, 1)

                    def reciprocal(b):
                        dve.wait_ge(pr_ok, DC * (b + 1))
                        nc.vector.reciprocal(rsum[:, :], psums[:, :]).then_inc(rsum_ok, 1)

                    def turned_lo(b):
                        for kt in range(2):
                            dve.wait_ge(pT_hi, 3 * b + kt + 1)
                            nc.vector.tensor_tensor(pT[:, 1, kt, :, :], bank[4 + kt][:, :].rearrange("p (c n) -> p c n", c=DC),
                                                    r(pT[:, 0, kt, :, :]), ALU.subtract).then_inc(pT_lo, 1)
                        dve.wait_ge(pT_hi, 3 * b + 3)
                        nc.vector.tensor_tensor(pTl[:, 1, :, :], bank[6][0:32, :].rearrange("p (c n) -> p c n", c=DC),
                                                r(pTl[:, 0, :, :]), ALU.subtract).then_inc(pT_lo, 1)

                    def threshold(b, cs):
                        for c in cs:
                            dve.wait_ge(s_ps, DC * b + c + 1)
                            nc.vector.tensor_scalar(u[:, c, 0:SK], bank[2 + c % 2][:, 0:SK], thr[:, c:c + 1], None,
                                                    ALU.subtract, ALU.max, accum_out=umax[:, c:c + 1]).then_inc(u_ok, 1)

                    def heads(k, b):
                        dve.wait_ge(pv_ps, b + 1)
                        for g in range(HPC):
                            rows = slice(g * XD, (g + 1) * XD)
                            nc.vector.tensor_tensor(oT[rows, :, k * S:(k + 1) * S],
                                                    bank[7][rows, :].rearrange("p (c n) -> p c n", c=DC)[:, :, g * S:(g + 1) * S],
                                                    vec[rows, VEC["bv"]:VEC["bv"] + DC].unsqueeze(2).broadcast_to([XD, DC, S]),
                                                    ALU.add).then_inc(oT_ok, 1)

                    def softmax_terms(b):
                        n = 5 * b
                        dve.wait_ge(u_ok, DC * b + DC)
                        nc.vector.tensor_scalar(keepany[:, :], umax[:, :], 0.0, None, ALU.is_gt).then_inc(soft_ok, 1)
                        nc.vector.tensor_scalar(floor[:, :], umax[:, :], 0.0, NEG_HUGE, ALU.is_le, ALU.mult).then_inc(soft_ok, 1)
                        dve.wait_ge(soft_ok, n + 2)
                        nc.vector.tensor_scalar(sc[:, :], keepany[:, :], INV_SQRT_XD, None, ALU.mult).then_inc(soft_ok, 1)
                        dve.wait_ge(soft_ok, n + 3)
                        nc.vector.tensor_tensor(nb[:, :], sc[:, :], umax[:, :], ALU.mult).then_inc(soft_ok, 1)
                        dve.wait_ge(soft_ok, n + 4)
                        nc.vector.tensor_scalar(nb[:, :], nb[:, :], -1.0, None, ALU.mult).then_inc(soft_ok, 1)

                    def project_lo(t):
                        dve.wait_ge(oT_hi, t + 1)
                        nc.vector.tensor_tensor(oT_hl[:, 1, :, :], oT[:, :, :], r(oT_hl[:, 0, :, :]), ALU.subtract).then_inc(oT_lo, 1)

                    def add_x(t):
                        dve.wait_ge(o_ps, t + 1)
                        xt = X[:, bass.ds(t, 1), :].rearrange("p o d -> p (o d)")
                        nc.vector.tensor_tensor(xt, bank[7][:, :], xt, ALU.add).then_inc(x1_sum, 1)

                    def body(it, first):
                        for k in range(BPT):
                            b = BPT * it + k
                            begin = first and k == 0
                            for dc in range(DC):
                                dve.wait_ge(k_hi, DC * b + dc + 1)
                                nc.vector.scalar_tensor_tensor(kT[:, 1, dc, :], bank[dc % 2][:, 0:SKE], col("bk", dc), r(kT[:, 0, dc, :]),
                                                               ALU.add, ALU.subtract).then_inc(k_lo, 1)
                                if not begin and dc == 0:
                                    weigh(b - 1, (0, 1))
                                if not begin and dc == 1:
                                    weigh(b - 1, (2, 3))
                                    reciprocal(b - 1)
                            if k == 1 and not first:
                                add_x(it - 1)
                            if not begin:
                                turned_lo(b - 1)
                            for kt in range(2):
                                dve.wait_ge(v_hi, 2 * b + kt + 1)
                                nc.vector.tensor_tensor(v[k % 2][:, 1, kt, :], bank[kt][:, :], r(v[k % 2][:, 0, kt, :]), ALU.subtract).then_inc(v_lo, 1)
                                if kt == 0 and not begin:
                                    heads((k - 1) % BPT, b - 1)
                                threshold(b, (2 * kt, 2 * kt + 1))
                            softmax_terms(b)
                            if k == 0 and not first:
                                project_lo(it - 1)
                    body(0, True)
                    with dve.Fori(1, NT) as it:
                        body(it, False)
                    weigh(NB - 1, range(DC))
                    reciprocal(NB - 1)
                    turned_lo(NB - 1)
                    heads(BPT - 1, NB - 1)
                    project_lo(NT - 1)
                    add_x(NT - 1)

                @block.tensor
                def _(pe):
                    def turn(b):
                        pe.wait_ge(pn_ok, b + 1)
                        for kt in range(2):
                            for c in range(DC):
                                last = nc.tensor.transpose(bank[4 + kt][:, c * P:(c + 1) * P], pr[:, c, kt * P:(kt + 1) * P], ident[:, :])
                            last.then_inc(p_turned, 1)
                        pe.wait_ge(plast_ok, b + 1)
                        for c in range(DC):
                            last = nc.tensor.transpose(bank[6][0:32, c * P:(c + 1) * P], plast[:, c, :], ident[:, :])
                        last.then_inc(p_turned, 1)

                    def attend(k, b, t_sum):
                        pe.wait_ge(pT_lo, 3 * b + 3)
                        if t_sum is not None:
                            pe.wait_ge(x1_sum, t_sum)
                        for c in range(DC):
                            cols = slice(c * P, (c + 1) * P)
                            steps = [(lambda h, kt=kt: v[k % 2][:, h, kt, cols], lambda h, kt=kt: pT[:, h, kt, c, :]) for kt in range(2)]
                            steps.append((lambda h: vlast[0:32, h, cols], lambda h: pTl[:, h, c, :]))
                            last = products(nc, bank[7][:, cols], range(3), lambda s, h: steps[s][0](h), lambda s, h: steps[s][1](h))
                        last.then_inc(pv_ps, 1)

                    def score(b, cs, begin):
                        for c in cs:
                            pe.wait_ge(k_lo, DC * b + c + 1)
                            if not (begin and c < 2):
                                pe.wait_ge(u_ok, DC * b + c - 1)
                            if c == 0:
                                pe.wait_ge(qbd_ok, b + 1)
                            products(nc, bank[2 + c % 2][:, 0:SKE], range(1), lambda _, h: qbd[:, h, c, :],
                                     lambda _, h: kT[:, h, c, :]).then_inc(s_ps, 1)

                    def project(t):
                        pe.wait_ge(oT_lo, t + 1)
                        products(nc, bank[7][:, :], range(DC), lambda c, h: oT_hl[:, h, c, :], lambda c, h: wo[:, h, c, :]).then_inc(o_ps, 1)

                    def body(it, first):
                        for k in range(BPT):
                            b = BPT * it + k
                            begin = first and k == 0
                            pe.wait_ge(ctx_lo, b + 1)
                            for dc in range(DC):
                                if dc < 2 and not begin:
                                    pe.wait_ge(v_lo, 2 * b - 1 + dc)
                                if dc >= 2:
                                    pe.wait_ge(k_lo, DC * b + dc - 1)
                                products(nc, bank[dc % 2][:, 0:SKE], range(DC), lambda c, h: wk[:, h, c, dc * P:(dc + 1) * P],
                                         lambda c, h: ctx[k % 2][:, h, c, :]).then_inc(k_ps, 1)
                            if k == 1 and not first:
                                project(it - 1)
                            if not begin:
                                turn(b - 1)
                            for kt in range(2):
                                pe.wait_ge(k_lo, DC * b + 3 + kt)
                                products(nc, bank[kt][:, :], range(DC), lambda c, h: ctx[k % 2][:, h, c, kt * P:(kt + 1) * P],
                                         lambda c, h: wv[:, h, c, :]).then_inc(v_ps, 1)
                                if kt == 0 and not begin:
                                    if not (first and k == 1):
                                        pe.wait_ge(oT_ok, HPC * (b - 1))
                                    attend(k - 1, b - 1, it if k == 1 and not first else None)
                                score(b, (2 * kt, 2 * kt + 1), begin)
                    body(0, True)
                    with pe.Fori(1, NT) as it:
                        body(it, False)
                    turn(NB - 1)
                    pe.wait_ge(oT_ok, HPC * (NB - 1))
                    attend(BPT - 1, NB - 1, None)
                    project(NT - 1)


def retention_layers(nc, a, whole, holder, sem, bank, X, A, ident, vec, mhalf, xg):
    with ExitStack() as phase:
        sb = holder(phase)
        gn_bc = sb("gn_bc", [P, 2, D])
        lnv = sb("lnv", [P, 2, 2, DC])
        rot = sb("rot", [P, 4, E // 2])
        decay = sb("decay", [P, 2, DC, P])
        mv = sb("r_mv", [P, NT, 2])
        stats = sb("r_stats", [P, NT, 6])
        veps = sb("r_veps", [P, NT])
        rstd = sb("r_rstd", [P, NT])
        xh = [sb(f"r_xh{i}", [P, D]) for i in range(2)]
        xf = sb("xf", [P, DC, P])
        zero = sb("zero", [P, D])
        att = ExitStack()
        sba = holder(att)
        wa = sba("wa", [P, 2, DC, 5 * D], F32R)
        wraw = [sba(f"wraw{i}", [P, DC, 256]) for i in range(2)]
        xn = [sba(f"xn{i}", [P, 2, DC, P], F32R) for i in range(2)]
        rc = sba("rc", [P, 2, D])
        rs = sba("rs", [P, 2, D])
        qk = sba("qk", [P, 2, D])
        qkT = sba("qkT", [P, 2, 2, DC, P], F32R)
        vv = sba("vv", [P, 2, D], F32R)
        sw = sba("sw", [P, D])
        sws = sba("sws", [P, 2, D])
        pf = sba("pf", [P, 2, DC, P])
        p_hl = sba("p_hl", [P, 2, 2, DC, P], F32R)
        gst = sba("gst", [P, H, 6])
        gmv = sba("gmv", [P, H, 2])
        gve = sba("gve", [P, H])
        grs = sba("grs", [P, H])
        y = sba("y", [P, D])
        yT = sba("yT", [P, 2, DC, P], F32R)
        att.close()
        ff = ExitStack()
        sbf = holder(ff)
        x2T = sbf("x2T", [P, 2, DC, TOK], F32R)
        fraw = [sbf(f"fraw{i}", [P, 2 * D]) for i in range(2)]
        fw = [sbf(f"fw{i}", [P, 2, 2 * D], F32R) for i in range(2)]
        hf32 = [sbf(f"hf32_{i}", [P, 512]) for i in range(2)]
        hh = [sbf(f"hh{i}", [P, 2, 512], F32R) for i in range(2)]
        ff.close()

        names = """zero_ok zeroed tab_in gn_in w_hi w_lo a0_ok st_ok ag_ok ve_ok rs_ok xh_ok x_turned xf_ok xn_hi xn_lo
            q_ps k_ps v_ps g_ps rc_ok qk_ok qk_turned qkT_hi qkT_lo v_hi v_lo sw_ok sws_ok s_ps pf_ok p_hi p_lo o_ps
            gst_ok gmv_ok gve_ok grs_ok cen_ok hn_ok ya_ok y_ok y_turned yT_hi yT_lo wo_ps res_ok
            st2_ok ag2_ok ve2_ok rs2_ok xh2_ok x2_turned xf2_ok x2_hi x2_lo
            f_hi f_lo up_ps h_ok h_hi h_lo down_ps ffn_ok ln0_st ln0_ag ln0_ve ln0_rs""".split()
        m = {n: sem("r_" + n) for n in names}
        w_in = [sem("r_w_in0"), sem("r_w_in1")]
        f_in = [sem("r_f_in0"), sem("r_f_in1")]

        def tile_of(tensor, t):
            if isinstance(t, int):
                return tensor[:, t, :]
            return tensor[:, bass.ds(t, 1), :].rearrange("p o d -> p (o d)")

        def pairs(eng, body):
            body(0, True, False)
            with eng.Fori(1, NT // 2 - 1) as it:
                body(it, False, False)
            body(NT // 2 - 1, False, True)

        halves = [slice(0, 32), slice(32, 64)]

        def split_halves(ap):
            return ap.rearrange("p (h two e) -> p h two e", two=2, e=E // 2)

        with nc.Block() as block:
            @block.sync
            def _(sp):
                sp.dma_start(rot[:, :, :], a["rot"]).then_inc(m["tab_in"], 16)
                sp.dma_start(decay[:, :, :, :], a["decay"]).then_inc(m["tab_in"], 16)
                with sp.Fori(0, L) as layer:
                    sp.wait_ge(m["ffn_ok"], 8 * layer + 1)
                    sp.dma_start(gn_bc[:, :, :], a["gn"][bass.ds(layer, 1), :, :, :].rearrange("o p k d -> p (o k) d")).then_inc(m["gn_in"], 16)
                    sp.dma_start(lnv[:, :, :, :], a["lnv"][bass.ds(layer, 1), :, :].rearrange("o p n -> p (o n)")).then_inc(m["gn_in"], 16)
                    for j in range(10):
                        if j >= 2:
                            sp.wait_ge(m["w_hi"], 10 * layer + j - 1)
                            sp.wait_ge(m["w_lo"], 10 * layer + j - 1)
                        sp.dma_start(wraw[j % 2][:, :, :], a["wa"][bass.ds(layer, 1), j, :, :].rearrange("o p (c n) -> p (o c) n", c=DC)).then_inc(w_in[j % 2], 16)
                    wait_alone(sp, m["res_ok"], 8 * layer + 8)
                    sp.wait_ge(m["wo_ps"], 8 * layer + 8)
                    with sp.Fori(0, 2) as half:
                        with sp.Fori(0, FC // 2) as it:
                            for k in range(2):
                                n = 32 * layer + 16 * half + 2 * it + k
                                sp.wait_ge(m["f_hi"], n + 1)
                                sp.wait_ge(m["f_lo"], n + 1)
                                sp.dma_start(fraw[k][:, :], a["wf"][bass.ds(layer, 1), bass.ds(2 * it + k, 1), :, :].rearrange("o q p n -> p (o q n)")).then_inc(f_in[k], 16)

            @block.gpsimd
            def _(pool):
                nc.gpsimd.memset(zero[:, :], 0.0).then_inc(m["zero_ok"], 1)
                pool.wait_ge(m["zero_ok"], 1)
                pool.dma_start(xg.rearrange("(n p) d -> p n d", p=P), zero[:, :].unsqueeze(1).broadcast_to([P, SLOTS // P, D])).then_inc(m["zeroed"], 16)

                def root(src, dst, n, ok, value, done):
                    pool.wait_ge(ok, value)
                    nc.gpsimd.tensor_tensor(dst, src, mhalf[:, 0:n], ALU.pow).then_inc(done, 1)
                root(veps[:, :], rstd[:, :], NT, m["ln0_ve"], 1, m["ln0_rs"])
                with pool.Fori(0, L) as layer:
                    n0 = 8 * layer

                    def combine(n, j):
                        pool.wait_ge(m["rc_ok"], 4 * n + 2 * j + 2)
                        c4, s4, o4 = (split_halves(z[:, j, :]) for z in (rc, rs, qk))
                        nc.gpsimd.tensor_tensor(o4[:, :, 0, :], c4[:, :, 0, :], s4[:, :, 1, :], ALU.subtract).then_inc(m["qk_ok"], 1)
                        nc.gpsimd.tensor_tensor(o4[:, :, 1, :], c4[:, :, 1, :], s4[:, :, 0, :], ALU.add).then_inc(m["qk_ok"], 1)

                    def norm_root(n):
                        root(veps[:, 0:1], rstd[:, 0:1], 1, m["ve_ok"], n + 1, m["rs_ok"])
                    norm_root(n0)
                    pool.wait_ge(m["gn_in"], 32 * layer + 32)

                    def body(it, first, last):
                        for k in range(2):
                            n = n0 + 2 * it + k
                            begin, end = first and k == 0, last and k == 1
                            combine(n, 0)
                            combine(n, 1)
                            if not begin:
                                root(gve[:, :], grs[:, :], H, m["gve_ok"], n, m["grs_ok"])
                                pool.wait_ge(m["ya_ok"], n)
                                pool.wait_ge(m["y_ok"], n)
                            pool.wait_ge(m["sw_ok"], n + 1)
                            for j in range(2):
                                nc.gpsimd.tensor_tensor(sws[:, j, :], sw[:, :], gn_bc[:, j, :], ALU.mult).then_inc(m["sws_ok"], 1)
                            if not end:
                                norm_root(n + 1)
                            for j in range(2):
                                pool.wait_ge(m["p_hi"], 2 * n + j + 1)
                                nc.gpsimd.tensor_tensor(p_hl[:, 1, j, :, :], pf[:, j, :, :], r(p_hl[:, 0, j, :, :]), ALU.subtract).then_inc(m["p_lo"], 1)
                    pairs(pool, body)
                    root(gve[:, :], grs[:, :], H, m["gve_ok"], n0 + 8, m["grs_ok"])
                    root(veps[:, :], rstd[:, :], NT, m["ve2_ok"], layer + 1, m["rs2_ok"])
                pool.wait_ge(m["zeroed"], 16)

            @block.scalar
            def _(act):
                for _ in range(2):
                    act.sem_inc(m["f_hi"], 1)
                    act.sem_inc(m["down_ps"], 1)
                with act.Fori(0, L) as layer:
                    n0 = 8 * layer

                    def weights_hi(j):
                        act.wait_ge(w_in[j % 2], 80 * layer + 16 * (j // 2) + 16)
                        nc.scalar.activation(wa[:, 0, :, j * 256:(j + 1) * 256], wraw[j % 2][:, :, :], ACT.Copy).then_inc(m["w_hi"], 1)

                    def scale_columns(n, name, bk, turned, value, done):
                        act.wait_ge(turned, value)
                        for c in range(DC):
                            nc.scalar.activation(xf[:, c, :], bk[:, c * P:(c + 1) * P], ACT.Identity, scale=lnv[:, name, 0, c:c + 1],
                                                 bias=lnv[:, name, 1, c:c + 1]).then_inc(done, 1)

                    def norm_hi(n, k):
                        scale_columns(n, 0, bank[7], m["x_turned"], n + 1, m["xf_ok"])
                        act.wait_ge(m["xf_ok"], DC * (n + 1))
                        nc.scalar.activation(xn[k][:, 0, :, :], xf[:, :, :], ACT.Copy).then_inc(m["xn_hi"], 1)

                    weights_hi(0)
                    act.wait_ge(m["gn_in"], 32 * layer + 32)
                    norm_hi(n0, 0)

                    def turned_hi(dst, bk):
                        return nc.scalar.activation(dst, bk[:, :].rearrange("p (c n) -> p c n", c=DC), ACT.Copy)

                    def body(it, first, last):
                        for k in range(2):
                            n = n0 + 2 * it + k
                            begin, end = first and k == 0, last and k == 1
                            if begin:
                                for j in range(1, 10):
                                    weights_hi(j)
                            act.wait_ge(m["v_ps"], n + 1)
                            nc.scalar.activation(vv[:, 0, :], bank[2][:, :], ACT.Copy).then_inc(m["v_hi"], 1)
                            act.wait_ge(m["g_ps"], n + 1)
                            if not begin:
                                act.wait_ge(m["sws_ok"], 2 * n)
                            nc.scalar.activation(sw[:, :], bank[3][:, :], ACT.Silu).then_inc(m["sw_ok"], 1)
                            if not begin:
                                act.wait_ge(m["y_turned"], n)
                                turned_hi(yT[:, 0, :, :], bank[6]).then_inc(m["yT_hi"], 1)
                            for j in range(2):
                                act.wait_ge(m["qk_turned"], 2 * n + j + 1)
                                turned_hi(qkT[:, j, 0, :, :], bank[4 + j]).then_inc(m["qkT_hi"], 1)
                            if not end:
                                norm_hi(n + 1, 1 - k)
                            for j in range(2):
                                act.wait_ge(m["pf_ok"], 2 * n + j + 1)
                                nc.scalar.activation(p_hl[:, 0, j, :, :], pf[:, j, :, :], ACT.Copy).then_inc(m["p_hi"], 1)
                    pairs(act, body)
                    act.wait_ge(m["y_turned"], n0 + 8)
                    turned_hi(yT[:, 0, :, :], bank[6]).then_inc(m["yT_hi"], 1)

                    def weights2_hi(k, n, use):
                        act.wait_ge(f_in[k], use)
                        nc.scalar.activation(fw[k][:, 0, :], fraw[k][:, :], ACT.Copy).then_inc(m["f_hi"], 1)
                    act.wait_ge(m["wo_ps"], n0 + 8)
                    for t in range(NT):
                        n = n0 + t
                        if t >= 1:
                            act.wait_ge(m["x2_lo"], n)
                        scale_columns(n, 1, bank[t % 2], m["x2_turned"], n + 1, m["xf2_ok"])
                        act.wait_ge(m["xf2_ok"], DC * (n + 1))
                        nc.scalar.activation(x2T[:, 0, :, t * P:(t + 1) * P], xf[:, :, :], ACT.Copy).then_inc(m["x2_hi"], 1)
                    with act.Fori(0, 2) as half:
                        with act.Fori(0, FC // 2) as it:
                            for k in range(2):
                                n = 32 * layer + 16 * half + 2 * it + k
                                act.wait_ge(m["down_ps"], n + 1)
                                weights2_hi(k, n, 16 * (16 * layer + 8 * half + it) + 16)
                                act.wait_ge(m["up_ps"], n + 1)
                                nc.scalar.activation(hh[k][:, 0, :], bank[k][:, :], ACT.Gelu_apprx_tanh).then_inc(m["h_hi"], 1)
                                nc.scalar.activation(hf32[k][:, :], bank[k][:, :], ACT.Gelu_apprx_tanh).then_inc(m["h_ok"], 1)

            @block.vector
            def _(dve):
                for t in range(NT):
                    nc.vector.bn_stats(stats[:, t, :], X[:, t, :]).then_inc(m["ln0_st"], 1)
                for t in range(NT):
                    dve.wait_ge(m["ln0_st"], t + 1)
                    nc.vector.bn_aggr(mv[:, t, :], stats[:, t, :]).then_inc(m["ln0_ag"], 1)
                dve.wait_ge(m["ln0_ag"], NT)
                nc.vector.tensor_scalar(veps[:, :], mv[:, :, 1], 1e-5, None, ALU.add).then_inc(m["ln0_ve"], 1)
                dve.wait_ge(m["ln0_rs"], 1)
                for t in range(NT):
                    nc.vector.tensor_scalar(A[:, t, :], X[:, t, :], mv[:, t, 0:1], rstd[:, t:t + 1], ALU.subtract, ALU.mult).then_inc(m["a0_ok"], 1)
                dve.wait_ge(m["a0_ok"], NT)
                dve.sem_inc(m["ffn_ok"], 1)
                for _ in range(2):
                    dve.sem_inc(m["f_lo"], 1)
                dve.wait_ge(m["tab_in"], 32)
                with dve.Fori(0, L) as layer:
                    n0 = 8 * layer

                    def weights_lo(j):
                        dve.wait_ge(m["w_hi"], 10 * layer + j + 1)
                        cols = slice(j * 256, (j + 1) * 256)
                        nc.vector.tensor_tensor(wa[:, 1, :, cols], wraw[j % 2][:, :, :], r(wa[:, 0, :, cols]), ALU.subtract).then_inc(m["w_lo"], 1)

                    def norm_stats(n, t):
                        nc.vector.bn_stats(stats[:, 0, :], tile_of(A, t)).then_inc(m["st_ok"], 1)
                        wait_alone(dve, m["st_ok"], n + 1)
                        nc.vector.bn_aggr(mv[:, 0, :], stats[:, 0, :]).then_inc(m["ag_ok"], 1)
                        dve.wait_ge(m["ag_ok"], n + 1)
                        nc.vector.tensor_scalar(veps[:, 0:1], mv[:, 0, 1:2], 1e-6, None, ALU.add).then_inc(m["ve_ok"], 1)

                    def norm_apply(n, t):
                        dve.wait_ge(m["rs_ok"], n + 1)
                        nc.vector.tensor_scalar(xh[0][:, :], tile_of(A, t), mv[:, 0, 0:1], rstd[:, 0:1], ALU.subtract, ALU.mult).then_inc(m["xh_ok"], 1)

                    def norm_lo(n, k):
                        dve.wait_ge(m["xn_hi"], n + 1)
                        nc.vector.tensor_tensor(xn[k][:, 1, :, :], xf[:, :, :], r(xn[k][:, 0, :, :]), ALU.subtract).then_inc(m["xn_lo"], 1)

                    norm_stats(n0, 0)
                    norm_apply(n0, 0)
                    weights_lo(0)
                    norm_lo(n0, 0)

                    def rotate(n, j):
                        dve.wait_ge(m["q_ps" if j == 0 else "k_ps"], n + 1)
                        src = bank[j][:, :].rearrange("p (g e) -> p g e", e=E // 2)
                        for z, w in ((rc, 2 * j), (rs, 2 * j + 1)):
                            nc.vector.tensor_tensor(z[:, j, :].rearrange("p (g e) -> p g e", e=E // 2), src,
                                                    rot[:, w:w + 1, :].broadcast_to([P, 2 * H, E // 2]), ALU.mult).then_inc(m["rc_ok"], 1)

                    def group_norm(n):
                        dve.wait_ge(m["o_ps"], n)
                        for h in range(H):
                            nc.vector.bn_stats(gst[:, h, :], bank[7][:, h * E:(h + 1) * E]).then_inc(m["gst_ok"], 1)
                        wait_alone(dve, m["gst_ok"], H * n)
                        for h in range(H):
                            nc.vector.bn_aggr(gmv[:, h, :], gst[:, h, :]).then_inc(m["gmv_ok"], 1)
                        dve.wait_ge(m["gmv_ok"], H * n)
                        nc.vector.tensor_scalar(gve[:, :], gmv[:, :, 1], 1e-6, None, ALU.add).then_inc(m["gve_ok"], 1)
                        heads = lambda z: z.rearrange("p (h e) -> p h e", e=E)
                        nc.vector.tensor_tensor(heads(y[:, :]), heads(bank[7][:, :]), gmv[:, :, 0:1].broadcast_to([P, H, E]), ALU.subtract).then_inc(m["cen_ok"], 1)
                        dve.wait_ge(m["grs_ok"], n)
                        dve.wait_ge(m["cen_ok"], n)
                        nc.vector.tensor_tensor(heads(y[:, :]), heads(y[:, :]), grs[:, :].unsqueeze(2).broadcast_to([P, H, E]), ALU.mult).then_inc(m["hn_ok"], 1)
                        dve.wait_ge(m["sws_ok"], 2 * n)
                        dve.wait_ge(m["hn_ok"], n)
                        nc.vector.tensor_tensor(y[:, :], y[:, :], sws[:, 0, :], ALU.mult).then_inc(m["ya_ok"], 1)
                        dve.wait_ge(m["ya_ok"], n)
                        nc.vector.tensor_tensor(y[:, :], y[:, :], sws[:, 1, :], ALU.add).then_inc(m["y_ok"], 1)

                    def turned_lo(dst, bk, hi):
                        return nc.vector.tensor_tensor(dst, bk[:, :].rearrange("p (c n) -> p c n", c=DC), r(hi), ALU.subtract)

                    def residual(n, t):
                        dve.wait_ge(m["wo_ps"], n + 1)
                        nc.vector.tensor_tensor(tile_of(A, t), bank[6][:, :], tile_of(A, t), ALU.add).then_inc(m["res_ok"], 1)

                    def body(it, first, last):
                        for k in range(2):
                            t = 2 * it + k
                            n = n0 + t
                            begin, end = first and k == 0, last and k == 1
                            if begin:
                                for j in range(1, 4):
                                    weights_lo(j)
                            rotate(n, 0)
                            rotate(n, 1)
                            if begin:
                                for j in range(4, 10):
                                    weights_lo(j)
                            if not begin:
                                group_norm(n)
                            dve.wait_ge(m["v_hi"], n + 1)
                            nc.vector.tensor_tensor(vv[:, 1, :], bank[2][:, :], r(vv[:, 0, :]), ALU.subtract).then_inc(m["v_lo"], 1)
                            if not end:
                                norm_stats(n + 1, t + 1)
                            if not begin:
                                dve.wait_ge(m["yT_hi"], n)
                                turned_lo(yT[:, 1, :, :], bank[6], yT[:, 0, :, :]).then_inc(m["yT_lo"], 1)
                            if not end:
                                norm_apply(n + 1, t + 1)
                            for j in range(2):
                                dve.wait_ge(m["qkT_hi"], 2 * n + j + 1)
                                turned_lo(qkT[:, j, 1, :, :], bank[4 + j], qkT[:, j, 0, :, :]).then_inc(m["qkT_lo"], 1)
                            if not end:
                                norm_lo(n + 1, 1 - k)
                            if not begin:
                                residual(n - 1, t - 1)
                            dve.wait_ge(m["s_ps"], n + 1)
                            if not begin:
                                dve.wait_ge(m["p_lo"], 2 * n)
                            for j in range(2):
                                nc.vector.tensor_tensor(pf[:, j, :, :], bank[2 + j][:, :].rearrange("p (c n) -> p c n", c=DC),
                                                        decay[:, j, :, :], ALU.mult).then_inc(m["pf_ok"], 1)
                    pairs(dve, body)
                    group_norm(n0 + 8)
                    dve.wait_ge(m["yT_hi"], n0 + 8)
                    turned_lo(yT[:, 1, :, :], bank[6], yT[:, 0, :, :]).then_inc(m["yT_lo"], 1)
                    residual(n0 + 7, 7)

                    dve.wait_ge(m["res_ok"], n0 + 8)
                    for t in range(NT):
                        nc.vector.bn_stats(stats[:, t, :], A[:, t, :]).then_inc(m["st2_ok"], 1)
                    wait_alone(dve, m["st2_ok"], n0 + 8)
                    for t in range(NT):
                        nc.vector.bn_aggr(mv[:, t, :], stats[:, t, :]).then_inc(m["ag2_ok"], 1)
                    dve.wait_ge(m["ag2_ok"], n0 + 8)
                    nc.vector.tensor_scalar(veps[:, :], mv[:, :, 1], 1e-6, None, ALU.add).then_inc(m["ve2_ok"], 1)
                    dve.wait_ge(m["rs2_ok"], layer + 1)

                    def norm2_lo(t):
                        dve.wait_ge(m["x2_hi"], n0 + t + 1)
                        cols = slice(t * P, (t + 1) * P)
                        nc.vector.tensor_tensor(x2T[:, 1, :, cols], xf[:, :, :], r(x2T[:, 0, :, cols]), ALU.subtract).then_inc(m["x2_lo"], 1)
                    for t in range(NT):
                        if t >= 2:
                            dve.wait_ge(m["x2_turned"], n0 + t - 1)
                        nc.vector.tensor_scalar(xh[t % 2][:, :], A[:, t, :], mv[:, t, 0:1], rstd[:, t:t + 1], ALU.subtract, ALU.mult).then_inc(m["xh2_ok"], 1)
                        if t >= 1:
                            norm2_lo(t - 1)
                    norm2_lo(NT - 1)

                    with dve.Fori(0, 2) as half:
                        with dve.Fori(0, FC // 2) as it:
                            for k in range(2):
                                n = 32 * layer + 16 * half + 2 * it + k
                                dve.wait_ge(m["f_hi"], n + 3)
                                nc.vector.tensor_tensor(fw[k][:, 1, :], fraw[k][:, :], r(fw[k][:, 0, :]), ALU.subtract).then_inc(m["f_lo"], 1)
                                dve.wait_ge(m["h_ok"], n + 1)
                                nc.vector.tensor_tensor(hh[k][:, 1, :], hf32[k][:, :], r(hh[k][:, 0, :]), ALU.subtract).then_inc(m["h_lo"], 1)
                        for j in range(4):
                            dve.wait_ge(m["down_ps"], 32 * layer + 16 * half + 18)
                            at = tile_of(A, 4 * half + j)
                            nc.vector.tensor_tensor(at, bank[4 + j][:, :], at, ALU.add).then_inc(m["ffn_ok"], 1)
                    dve.wait_ge(m["ffn_ok"], n0 + 9)

            @block.tensor
            def _(pe):
                with pe.Fori(0, L) as layer:
                    n0 = 8 * layer

                    def turn(src, bk):
                        for c in range(DC):
                            last = nc.tensor.transpose(bk[:, c * P:(c + 1) * P], src[:, c * P:(c + 1) * P], ident[:, :])
                        return last

                    def project(which, bk, k):
                        return products(nc, bk[:, :], range(DC), lambda c, h: xn[k][:, h, c, :],
                                        lambda c, h: wa[:, h, c, which * D:(which + 1) * D])

                    def apply_scores(n):
                        pe.wait_ge(m["p_lo"], 2 * n)
                        pe.wait_ge(m["v_lo"], n)
                        for h in range(H):
                            last = products(nc, bank[7][:, h * E:(h + 1) * E], range(1), lambda _, i: p_hl[:, i, h % 2, h // 2, :],
                                            lambda _, i: vv[:, i, h * E:(h + 1) * E])
                        last.then_inc(m["o_ps"], 1)

                    def project_out(n):
                        pe.wait_ge(m["yT_lo"], n)
                        products(nc, bank[6][:, :], range(DC), lambda c, h: yT[:, h, c, :],
                                 lambda c, h: wa[:, h, c, 4 * D:5 * D]).then_inc(m["wo_ps"], 1)

                    pe.wait_ge(m["xh_ok"], n0 + 1)
                    turn(xh[0], bank[7]).then_inc(m["x_turned"], 1)

                    def body(it, first, last):
                        for k in range(2):
                            n = n0 + 2 * it + k
                            begin, end = first and k == 0, last and k == 1
                            pe.wait_ge(m["xn_lo"], n + 1)
                            if begin:
                                pe.wait_ge(m["w_lo"], 10 * layer + 2)
                            else:
                                pe.wait_ge(m["rc_ok"], 4 * n - 2)
                            project(0, bank[0], k).then_inc(m["q_ps"], 1)
                            if begin:
                                pe.wait_ge(m["w_lo"], 10 * layer + 4)
                            else:
                                pe.wait_ge(m["rc_ok"], 4 * n)
                            project(1, bank[1], k).then_inc(m["k_ps"], 1)
                            if not begin:
                                apply_scores(n)
                                pe.wait_ge(m["pf_ok"], 2 * n)
                            else:
                                pe.wait_ge(m["w_lo"], 10 * layer + 6)
                            project(2, bank[2], k).then_inc(m["v_ps"], 1)
                            if begin:
                                pe.wait_ge(m["w_lo"], 10 * layer + 8)
                            project(3, bank[3], k).then_inc(m["g_ps"], 1)
                            if not begin:
                                pe.wait_ge(m["y_ok"], n)
                                if not (first and k == 1):
                                    pe.wait_ge(m["res_ok"], n - 1)
                                turn(y, bank[6]).then_inc(m["y_turned"], 1)
                            for j in range(2):
                                pe.wait_ge(m["qk_ok"], 4 * n + 2 * j + 2)
                                turn(qk[:, j, :], bank[4 + j]).then_inc(m["qk_turned"], 1)
                            if not end:
                                pe.wait_ge(m["xh_ok"], n + 2)
                                turn(xh[0], bank[7]).then_inc(m["x_turned"], 1)
                            if not begin:
                                if first:
                                    pe.wait_ge(m["w_lo"], 10 * layer + 10)
                                project_out(n)
                            pe.wait_ge(m["qkT_lo"], 2 * n + 2)
                            pe.wait_ge(m["v_lo"], n + 1)
                            pe.wait_ge(m["sw_ok"], n + 1)
                            for h in range(H):
                                rows = slice((h % 2) * E, (h % 2 + 1) * E)
                                c = h // 2
                                last_mm = products(nc, bank[2 + h % 2][:, c * P:(c + 1) * P], range(1), lambda _, i: qkT[rows, 1, i, c, :],
                                                   lambda _, i: qkT[rows, 0, i, c, :])
                            last_mm.then_inc(m["s_ps"], 1)
                    pairs(pe, body)
                    apply_scores(n0 + 8)
                    pe.wait_ge(m["y_ok"], n0 + 8)
                    pe.wait_ge(m["res_ok"], n0 + 7)
                    turn(y, bank[6]).then_inc(m["y_turned"], 1)
                    project_out(n0 + 8)

                    for t in range(NT):
                        pe.wait_ge(m["xh2_ok"], n0 + t + 1)
                        if t >= 2:
                            pe.wait_ge(m["xf2_ok"], DC * (n0 + t - 1))
                        turn(xh[t % 2], bank[t % 2]).then_inc(m["x2_turned"], 1)
                    wait_alone(pe, m["x2_lo"], n0 + 8)

                    def up(n, k, half):
                        pe.wait_ge(m["f_lo"], n + 3)
                        products(nc, bank[k][:, :], range(DC), lambda c, h: fw[k][:, h, c * P:(c + 1) * P],
                                 lambda c, h: x2T[:, h, c, bass.ds(half * 512, 512)]).then_inc(m["up_ps"], 1)

                    def down(n, k, start, stop):
                        pe.wait_ge(m["h_lo"], n + 1)
                        for j in range(4):
                            for i, (x, w) in enumerate(PARTS):
                                last = nc.tensor.matmul(bank[4 + j][:, :], hh[k][:, x, j * P:(j + 1) * P], fw[k][:, w, D:2 * D],
                                                        start=start and i == 0, stop=stop and i == 2)
                        return last

                    with pe.Fori(0, 2) as half:
                        b = 32 * layer + 16 * half
                        up(b, 0, half)
                        up(b + 1, 1, half)
                        pe.wait_ge(m["ffn_ok"], 8 * layer + 4 * half + 1)
                        down(b, 0, True, False).then_inc(m["down_ps"], 1)
                        with pe.Fori(1, FC // 2) as it:
                            up(b + 2 * it, 0, half)
                            down(b + 2 * it - 1, 1, False, False).then_inc(m["down_ps"], 1)
                            up(b + 2 * it + 1, 1, half)
                            down(b + 2 * it, 0, False, False).then_inc(m["down_ps"], 1)
                        down(b + FC - 1, 1, False, True).then_inc(m["down_ps"], 1)


def mixture(nc, a, out, whole, holder, sem, bank, X, A, ident, mhalf, xg, yg):
    with ExitStack() as phase:
        sb = holder(phase)
        slot = sb("slot", [P, 2, NT], I32)
        gate = sb("gate", [P, 2, NT])
        group_expert = sb("group_expert", [1, NG], I32)

        with ExitStack() as inner:
            sbi = holder(inner)
            tab = sbi("tab", [P, 2 * P + NE + NE * NE + NG])
            upper, ones = tab[:, 0:P], tab[:, P:2 * P]
            iota_e = tab[:, 2 * P:2 * P + NE]
            before = tab[:, 2 * P + NE:2 * P + NE + NE * NE].rearrange("p (e f) -> p e f", f=NE)
            iota_g = tab[:, 2 * P + NE + NE * NE:]
            rw = sbi("rw", [P, DC, NE])
            rw_hl = sbi("rw_hl", [P, 2, DC, NE], F32R)
            stats = sbi("m_stats", [P, NT, 6])
            mv = sbi("m_mv", [P, NT, 2])
            veps = sbi("m_veps", [P, NT])
            rstd = sbi("m_rstd", [P, NT])
            xr = [sbi(f"xr{i}", [P, 2, DC, P], F32R) for i in range(2)]
            logits = sbi("logits", [P, NT, NE])
            top = sbi("top", [P, NT, NE])
            topi = sbi("topi", [P, NT, NE], U32)
            chosen = sbi("chosen", [P, 2, NT])
            diff = sbi("diff", [P, NT])
            odds = sbi("odds", [P, NT])
            sum1 = sbi("sum1", [P, NT])
            hot = sbi("hot", [P, 2, NT, NE])
            both = sbi("both", [P, NT, NE])
            cnt = sbi("cnt", [P, 2, NT, NE])
            cum = sbi("cum", [P, NT + 1, NE])
            groups = sbi("groups", [P, 5, NE])
            tri = sbi("tri", [P, NE, NE])
            gs = sbi("gs", [P, 3, NE])
            where = sbi("where", [P, 2, NT, NE])
            picked = sbi("picked", [P, 2, NT, NE])
            slotf = sbi("slotf", [P, 2, NT])
            ge = sbi("ge", [P, NG, NE])
            gsum = sbi("gsum", [P, NG])
            gmin = sbi("gmin", [P, NG])
            names = """tab_in x2_ok st_ok ag_ok ve_ok rs_ok xh_ok turned hi lo rw_hi rw_lo logit_ps logit_ok top_ok topi_ok
                route odds_ok both_ok cnt_ps cum_ok slot_ok scattered""".split()
            m = {n: sem("m_" + n) for n in names}
            with nc.Block() as block:
                @block.sync
                def _(sp):
                    sp.dma_start(tab[:, :], a["route_tab"]).then_inc(m["tab_in"], 16)
                    sp.dma_start(rw[:, :, :], a["rw"]).then_inc(m["tab_in"], 16)

                @block.gpsimd
                def _(pool):
                    pool.wait_ge(m["ve_ok"], 1)
                    nc.gpsimd.tensor_tensor(rstd[:, :], veps[:, :], mhalf[:, 0:NT], ALU.pow).then_inc(m["rs_ok"], 1)
                    pool.wait_ge(m["slot_ok"], 1)
                    for t in range(NT):
                        for k in range(2):
                            nc.gpsimd.indirect_dma_start(out=xg[:, :], out_offset=bass.IndirectOffsetOnAxis(ap=slot[:, k, t:t + 1], axis=0),
                                                         in_=A[:, t, :], in_offset=None).then_inc(m["scattered"], 16)
                    pool.wait_ge(m["scattered"], 16 * 2 * NT)

                @block.scalar
                def _(act):
                    act.wait_ge(m["tab_in"], 32)
                    nc.scalar.activation(rw_hl[:, 0, :, :], rw[:, :, :], ACT.Copy).then_inc(m["rw_hi"], 1)
                    for t in range(NT):
                        act.wait_ge(m["turned"], t + 1)
                        if t >= 2:
                            act.wait_ge(m["logit_ps"], t - 1)
                        nc.scalar.activation(xr[t % 2][:, 0, :, :], bank[t % 2][:, :].rearrange("p (c n) -> p c n", c=DC), ACT.Copy).then_inc(m["hi"], 1)
                    act.wait_ge(m["route"], 2)
                    nc.scalar.activation(odds[:, :], diff[:, :], ACT.Exp).then_inc(m["odds_ok"], 1)

                @block.vector
                def _(dve):
                    for t in range(NT):
                        nc.vector.tensor_tensor(X[:, t, :], X[:, t, :], A[:, t, :], ALU.add).then_inc(m["x2_ok"], 1)
                    for t in range(NT):
                        dve.wait_ge(m["x2_ok"], t + 1)
                        nc.vector.bn_stats(stats[:, t, :], X[:, t, :]).then_inc(m["st_ok"], 1)
                    for t in range(NT):
                        dve.wait_ge(m["st_ok"], t + 1)
                        nc.vector.bn_aggr(mv[:, t, :], stats[:, t, :]).then_inc(m["ag_ok"], 1)
                    dve.wait_ge(m["ag_ok"], NT)
                    nc.vector.tensor_scalar(veps[:, :], mv[:, :, 1], 1e-5, None, ALU.add).then_inc(m["ve_ok"], 1)
                    dve.wait_ge(m["rw_hi"], 1)
                    nc.vector.tensor_tensor(rw_hl[:, 1, :, :], rw[:, :, :], r(rw_hl[:, 0, :, :]), ALU.subtract).then_inc(m["rw_lo"], 1)
                    dve.wait_ge(m["rs_ok"], 1)

                    def lo(t):
                        dve.wait_ge(m["hi"], t + 1)
                        nc.vector.tensor_tensor(xr[t % 2][:, 1, :, :], bank[t % 2][:, :].rearrange("p (c n) -> p c n", c=DC),
                                                r(xr[t % 2][:, 0, :, :]), ALU.subtract).then_inc(m["lo"], 1)
                    for t in range(NT):
                        nc.vector.tensor_scalar(A[:, t, :], X[:, t, :], mv[:, t, 0:1], rstd[:, t:t + 1], ALU.subtract, ALU.mult).then_inc(m["xh_ok"], 1)
                        if t >= 1:
                            lo(t - 1)
                    lo(NT - 1)
                    dve.wait_ge(m["logit_ps"], NT)
                    nc.vector.tensor_copy(logits[:, :, :], bank[2][:, 0:NT * NE].rearrange("p (t e) -> p t e", e=NE)).then_inc(m["logit_ok"], 1)
                    dve.wait_ge(m["logit_ok"], 1)
                    for t in range(NT):
                        nc.vector.max(top[:, t, :], logits[:, t, :]).then_inc(m["top_ok"], 1)
                    for t in range(NT):
                        dve.wait_ge(m["top_ok"], t + 1)
                        nc.vector.max_index(topi[:, t, :], top[:, t, :], logits[:, t, :]).then_inc(m["topi_ok"], 1)
                    step = [0]

                    def link(ins):
                        step[0] += 1
                        ins.then_inc(m["route"], 1)
                        dve.wait_ge(m["route"], step[0])
                    dve.wait_ge(m["topi_ok"], NT)
                    link(nc.vector.tensor_copy(chosen[:, :, :].rearrange("p k t -> p t k"), topi[:, :, 0:2]))
                    link(nc.vector.tensor_tensor(diff[:, :], top[:, :, 1], top[:, :, 0], ALU.subtract))
                    for k in range(2):
                        link(nc.vector.tensor_tensor(hot[:, k, :, :], chosen[:, k, :].unsqueeze(2).broadcast_to([P, NT, NE]),
                                                     iota_e.unsqueeze(1).broadcast_to([P, NT, NE]), ALU.is_equal))
                    nc.vector.tensor_tensor(both[:, :, :], hot[:, 0, :, :], hot[:, 1, :, :], ALU.add).then_inc(m["both_ok"], 1)
                    dve.wait_ge(m["odds_ok"], 1)
                    link(nc.vector.tensor_scalar(sum1[:, :], odds[:, :], 1.0, None, ALU.add))
                    link(nc.vector.reciprocal(gate[:, 0, :], sum1[:, :]))
                    link(nc.vector.tensor_tensor(gate[:, 1, :], gate[:, 0, :], odds[:, :], ALU.mult))
                    dve.wait_ge(m["cnt_ps"], 1)
                    link(nc.vector.tensor_copy(cnt[:, :, :, :].rearrange("p a t e -> p (a t e)"), bank[3][:, 0:2 * NT * NE]))
                    link(nc.vector.memset(cum[:, 0, :], 0.0))
                    for t in range(NT):
                        link(nc.vector.tensor_tensor(cum[:, t + 1, :], cum[:, t, :], cnt[:, 1, t, :], ALU.add))
                    link(nc.vector.tensor_scalar(groups[:, 0, :], cum[:, NT, :], 0.0, None, ALU.is_gt))
                    for j in range(1, TOK // GT):
                        link(nc.vector.scalar_tensor_tensor(groups[:, j, :], cum[:, NT, :], float(j * GT), groups[:, j - 1, :], ALU.is_gt, ALU.add))
                    per_expert = groups[:, TOK // GT - 1, :]
                    link(nc.vector.tensor_tensor(tri[:, :, :], before, per_expert.unsqueeze(1).broadcast_to([P, NE, NE]), ALU.mult))
                    link(nc.vector.tensor_reduce(gs[:, 0, :], tri[:, :, :], AX.X, ALU.add))
                    link(nc.vector.tensor_tensor(gs[:, 1, :], gs[:, 0, :], per_expert, ALU.add))
                    link(nc.vector.tensor_scalar(gs[:, 2, :], gs[:, 0, :], float(GT), None, ALU.mult))
                    link(nc.vector.tensor_tensor(where[:, 0, :, :], cnt[:, 0, :, :], cum[:, 0:NT, :], ALU.add))
                    link(nc.vector.tensor_tensor(where[:, 1, :, :], where[:, 0, :, :], gs[:, 2, :].unsqueeze(1).broadcast_to([P, NT, NE]), ALU.add))
                    for k in range(2):
                        link(nc.vector.tensor_tensor(picked[:, k, :, :], hot[:, k, :, :], where[:, 1, :, :], ALU.mult))
                    link(nc.vector.tensor_reduce(slotf[:, :, :], picked[:, :, :, :], AX.X, ALU.add))
                    nc.vector.tensor_copy(slot[:, :, :], slotf[:, :, :]).then_inc(m["slot_ok"], 1)
                    link(nc.vector.tensor_tensor(ge[:, :, :], gs[:, 1, :].unsqueeze(1).broadcast_to([P, NG, NE]),
                                                 iota_g.unsqueeze(2).broadcast_to([P, NG, NE]), ALU.is_le))
                    link(nc.vector.tensor_reduce(gsum[:, :], ge[:, :, :], AX.X, ALU.add))
                    link(nc.vector.tensor_scalar(gmin[:, :], gsum[:, :], float(NE - 1), None, ALU.min))
                    link(nc.vector.tensor_copy(group_expert[:, :], gmin[0:1, :]))

                @block.tensor
                def _(pe):
                    def score(t):
                        pe.wait_ge(m["lo"], t + 1)
                        products(nc, bank[2][:, t * NE:(t + 1) * NE], range(DC), lambda c, h: xr[t % 2][:, h, c, :],
                                 lambda c, h: rw_hl[:, h, c, :]).then_inc(m["logit_ps"], 1)
                    pe.wait_ge(m["rw_lo"], 1)
                    for t in range(NT):
                        pe.wait_ge(m["xh_ok"], t + 1)
                        if t >= 2:
                            pe.wait_ge(m["lo"], t - 1)
                        for c in range(DC):
                            last = nc.tensor.transpose(bank[t % 2][:, c * P:(c + 1) * P], A[:, t, c * P:(c + 1) * P], ident[:, :])
                        last.then_inc(m["turned"], 1)
                        if t >= 1:
                            score(t - 1)
                    score(NT - 1)
                    pe.wait_ge(m["both_ok"], 1)
                    pe.wait_ge(m["tab_in"], 32)
                    flat = both[:, :, :].rearrange("p t e -> p (t e)")
                    nc.tensor.matmul(bank[3][:, 0:NT * NE], upper, flat, start=True, stop=True)
                    nc.tensor.matmul(bank[3][:, NT * NE:2 * NT * NE], ones, flat, start=True, stop=True).then_inc(m["cnt_ps"], 1)

        with ExitStack() as inner:
            sbi = holder(inner)
            xin = sbi("xin", [P, 2, D])
            xT = sbi("e_xT", [P, 2, 2, DC, P], F32R)
            raw = [sbi(f"e_raw{i}", [P, DC, 512]) for i in range(3)]
            w = [sbi(f"e_w{i}", [P, 2, DC, 512], F32R) for i in range(3)]
            si = sbi("si", [P, 2, 512])
            hid = sbi("hid", [P, 2, 512])
            hT = [sbi(f"e_hT{i}", [P, 2, 2, DC, P], F32R) for i in range(2)]
            yb = sbi("yb", [P, 2, D])
            names = """x_in x_turned x_hi x_lo w_hi w_lo step_ps si_ok hid_ok h_turned h_hi h_lo y_ok y_out""".split()
            m = {n: sem("e_" + n) for n in names}
            w_in = [sem(f"e_w_in{i}") for i in range(3)]
            G0, D1, U0, G1, U1, D0 = range(6)
            PIECE_AT = {G0: 0, U0: 1, G1: 2, U1: 3, D0: 4, D1: 5}

            def count(g, pos):
                if isinstance(g, int) and g == 0 and pos == G0:
                    return 1
                if isinstance(g, int) and g == NG:
                    return PIECES * NG
                return PIECES * g + pos

            def slot_before(g, pos):
                if isinstance(g, int) and g == 0:
                    return {G0: None, U0: None, G1: 1, U1: None, D0: 2}[pos]
                if isinstance(g, int) and g == NG:
                    return count(NG - 1, U1)
                return count(g, pos) - 3

            with nc.Block() as block:
                @block.sync
                def _(sp):
                    x_v = xg.rearrange("(g t p) d -> g p t d", p=P, t=2)

                    def load(g, pos, expert):
                        n = slot_before(g, pos)
                        if n is not None:
                            sp.wait_ge(m["w_hi"], n)
                            sp.wait_ge(m["w_lo"], n)
                        sp.dma_start(raw[pos % 3][:, :, :], a["we"][bass.ds(expert, 1), PIECE_AT[pos], :, :]
                                     .rearrange("o p (c n) -> p (o c) n", c=DC)).then_inc(w_in[pos % 3], 16)

                    def load_x(g):
                        sp.dma_start(xin[:, :, :], x_v[bass.ds(g, 1), :, :, :].rearrange("o p t d -> p (o t) d")).then_inc(m["x_in"], 16)

                    def body(g, first):
                        expert = sp.value_load(group_expert[0:1, bass.ds(g, 1)], min_val=0, max_val=NE - 1)
                        load(g, G0, expert)
                        if not first:
                            before = sp.value_load(group_expert[0:1, bass.ds(g - 1, 1)], min_val=0, max_val=NE - 1)
                            load(g, D1, before)
                        for pos in (U0, G1, U1, D0):
                            load(g, pos, expert)
                        return expert
                    load_x(0)
                    body(0, True)
                    with sp.Fori(1, NG) as g:
                        sp.wait_ge(m["x_turned"], g)
                        load_x(g)
                        body(g, False)
                    last = sp.value_load(group_expert[0:1, NG - 1:NG], min_val=0, max_val=NE - 1)
                    load(NG, D1, last)

                @block.scalar
                def _(act):
                    y_v = yg.rearrange("(g t p) d -> g p t d", p=P, t=2)

                    def split_hi(g, pos):
                        n = slot_before(g, pos)
                        if isinstance(g, int) and g == NG:
                            loads = 2 * NG
                        else:
                            loads = {G0: 2 * g + 1, G1: 2 * g + 2, U0: 2 * g + 1, D0: 2 * g + 2, D1: 2 * g, U1: 2 * g + 1}[pos]
                        act.wait_ge(w_in[pos % 3], 16 * loads)
                        if n is not None:
                            act.wait_ge(m["step_ps"], n)
                        nc.scalar.activation(w[pos % 3][:, 0, :, :], raw[pos % 3][:, :, :], ACT.Copy).then_inc(m["w_hi"], 1)

                    def silu(g, j):
                        act.wait_ge(m["step_ps"], count(g, G0 if j == 0 else G1))
                        if not (isinstance(g, int) and g == 0 and j == 0):
                            act.wait_ge(m["hid_ok"], 4 * g + 2 * j)
                        for t in range(2):
                            nc.scalar.activation(si[:, t, :], bank[t][:, :], ACT.Silu).then_inc(m["si_ok"], 1)

                    def hidden_hi(g, j):
                        for t in range(2):
                            act.wait_ge(m["h_turned"], 4 * g + 2 * j + t + 1)
                            nc.scalar.activation(hT[j][:, 0, t, :, :], bank[6 + t][:, :].rearrange("p (c n) -> p c n", c=DC), ACT.Copy).then_inc(m["h_hi"], 1)

                    def x_hi(g):
                        for t in range(2):
                            act.wait_ge(m["x_turned"], g + 1)
                            nc.scalar.activation(xT[:, 0, t, :, :], bank[6 + t][:, :].rearrange("p (c n) -> p c n", c=DC), ACT.Copy).then_inc(m["x_hi"], 1)

                    def store(g, n, first):
                        act.wait_ge(m["step_ps"], n)
                        if not first:
                            act.wait_ge(m["y_out"], 16 * g)
                        for t in range(2):
                            nc.scalar.activation(yb[:, t, :], bank[4 + t][:, :], ACT.Copy).then_inc(m["y_ok"], 1)
                        act.wait_ge(m["y_ok"], 2 * g + 2)
                        act.dma_start(y_v[bass.ds(g, 1), :, :, :].rearrange("o p t d -> p (o t) d"), yb[:, :, :]).then_inc(m["y_out"], 16)

                    def body(g, first, second=False):
                        if not first:
                            hidden_hi(g - 1, 1)
                        split_hi(g, U0)
                        silu(g, 0)
                        split_hi(g, G1)
                        if not first:
                            store(g - 1, count(g, D1), second)
                        split_hi(g, U1)
                        split_hi(g, D0)
                        hidden_hi(g, 0)
                        silu(g, 1)
                    def tail(g):
                        split_hi(g + 1, G0)
                        x_hi(g + 1)
                        split_hi(g + 1, D1)
                    x_hi(0)
                    split_hi(0, G0)
                    body(0, True)
                    tail(0)
                    body(1, False, True)
                    tail(1)
                    with act.Fori(2, NG - 1) as g:
                        body(g, False)
                        tail(g)
                    body(NG - 1, False)
                    split_hi(NG, D1)
                    hidden_hi(NG - 1, 1)
                    store(NG - 1, PIECES * NG, False)
                    act.wait_ge(m["y_out"], 16 * NG)

                @block.vector
                def _(dve):
                    def split_lo(g, pos):
                        dve.wait_ge(m["w_hi"], count(g, pos))
                        nc.vector.tensor_tensor(w[pos % 3][:, 1, :, :], raw[pos % 3][:, :, :], r(w[pos % 3][:, 0, :, :]), ALU.subtract).then_inc(m["w_lo"], 1)

                    def hidden(g, j):
                        dve.wait_ge(m["step_ps"], count(g, U0 if j == 0 else U1))
                        for t in range(2):
                            dve.wait_ge(m["si_ok"], 4 * g + 2 * j + t + 1)
                            nc.vector.tensor_tensor(hid[:, t, :], bank[2 + t][:, :], si[:, t, :], ALU.mult).then_inc(m["hid_ok"], 1)

                    def hidden_lo(g, j):
                        for t in range(2):
                            dve.wait_ge(m["h_hi"], 4 * g + 2 * j + t + 1)
                            nc.vector.tensor_tensor(hT[j][:, 1, t, :, :], bank[6 + t][:, :].rearrange("p (c n) -> p c n", c=DC),
                                                    r(hT[j][:, 0, t, :, :]), ALU.subtract).then_inc(m["h_lo"], 1)

                    def x_lo(g):
                        for t in range(2):
                            dve.wait_ge(m["x_hi"], 2 * g + t + 1)
                            nc.vector.tensor_tensor(xT[:, 1, t, :, :], bank[6 + t][:, :].rearrange("p (c n) -> p c n", c=DC),
                                                    r(xT[:, 0, t, :, :]), ALU.subtract).then_inc(m["x_lo"], 1)

                    def body(g, first):
                        if not first:
                            hidden_lo(g - 1, 1)
                        split_lo(g, U0)
                        split_lo(g, G1)
                        split_lo(g, U1)
                        hidden(g, 0)
                        split_lo(g, D0)
                        hidden_lo(g, 0)

                    def tail(g):
                        split_lo(g + 1, G0)
                        x_lo(g + 1)
                        hidden(g, 1)
                        split_lo(g + 1, D1)
                    x_lo(0)
                    split_lo(0, G0)
                    body(0, True)
                    tail(0)
                    with dve.Fori(1, NG - 1) as g:
                        body(g, False)
                        tail(g)
                    body(NG - 1, False)
                    hidden(NG - 1, 1)
                    split_lo(NG, D1)
                    hidden_lo(NG - 1, 1)

                @block.tensor
                def _(pe):
                    def wide(g, pos, banks):
                        pe.wait_ge(m["w_lo"], count(g, pos))
                        for t in range(2):
                            last = products(nc, bank[banks + t][:, :], range(DC), lambda c, h: xT[:, h, t, c, :], lambda c, h: w[pos % 3][:, h, c, :])
                        last.then_inc(m["step_ps"], 1)

                    def down(n, pos, j):
                        pe.wait_ge(m["w_lo"], n)
                        for t in range(2):
                            for c in range(DC):
                                for i, (x, y) in enumerate(PARTS):
                                    last = nc.tensor.matmul(bank[4 + t][:, :], hT[j][:, x, t, c, :], w[pos % 3][:, y, c, :],
                                                            start=j == 0 and c == 0 and i == 0, stop=j == 1 and c == DC - 1 and i == 2,
                                                            skip_group_check=False)
                        last.then_inc(m["step_ps"], 1)

                    def turn_hidden(g, j):
                        for t in range(2):
                            pe.wait_ge(m["hid_ok"], 4 * g + 2 * j + t + 1)
                            for c in range(DC):
                                last = nc.tensor.transpose(bank[6 + t][:, c * P:(c + 1) * P], hid[:, t, c * P:(c + 1) * P], ident[:, :])
                            last.then_inc(m["h_turned"], 1)

                    def turn_x(g):
                        pe.wait_ge(m["x_in"], 16 * g + 16)
                        for t in range(2):
                            for c in range(DC):
                                last = nc.tensor.transpose(bank[6 + t][:, c * P:(c + 1) * P], xin[:, t, c * P:(c + 1) * P], ident[:, :])
                        last.then_inc(m["x_turned"], 1)

                    def body(g, first, last=False):
                        pe.wait_ge(m["x_lo"], 2 * g + 2)
                        wide(g, G0, 0)
                        if not first:
                            pe.wait_ge(m["h_lo"], 4 * g)
                            down(count(g, D1), D1, 1)
                        wide(g, U0, 2)
                        pe.wait_ge(m["si_ok"], 4 * g + 2)
                        wide(g, G1, 0)
                        turn_hidden(g, 0)
                        wide(g, U1, 2)
                        pe.wait_ge(m["h_lo"], 4 * g + 2)
                        if not last:
                            turn_x(g + 1)
                        if not first:
                            pe.wait_ge(m["y_ok"], 2 * g)
                        down(count(g, D0), D0, 0)
                        if not last:
                            pe.wait_ge(m["x_lo"], 2 * g + 4)
                        pe.wait_ge(m["si_ok"], 4 * g + 4)
                        turn_hidden(g, 1)
                    turn_x(0)
                    body(0, True)
                    with pe.Fori(1, NG - 1) as g:
                        body(g, False)
                    body(NG - 1, False, True)
                    pe.wait_ge(m["h_lo"], 4 * NG)
                    down(PIECES * NG, D1, 1)

        with ExitStack() as inner:
            sbi = holder(inner)
            rows = sbi("rows", [P, NT, 2, D])
            got = [sem(f"c_got{t}") for t in range(NT)]
            part, summed, stored = sem("c_part"), sem("c_summed"), sem("c_stored")
            with nc.Block() as block:
                @block.gpsimd
                def _(pool):
                    for t in range(NT):
                        for k in range(2):
                            nc.gpsimd.indirect_dma_start(out=rows[:, t, k, :], out_offset=None, in_=yg[:, :],
                                                         in_offset=bass.IndirectOffsetOnAxis(ap=slot[:, k, t:t + 1], axis=0)).then_inc(got[t], 16)

                @block.vector
                def _(dve):
                    for t in range(NT):
                        dve.wait_ge(got[t], 32)
                        nc.vector.scalar_tensor_tensor(X[:, t, :], rows[:, t, 0, :], gate[:, 0, t:t + 1], X[:, t, :], ALU.mult, ALU.add).then_inc(part, 1)
                        dve.wait_ge(part, t + 1)
                        nc.vector.scalar_tensor_tensor(X[:, t, :], rows[:, t, 1, :], gate[:, 1, t:t + 1], X[:, t, :], ALU.mult, ALU.add).then_inc(summed, 1)

                @block.sync
                def _(sp):
                    out_v = out.rearrange("(t p) d -> t p d", p=P)
                    for t in range(NT):
                        sp.wait_ge(summed, t + 1)
                        sp.dma_start(out_v[t, :, :], X[:, t, :]).then_inc(stored, 16)
                    sp.wait_ge(stored, 16 * NT)


def chunked(w):
    return np.ascontiguousarray(np.asarray(w).reshape(-1, P, w.shape[-1]).transpose(1, 0, 2))


def by_partition(v):
    return np.asarray(v).reshape(-1, P).T


def position_tables():
    f = np.float32
    base = (np.arange(0, E, 2, dtype=f) + f(0.4 * E)) / f(1.4 * E)
    pos = np.arange(S, dtype=f)
    scale = base[None, :] ** (pos[:, None] / f(256))
    angle = pos[:, None] * (f(1.0) / f(10000.0) ** (np.arange(E // 2, dtype=f) / f(E // 2)))[None, :]
    sin, cos = np.sin(angle), np.cos(angle)
    rot = np.stack([cos * scale, sin * scale, cos * (f(1) / scale), sin * (f(1) / scale)], axis=1)
    gammas = f(1.0) - f(2.0) ** (f(-5.0) - np.arange(H, dtype=f))
    tok = np.arange(P)
    diff = (tok[None, :] % S - tok[:, None] % S).astype(f)
    same = (tok[None, :] // S == tok[:, None] // S) & (diff >= 0)
    d = np.where(same[None], gammas[:, None, None] ** np.maximum(diff, 0)[None], f(0))
    decay = d.reshape(DC, 2, P, P).transpose(2, 1, 0, 3)
    return np.tile(rot, (BPT, 1, 1)).astype(f), decay.astype(f)


def arrays_of(inputs):
    g = {k: np.asarray(v) for k, v in inputs.items()}
    out = {"x": g["x"].reshape(TOK, D)}
    ctx = g["ctx_1024"]
    cT = ctx.transpose(0, 2, 1).reshape(NB, DC, P, SK).transpose(0, 2, 1, 3)
    out["ctx"] = cT.reshape(NB, P, DC * SK)
    last = np.zeros((P, DC, P), np.float32)
    last[:, :, :NB] = ctx[:, SK - 1, :].T.reshape(DC, P, NB).transpose(1, 0, 2)
    out["ctx_last"] = last
    for n, k in (("xwq", "Wq"), ("xwk", "Wk"), ("xwv", "Wv"), ("xwo", "Wo")):
        out[n] = chunked(g["L0_xattn_" + k].T)
    thr = g["L0_xattn_raw_thresholds"].reshape(XH)
    vecs = [by_partition(g["L0_xattn_" + k]) for k in ("bq", "bk", "bv")]
    vecs.append(np.repeat(thr.reshape(DC, HPC), XD, axis=1).T)
    vecs.append(np.repeat(np.eye(HPC, dtype=np.float32), XD, axis=0))
    out["vec"] = np.concatenate(vecs, axis=1)
    out["bo_bc"] = np.broadcast_to(g["L0_xattn_bo"], (P, D))
    out["ident"] = np.eye(P, dtype=np.float32)
    out["eye32"] = np.broadcast_to(np.eye(NB, 32, dtype=np.float32), (P, NB, 32))
    split = lambda w: w.transpose(0, 2, 1, 3).reshape(L, D, H, E // 2, 2).transpose(0, 1, 2, 4, 3).reshape(L, D, D)
    wq, wk = split(g["L0_attn_Wq"]), split(g["L0_attn_Wk"])
    wv = g["L0_attn_Wv"].transpose(0, 2, 1, 3).reshape(L, D, D)
    wa = np.concatenate([wq, wk, wv, g["L0_attn_Wg"], g["L0_attn_Wo"]], axis=2)
    out["wa"] = wa.reshape(L, DC, P, 10, 256).transpose(0, 3, 2, 1, 4).reshape(L, 10, P, DC * 256)
    w1 = g["L0_attn_ffn_w1"].reshape(L, DC, P, FC, P).transpose(0, 3, 2, 1, 4).reshape(L, FC, P, D)
    w2 = g["L0_attn_ffn_w2"].reshape(L, FC, P, D)
    out["wf"] = np.concatenate([w1, w2], axis=3)
    out["gn"] = np.broadcast_to(np.stack([g["L0_attn_gn_scale"], g["L0_attn_gn_bias"]], 1)[:, None], (L, P, 2, D))
    out["rot"], out["decay"] = position_tables()
    up, gt, down = g["L0_ffn_w_up"], g["L0_ffn_w_gate"], g["L0_ffn_w_down"]
    pieces = []
    for j in range(2):
        for w in (gt, up):
            pieces.append(w[:, 512 * j:512 * (j + 1), :].transpose(0, 2, 1).reshape(NE, DC, P, 512).transpose(0, 2, 1, 3))
    for j in range(2):
        pieces.append(down[:, :, 512 * j:512 * (j + 1)].transpose(0, 2, 1).reshape(NE, DC, P, D).transpose(0, 2, 1, 3))
    out["we"] = np.stack(pieces, axis=1).reshape(NE, PIECES, P, DC * 512)
    lnv = np.stack([g["L0_attn_" + k].reshape(L, DC, P) for k in ("ln1_scale", "ln1_bias", "ln2_scale", "ln2_bias")], axis=1)
    out["lnv"] = lnv.transpose(0, 3, 1, 2).reshape(L, P, 4 * DC)
    out["rw"] = chunked(g["L0_ffn_router_w"].T)
    col = lambda v: np.broadcast_to(v.astype(np.float32).reshape(-1), (P, v.size))
    i, e = np.arange(P), np.arange(NE)
    out["route_tab"] = np.concatenate([(i[:, None] < i[None, :]).astype(np.float32), np.ones((P, P), np.float32), col(e),
                                       col(e[None, :] < e[:, None]), col(np.arange(NG))], axis=1)
    return {k: np.ascontiguousarray(v) for k, v in out.items()}


def kernel(**inputs):
    import concourse.bacc as bacc
    from concourse.bass_utils import run_bass_kernel_spmd

    nc = bacc.Bacc("TRN2", target_bir_lowering=False, num_devices=1)
    arrays = {f"in_{name}": value for name, value in arrays_of(inputs).items()}
    aps = {name[3:]: nc.dram_tensor(name, value.shape, mybir.dt.from_np(value.dtype), kind="ExternalInput").ap()
           for name, value in arrays.items()}
    out = nc.dram_tensor("out", (TOK, D), F32, kind="ExternalOutput").ap()
    build(nc, aps, out)
    result = run_bass_kernel_spmd(nc, [arrays], core_ids=[0])
    return result.results[0]["out"].reshape(NB, S, D)
```

```python
from contextlib import ExitStack

import numpy as np
import concourse.bass as bass
from concourse import mybir

F32 = mybir.dt.float32
F32R = mybir.dt.float32r
I32 = mybir.dt.int32
U32 = mybir.dt.uint32
ALU = mybir.AluOpType
ACT = mybir.ActivationFunctionType
AX = mybir.AxisListType

P = 128
D = 512
DC = D // P
NB, S = 32, 32
TOK = NB * S
NT = TOK // P
BPT = P // S
SK = 257
SKE = SK + 1
XH = 16
XD = D // XH
HPC = P // XD
L, H, E = 2, 8, 64
F = 2048
FC = F // P
FS = 4
K_BANK = (0, 1, 4, 5)
EARLY = 6
X2_BANK = (1, 2, 3, 4, 5, 1, 2, 3)
WS = 4
NE, HID = 8, 1024
GT = 256
NG = (2 * TOK - NE) // GT + NE
SLOTS = NG * GT
PIECES = 6
NEG_HUGE = -3.0e38
INV_SQRT_XD = float(1.0 / np.sqrt(np.float32(XD)))

PARTS = [(0, 0), (0, 1), (1, 0)]

VEC = {"bq": 0, "bk": 4, "bv": 8, "thr": 12, "head": 16}
NVEC = 20


def r(ap):
    return ap.bitcast(F32)


def wait_alone(eng, semaphore, value):
    value = eng.compute_val(value)
    eng.wait_ge(semaphore, 1)
    eng.wait_ge(semaphore, value)


def products(nc, out, terms, lhs, rhs):
    steps = [(t, a, b) for t in terms for a, b in PARTS]
    for n, (t, a, b) in enumerate(steps):
        last = nc.tensor.matmul(out, lhs(t, a), rhs(t, b), start=n == 0, stop=n == len(steps) - 1)
    return last


def build(nc, a, out, dbg=None):
    with ExitStack() as whole:
        def holder(stack):
            def sb(name, shape, dt=F32):
                return stack.enter_context(nc.sbuf_tensor(name, shape, dt))
            return sb

        taken = []

        def sem(name):
            taken.append(nc.alloc_semaphore(name))
            return taken[-1]

        def end_phase():
            nc.clear_and_free_semaphores(list(taken))
            nc.all_engine_barrier()
            taken.clear()

        keep = holder(whole)
        bank = [whole.enter_context(nc.psum_tensor(f"bank{i}", [P, 512], F32)) for i in range(8)]
        X = keep("X", [P, NT, D])
        ident = keep("ident", [P, P])
        vec = keep("vec", [P, NVEC])
        mhalf = keep("mhalf", [P, 64])
        xg = nc.dram_tensor("xg", (SLOTS, D), F32).ap()
        cross_attention(nc, a, whole, holder, sem, bank, X, ident, vec, mhalf, xg)
        end_phase()
        A = keep("A", [P, NT, D])
        if dbg != "x1":
            yg = nc.dram_tensor("yg", (SLOTS, D), F32).ap()
            retention_layers(nc, a, whole, holder, sem, bank, X, A, ident, vec, mhalf)
            end_phase()
            if dbg is None or dbg == "x3":
                mixture(nc, a, out, whole, holder, sem, bank, X, A, ident, mhalf, xg, yg)
                return
            done = sem("dbg_done")
            with nc.Block() as block:
                @block.sync
                def _(sp):
                    sp.dma_start(out.rearrange("(t p) d -> p t d", p=P), A[:, :, :]).then_inc(done, 16)
                    sp.wait_ge(done, 16)
            return
        if dbg == "x1":
            done = sem("dbg_done")
            with nc.Block() as block:
                @block.sync
                def _(sp):
                    sp.dma_start(out.rearrange("(t p) d -> p t d", p=P), X[:, :, :]).then_inc(done, 16)
                    sp.wait_ge(done, 16)
            return


def cross_attention(nc, a, whole, holder, sem, bank, X, ident, vec, mhalf, xg):
    def col(name, c=0):
        return vec[:, VEC[name] + c:VEC[name] + c + 1]

    with ExitStack() as phase:
        sb = holder(phase)
        wk = sb("wk", [P, 2, DC, D], F32R)
        wv = sb("wv", [P, 2, DC, D], F32R)
        wo = sb("wo", [P, 2, DC, D], F32R)
        qT = sb("qT", [P, 2, DC, TOK], F32R)
        vlast = sb("vlast", [P, 2, D], F32R)
        thr = sb("thr", [P, DC])
        bo_bc = sb("bo_bc", [P, D])
        eye32 = sb("eye32", [P, NB, 32])

        with ExitStack() as inner:
            sbi = holder(inner)
            xT = sbi("xT", [P, 2, DC, TOK], F32R)
            raw = [sbi(f"raw{i}", [P, DC, D]) for i in range(3)]
            wq = sbi("wq", [P, 2, DC, D], F32R)
            craw = sbi("craw", [P, DC, P])
            cl = sbi("cl", [P, 2, DC, P], F32R)
            stats = sbi("stats", [P, NT, 6])
            mv = sbi("mv", [P, NT, 2])
            veps = sbi("veps", [P, NT])
            rstd = sbi("rstd", [P, NT])
            xh = sbi("xh", [P, 2, D])
            qf = sbi("qf", [P, 2, 512])
            th = sbi("th", [P, 5, DC])
            x_in = [sem(f"x_in{i}") for i in range(2)]
            vec_in, id_in, cl_in, misc_in = sem("vec_in"), sem("id_in"), sem("cl_in"), sem("misc_in")
            w_in = [sem(f"w_in{i}") for i in range(4)]
            half_set, x_stats, x_aggr, veps_ok, rstd_ok = sem("half_set"), sem("x_stats"), sem("x_aggr"), sem("veps_ok"), sem("rstd_ok")
            xh_ok, x_turned, xT_hi, xT_lo = sem("xh_ok"), sem("x_turned"), sem("xT_hi"), sem("xT_lo")
            w_hi, w_lo, cl_hi, cl_lo = sem("w_hi"), sem("w_lo"), sem("cl_hi"), sem("cl_lo")
            q_ps, q_f, q_hi, q_lo = sem("q_ps"), sem("q_f"), sem("q_hi"), sem("q_lo")
            vl_ps, vl_hi, vl_lo = sem("vl_ps"), sem("vl_hi"), sem("vl_lo")
            th_act, th_dve = sem("th_act"), sem("th_dve")
            weights = [(a["xwq"], wq), (a["xwv"], wv), (a["xwk"], wk), (a["xwo"], wo)]
            with nc.Block() as block:
                @block.sync
                def _(sp):
                    xv = a["x"].rearrange("(t p) d -> p t d", p=P)
                    for i in range(2):
                        sp.dma_start(X[:, 4 * i:4 * i + 4, :], xv[:, 4 * i:4 * i + 4, :]).then_inc(x_in[i], 16)
                        if i == 0:
                            sp.dma_start(ident[:, :], a["ident"]).then_inc(id_in, 16)
                            sp.dma_start(vec[:, :], a["vec"]).then_inc(vec_in, 16)
                            sp.dma_start(raw[0][:, :, :], weights[0][0]).then_inc(w_in[0], 16)
                    sp.dma_start(craw[:, :, :], a["ctx_last"]).then_inc(cl_in, 16)
                    for i in (1, 2):
                        sp.dma_start(raw[i][:, :, :], weights[i][0]).then_inc(w_in[i], 16)
                    sp.dma_start(bo_bc[:, :], a["bo_bc"]).then_inc(misc_in, 16)
                    sp.dma_start(eye32[:, :, :], a["eye32"]).then_inc(misc_in, 16)
                    sp.wait_ge(w_hi, 1)
                    sp.wait_ge(w_lo, 1)
                    sp.dma_start(raw[0][:, :, :], weights[3][0]).then_inc(w_in[3], 16)
                    sp.wait_ge(misc_in, 32)

                @block.gpsimd
                def _(pool):
                    nc.gpsimd.memset(mhalf[:, :], -0.5).then_inc(half_set, 1)
                    pool.wait_ge(half_set, 1)
                    pool.wait_ge(veps_ok, 1)
                    nc.gpsimd.tensor_tensor(rstd[:, :], veps[:, :], mhalf[:, 0:NT], ALU.pow).then_inc(rstd_ok, 1)

                @block.vector
                def _(dve):
                    for t in range(NT):
                        dve.wait_ge(x_in[t // 4], 16)
                        nc.vector.bn_stats(stats[:, t, :], X[:, t, :]).then_inc(x_stats, 1)
                    for t in range(NT):
                        dve.wait_ge(x_stats, t + 1)
                        nc.vector.bn_aggr(mv[:, t, :], stats[:, t, :]).then_inc(x_aggr, 1)
                    dve.wait_ge(x_aggr, NT)
                    nc.vector.tensor_scalar(veps[:, :], mv[:, :, 1], 1e-5, None, ALU.add).then_inc(veps_ok, 1)
                    dve.wait_ge(w_hi, 1)
                    nc.vector.tensor_tensor(wq[:, 1, :, :], raw[0][:, :, :], r(wq[:, 0, :, :]), ALU.subtract).then_inc(w_lo, 1)
                    dve.wait_ge(rstd_ok, 1)

                    def turned_lo(t):
                        dve.wait_ge(xT_hi, t + 1)
                        nc.vector.tensor_tensor(xT[:, 1, :, t * P:(t + 1) * P], bank[t % 2][:, :].rearrange("p (c n) -> p c n", c=DC),
                                                r(xT[:, 0, :, t * P:(t + 1) * P]), ALU.subtract).then_inc(xT_lo, 1)
                    for t in range(NT):
                        if t >= 2:
                            dve.wait_ge(x_turned, t - 1)
                        nc.vector.tensor_scalar(xh[:, t % 2, :], X[:, t, :], mv[:, t, 0:1], rstd[:, t:t + 1],
                                                ALU.subtract, ALU.mult).then_inc(xh_ok, 1)
                        if t >= 1:
                            turned_lo(t - 1)
                    turned_lo(NT - 1)
                    for i in (1, 2):
                        dve.wait_ge(w_hi, i + 1)
                        nc.vector.tensor_tensor(weights[i][1][:, 1, :, :], raw[i][:, :, :], r(weights[i][1][:, 0, :, :]), ALU.subtract).then_inc(w_lo, 1)
                        if i == 1:
                            dve.wait_ge(cl_hi, 1)
                            nc.vector.tensor_tensor(cl[:, 1, :, :], craw[:, :, :], r(cl[:, 0, :, :]), ALU.subtract).then_inc(cl_lo, 1)
                        for n in range(4 * i - 4, 4 * i):
                            dc, half = n // 2, n % 2
                            dve.wait_ge(q_hi, n + 1)
                            hi = qT[:, 0, dc, half * 512:(half + 1) * 512]
                            nc.vector.scalar_tensor_tensor(qT[:, 1, dc, half * 512:(half + 1) * 512], bank[2 + n % 2][:, :], col("bq", dc),
                                                           r(hi), ALU.add, ALU.subtract).then_inc(q_lo, 1)
                    dve.wait_ge(w_hi, 4)
                    nc.vector.tensor_tensor(wo[:, 1, :, :], raw[0][:, :, :], r(wo[:, 0, :, :]), ALU.subtract).then_inc(w_lo, 1)
                    dve.wait_ge(vl_hi, 1)
                    nc.vector.tensor_tensor(vlast[:, 1, :], bank[4][:, :], r(vlast[:, 0, :]), ALU.subtract).then_inc(vl_lo, 1)
                    dve.wait_ge(vec_in, 16)
                    raw_thr = vec[:, VEC["thr"]:VEC["thr"] + DC]
                    nc.vector.scalar_tensor_tensor(th[:, 0, :], raw_thr, -1.0, raw_thr, ALU.mult, ALU.max).then_inc(th_dve, 1)
                    nc.vector.tensor_scalar(th[:, 1, :], raw_thr, 0.0, None, ALU.max).then_inc(th_dve, 1)
                    dve.wait_ge(th_act, 2)
                    dve.wait_ge(th_dve, 2)
                    nc.vector.tensor_tensor(th[:, 4, :], th[:, 1, :], th[:, 3, :], ALU.add).then_inc(th_dve, 1)
                    dve.wait_ge(th_dve, 3)
                    nc.vector.tensor_scalar(thr[:, :], th[:, 4, :], float(np.sqrt(np.float32(XD))), None, ALU.mult).then_inc(th_dve, 1)

                @block.scalar
                def _(act):
                    act.wait_ge(w_in[0], 16)
                    nc.scalar.activation(wq[:, 0, :, :], raw[0][:, :, :], ACT.Copy).then_inc(w_hi, 1)
                    act.wait_ge(cl_in, 16)
                    nc.scalar.activation(cl[:, 0, :, :], craw[:, :, :], ACT.Copy).then_inc(cl_hi, 1)
                    act.wait_ge(w_in[1], 16)
                    nc.scalar.activation(wv[:, 0, :, :], raw[1][:, :, :], ACT.Copy).then_inc(w_hi, 1)
                    for t in range(NT):
                        act.wait_ge(x_turned, t + 1)
                        nc.scalar.activation(xT[:, 0, :, t * P:(t + 1) * P], bank[t % 2][:, :].rearrange("p (c n) -> p c n", c=DC),
                                             ACT.Copy).then_inc(xT_hi, 1)
                    act.wait_ge(w_in[2], 16)
                    nc.scalar.activation(wk[:, 0, :, :], raw[2][:, :, :], ACT.Copy).then_inc(w_hi, 1)
                    act.wait_ge(vec_in, 16)
                    for n in range(8):
                        dc, half = n // 2, n % 2
                        act.wait_ge(q_ps, n + 1)
                        nc.scalar.activation(qT[:, 0, dc, half * 512:(half + 1) * 512], bank[2 + n % 2][:, :], ACT.Identity,
                                             bias=col("bq", dc)).then_inc(q_hi, 1)
                    act.wait_ge(w_in[3], 16)
                    nc.scalar.activation(wo[:, 0, :, :], raw[0][:, :, :], ACT.Copy).then_inc(w_hi, 1)
                    act.wait_ge(vl_ps, 1)
                    nc.scalar.activation(vlast[:, 0, :], bank[4][:, :], ACT.Copy).then_inc(vl_hi, 1)
                    act.wait_ge(th_dve, 1)
                    nc.scalar.activation(th[:, 2, :], th[:, 0, :], ACT.Exp, scale=-1.0).then_inc(th_act, 1)
                    act.wait_ge(th_act, 1)
                    nc.scalar.activation(th[:, 3, :], th[:, 2, :], ACT.Ln, bias=1.0).then_inc(th_act, 1)

                @block.tensor
                def _(pe):
                    pe.wait_ge(id_in, 16)
                    for t in range(NT):
                        pe.wait_ge(xh_ok, t + 1)
                        if t >= 2:
                            pe.wait_ge(xT_hi, t - 1)
                            pe.wait_ge(xT_lo, t - 1)
                        for c in range(DC):
                            last = nc.tensor.transpose(bank[t % 2][:, c * P:(c + 1) * P], xh[:, t % 2, c * P:(c + 1) * P], ident[:, :])
                        last.then_inc(x_turned, 1)
                    pe.wait_ge(w_lo, 1)
                    pe.wait_ge(xT_lo, NT)
                    for n in range(8):
                        dc, half = n // 2, n % 2
                        if n >= 2:
                            pe.wait_ge(q_lo, n - 1)
                        products(nc, bank[2 + n % 2][:, :], range(DC), lambda c, h: wq[:, h, c, dc * P:(dc + 1) * P],
                                 lambda c, h: xT[:, h, c, half * 512:(half + 1) * 512]).then_inc(q_ps, 1)
                    pe.wait_ge(w_lo, 2)
                    pe.wait_ge(cl_lo, 1)
                    products(nc, bank[4][:, :], range(DC), lambda c, h: cl[:, h, c, :], lambda c, h: wv[:, h, c, :]).then_inc(vl_ps, 1)

        with ExitStack() as inner:
            sbi = holder(inner)
            craw = [sbi(f"ctxraw{i}", [P, DC, SK]) for i in range(2)]
            ctx = [sbi(f"ctx{i}", [P, 2, DC, SKE], F32R) for i in range(2)]
            kT = sbi("kT", [P, 2, DC, SKE], F32R)
            v = [sbi(f"v{i}", [P, 2, 2, D], F32R) for i in range(2)]
            qbd = sbi("qbd", [P, 2, DC, P], F32R)
            u = sbi("u", [P, DC, SKE])
            ex = sbi("ex", [P, DC, SKE])
            pr = sbi("pr", [P, DC, SKE])
            umax = sbi("umax", [P, DC])
            keepany = sbi("keepany", [P, DC])
            sc = sbi("sc", [P, DC])
            nb = sbi("nb", [P, DC])
            floor = sbi("floor", [P, DC])
            psums = sbi("psums", [P, DC])
            rsum = sbi("rsum", [P, DC])
            plast = sbi("plast", [P, DC, 32])
            pT = sbi("pT", [P, 2, 2, DC, P], F32R)
            pTl = sbi("pTl", [32, 2, DC, P], F32R)
            oT = sbi("oT", [P, DC, P])
            zero = sbi("zero", [P, D])
            oT_hl = sbi("oT_hl", [P, 2, DC, P], F32R)
            ctx_in = [sem("ctx_in0"), sem("ctx_in1")]
            zeroed, ctx_hi, ctx_lo = sem("zeroed"), sem("ctx_hi"), sem("ctx_lo")
            k_ps, v_ps, s_ps, p_turned, pv_ps, o_ps = (sem(n) for n in ("k_ps", "v_ps", "s_ps", "p_turned", "pv_ps", "o_ps"))
            k_hi, k_lo, v_hi, v_lo = (sem(n) for n in ("k_hi", "k_lo", "v_hi", "v_lo"))
            u_ok, soft_ok, ex_ok, pr_ok, rsum_ok, pn_ok, plast_ok = (
                sem(n) for n in ("u_ok", "soft_ok", "ex_ok", "pr_ok", "rsum_ok", "pn_ok", "plast_ok"))
            pT_hi, pT_lo, oT_ok, oT_hi, oT_lo, x1_sum, x1_ok = (
                sem(n) for n in ("pT_hi", "pT_lo", "oT_ok", "oT_hi", "oT_lo", "x1_sum", "x1_ok"))
            qbd_ok, filled = sem("qbd_ok"), sem("filled")
            ctx_view = a["ctx"]

            with nc.Block() as block:
                @block.sync
                def _(sp):
                    def load(it, k):
                        b = BPT * it + k
                        sp.dma_start(craw[k % 2][:, :, :], ctx_view[bass.ds(b, 1), :, :].rearrange("o p (c n) -> p (o c) n", c=DC)).then_inc(ctx_in[k % 2], 16)
                    ZT = SLOTS // P // NT
                    xg_tiles = xg.rearrange("(n p) d -> p n d", p=P)
                    for k in range(BPT):
                        if k >= 2:
                            sp.wait_ge(ctx_hi, k - 1)
                            sp.wait_ge(ctx_lo, k - 1)
                        load(0, k)
                    sp.wait_ge(zeroed, 3)
                    with sp.Fori(1, NT) as it:
                        for k in range(BPT):
                            sp.wait_ge(ctx_hi, BPT * it + k - 1)
                            sp.wait_ge(ctx_lo, BPT * it + k - 1)
                            load(it, k)
                        sp.dma_start(xg_tiles[:, bass.ds(ZT * (it - 1), ZT), :], zero[:, :].unsqueeze(1).broadcast_to([P, ZT, D])).then_inc(filled, 16)
                    rest = ZT * (NT - 1)
                    sp.dma_start(xg_tiles[:, rest:, :], zero[:, :].unsqueeze(1).broadcast_to([P, SLOTS // P - rest, D])).then_inc(filled, 16)
                    sp.wait_ge(filled, 16 * NT)

                @block.gpsimd
                def _(pool):
                    for i in range(2):
                        nc.gpsimd.memset(r(ctx[i][:, :, :, SK:SKE]), 0.0).then_inc(zeroed, 1)
                    nc.gpsimd.memset(zero[:, :], 0.0).then_inc(zeroed, 1)

                    def context_lo(it, k, b):
                        pool.wait_ge(ctx_hi, b + 1)
                        nc.gpsimd.tensor_tensor(ctx[k % 2][:, 1, :, 0:SK], craw[k % 2][:, :, :], r(ctx[k % 2][:, 0, :, 0:SK]),
                                                ALU.subtract).then_inc(ctx_lo, 1)

                    def spread_q(b):
                        src = r(qT[:, :, :, :]).rearrange("p h c n -> p (h c) n")[:, :, bass.ds(b * S, S)]
                        nc.gpsimd.tensor_tensor(qbd[:, :, :, :].rearrange("p h c (g n) -> p (h c) g n", g=HPC),
                                                src.unsqueeze(2).broadcast_to([P, 2 * DC, HPC, S]),
                                                vec[:, VEC["head"]:VEC["head"] + HPC].unsqueeze(1).unsqueeze(3).broadcast_to([P, 2 * DC, HPC, S]),
                                                ALU.mult).then_inc(qbd_ok, 1)

                    def normalise(b):
                        pool.wait_ge(rsum_ok, b + 1)
                        nc.gpsimd.tensor_tensor(pr[:, :, 0:SK], pr[:, :, 0:SK], rsum[:, :].unsqueeze(2).broadcast_to([P, DC, SK]),
                                                ALU.mult).then_inc(pn_ok, 1)
                        pool.wait_ge(pn_ok, b + 1)
                        nc.gpsimd.tensor_tensor(plast[:, :, :], pr[:, :, SK - 1:SK].broadcast_to([P, DC, 32]),
                                                eye32[:, bass.ds(b, 1), :].broadcast_to([P, DC, 32]), ALU.mult).then_inc(plast_ok, 1)

                    def body(it, first, last):
                        for k in range(BPT):
                            b = BPT * it + k
                            if not (first and k == 0):
                                pool.wait_ge(s_ps, DC * b)
                            spread_q(b)
                            if not (last and k == BPT - 1):
                                if not (first and k == 0):
                                    pool.wait_ge(v_ps, 2 * b)
                                context_lo(it, k + 1, b + 1)
                            if k == 2 and not first:
                                add_bias(it - 1)
                            normalise(b)

                    def add_bias(t):
                        pool.wait_ge(x1_sum, t + 1)
                        xt = X[:, bass.ds(t, 1), :].rearrange("p o d -> p (o d)")
                        nc.gpsimd.tensor_tensor(xt, xt, bo_bc[:, :], ALU.add).then_inc(x1_ok, 1)
                    context_lo(0, 0, 0)
                    body(0, True, False)
                    with pool.Fori(1, NT - 1) as it:
                        body(it, False, False)
                    body(NT - 1, False, True)
                    add_bias(NT - 1)

                @block.scalar
                def _(act):
                    def context_hi(k, use, b):
                        act.wait_ge(ctx_in[k % 2], 16 * use)
                        nc.scalar.activation(ctx[k % 2][:, 0, :, 0:SK], craw[k % 2][:, :, :], ACT.Copy).then_inc(ctx_hi, 1)

                    def exps(b):
                        act.wait_ge(soft_ok, 5 * b + 5)
                        for c in range(DC):
                            nc.scalar.activation(ex[:, c, 0:SK], u[:, c, 0:SK], ACT.Exp, bias=nb[:, c:c + 1], scale=sc[:, c:c + 1]).then_inc(ex_ok, 1)

                    def turned(b):
                        for kt in range(2):
                            act.wait_ge(p_turned, 3 * b + kt + 1)
                            nc.scalar.activation(pT[:, 0, kt, :, :], bank[4 + kt][:, :].rearrange("p (c n) -> p c n", c=DC), ACT.Copy).then_inc(pT_hi, 1)
                        act.wait_ge(p_turned, 3 * b + 3)
                        nc.scalar.activation(pTl[:, 0, :, :], bank[6][0:32, :].rearrange("p (c n) -> p c n", c=DC), ACT.Copy).then_inc(pT_hi, 1)

                    def heads_hi(t):
                        act.wait_ge(oT_ok, HPC * BPT * (t + 1))
                        nc.scalar.activation(oT_hl[:, 0, :, :], oT[:, :, :], ACT.Copy).then_inc(oT_hi, 1)

                    def body(it, first, last):
                        for k in range(BPT):
                            b = BPT * it + k
                            begin = first and k == 0
                            if begin:
                                act.wait_ge(zeroed, 3)
                            for dc in range(DC):
                                act.wait_ge(k_ps, DC * b + dc + 1)
                                nc.scalar.activation(kT[:, 0, dc, :], bank[K_BANK[dc]][:, 0:SKE], ACT.Identity, bias=col("bk", dc)).then_inc(k_hi, 1)
                                if dc == 1 and k == 1 and not first:
                                    heads_hi(it - 1)
                                if dc == 1 and not (last and k == BPT - 1):
                                    context_hi(k + 1, 2 * it + (k + 1) // 2 + 1, b + 1)
                            act.wait_ge(v_ps, 2 * b + 1)
                            nc.scalar.activation(v[k % 2][:, 0, 0, :], bank[0][:, :], ACT.Copy).then_inc(v_hi, 1)
                            if not begin:
                                turned(b - 1)
                            act.wait_ge(v_ps, 2 * b + 2)
                            nc.scalar.activation(v[k % 2][:, 0, 1, :], bank[1][:, :], ACT.Copy).then_inc(v_hi, 1)
                            exps(b)
                    context_hi(0, 1, 0)
                    body(0, True, False)
                    with act.Fori(1, NT - 1) as it:
                        body(it, False, False)
                    body(NT - 1, False, True)
                    turned(NB - 1)
                    heads_hi(NT - 1)

                @block.vector
                def _(dve):
                    def weigh(b):
                        for c in range(DC):
                            dve.wait_ge(ex_ok, DC * b + c + 1)
                            nc.vector.scalar_tensor_tensor(pr[:, c, 0:SK], u[:, c, 0:SK], floor[:, c:c + 1], ex[:, c, 0:SK],
                                                           ALU.is_gt, ALU.mult, accum_out=psums[:, c:c + 1]).then_inc(pr_ok, 1)

                    def reciprocal(b):
                        dve.wait_ge(pr_ok, DC * (b + 1))
                        nc.vector.reciprocal(rsum[:, :], psums[:, :]).then_inc(rsum_ok, 1)

                    def turned_lo(b):
                        for kt in range(2):
                            dve.wait_ge(pT_hi, 3 * b + kt + 1)
                            nc.vector.tensor_tensor(pT[:, 1, kt, :, :], bank[4 + kt][:, :].rearrange("p (c n) -> p c n", c=DC),
                                                    r(pT[:, 0, kt, :, :]), ALU.subtract).then_inc(pT_lo, 1)
                        dve.wait_ge(pT_hi, 3 * b + 3)
                        nc.vector.tensor_tensor(pTl[:, 1, :, :], bank[6][0:32, :].rearrange("p (c n) -> p c n", c=DC),
                                                r(pTl[:, 0, :, :]), ALU.subtract).then_inc(pT_lo, 1)

                    def threshold(b, cs):
                        for c in cs:
                            dve.wait_ge(s_ps, DC * b + c + 1)
                            nc.vector.tensor_scalar(u[:, c, 0:SK], bank[2 + c % 2][:, 0:SK], thr[:, c:c + 1], None,
                                                    ALU.subtract, ALU.max, accum_out=umax[:, c:c + 1]).then_inc(u_ok, 1)

                    def heads(k, b):
                        dve.wait_ge(pv_ps, b + 1)
                        for g in range(HPC):
                            rows = slice(g * XD, (g + 1) * XD)
                            nc.vector.tensor_tensor(oT[rows, :, k * S:(k + 1) * S],
                                                    bank[7][rows, :].rearrange("p (c n) -> p c n", c=DC)[:, :, g * S:(g + 1) * S],
                                                    vec[rows, VEC["bv"]:VEC["bv"] + DC].unsqueeze(2).broadcast_to([XD, DC, S]),
                                                    ALU.add).then_inc(oT_ok, 1)

                    def softmax_terms(b):
                        n = 5 * b
                        dve.wait_ge(u_ok, DC * b + DC)
                        nc.vector.tensor_scalar(keepany[:, :], umax[:, :], 0.0, None, ALU.is_gt).then_inc(soft_ok, 1)
                        nc.vector.tensor_scalar(floor[:, :], umax[:, :], 0.0, NEG_HUGE, ALU.is_le, ALU.mult).then_inc(soft_ok, 1)
                        dve.wait_ge(soft_ok, n + 2)
                        nc.vector.tensor_scalar(sc[:, :], keepany[:, :], INV_SQRT_XD, None, ALU.mult).then_inc(soft_ok, 1)
                        dve.wait_ge(soft_ok, n + 3)
                        nc.vector.tensor_tensor(nb[:, :], sc[:, :], umax[:, :], ALU.mult).then_inc(soft_ok, 1)
                        dve.wait_ge(soft_ok, n + 4)
                        nc.vector.tensor_scalar(nb[:, :], nb[:, :], -1.0, None, ALU.mult).then_inc(soft_ok, 1)

                    def project_lo(t):
                        dve.wait_ge(oT_hi, t + 1)
                        nc.vector.tensor_tensor(oT_hl[:, 1, :, :], oT[:, :, :], r(oT_hl[:, 0, :, :]), ALU.subtract).then_inc(oT_lo, 1)

                    def add_x(t):
                        dve.wait_ge(o_ps, t + 1)
                        xt = X[:, bass.ds(t, 1), :].rearrange("p o d -> p (o d)")
                        nc.vector.tensor_tensor(xt, bank[7][:, :], xt, ALU.add).then_inc(x1_sum, 1)

                    def body(it, first):
                        for k in range(BPT):
                            b = BPT * it + k
                            begin = first and k == 0
                            for dc in range(DC):
                                dve.wait_ge(k_hi, DC * b + dc + 1)
                                nc.vector.scalar_tensor_tensor(kT[:, 1, dc, :], bank[K_BANK[dc]][:, 0:SKE], col("bk", dc), r(kT[:, 0, dc, :]),
                                                               ALU.add, ALU.subtract).then_inc(k_lo, 1)
                                if dc == 1 and k == 1 and not first:
                                    project_lo(it - 1)

                            def value_lo(kt):
                                dve.wait_ge(v_hi, 2 * b + kt + 1)
                                nc.vector.tensor_tensor(v[k % 2][:, 1, kt, :], bank[kt][:, :], r(v[k % 2][:, 0, kt, :]), ALU.subtract).then_inc(v_lo, 1)
                            value_lo(0)
                            if k == 1 and not first:
                                add_x(it - 1)
                            threshold(b, (0, 1))
                            if not begin:
                                turned_lo(b - 1)
                            value_lo(1)
                            threshold(b, (2, 3))
                            softmax_terms(b)
                            weigh(b)
                            reciprocal(b)
                            if not begin:
                                heads((k - 1) % BPT, b - 1)
                    body(0, True)
                    with dve.Fori(1, NT) as it:
                        body(it, False)
                    turned_lo(NB - 1)
                    heads(BPT - 1, NB - 1)
                    project_lo(NT - 1)
                    add_x(NT - 1)

                @block.tensor
                def _(pe):
                    def turn(b):
                        pe.wait_ge(pn_ok, b + 1)
                        for kt in range(2):
                            for c in range(DC):
                                last = nc.tensor.transpose(bank[4 + kt][:, c * P:(c + 1) * P], pr[:, c, kt * P:(kt + 1) * P], ident[:, :])
                            last.then_inc(p_turned, 1)
                        pe.wait_ge(plast_ok, b + 1)
                        for c in range(DC):
                            last = nc.tensor.transpose(bank[6][0:32, c * P:(c + 1) * P], plast[:, c, :], ident[:, :])
                        last.then_inc(p_turned, 1)

                    def attend(k, b, t_sum):
                        pe.wait_ge(pT_lo, 3 * b + 3)
                        if t_sum is not None:
                            pe.wait_ge(x1_sum, t_sum)
                        for c in range(DC):
                            cols = slice(c * P, (c + 1) * P)
                            steps = [(lambda h, kt=kt: v[k % 2][:, h, kt, cols], lambda h, kt=kt: pT[:, h, kt, c, :]) for kt in range(2)]
                            steps.append((lambda h: vlast[0:32, h, cols], lambda h: pTl[:, h, c, :]))
                            last = products(nc, bank[7][:, cols], range(3), lambda s, h: steps[s][0](h), lambda s, h: steps[s][1](h))
                        last.then_inc(pv_ps, 1)

                    def score(b, cs, begin):
                        for c in cs:
                            pe.wait_ge(k_lo, DC * b + c + 1)
                            if not (begin and c < 2):
                                pe.wait_ge(u_ok, DC * b + c - 1)
                            if c == 0:
                                pe.wait_ge(qbd_ok, b + 1)
                            products(nc, bank[2 + c % 2][:, 0:SKE], range(1), lambda _, h: qbd[:, h, c, :],
                                     lambda _, h: kT[:, h, c, :]).then_inc(s_ps, 1)

                    def project(t):
                        pe.wait_ge(oT_lo, t + 1)
                        products(nc, bank[7][:, :], range(DC), lambda c, h: oT_hl[:, h, c, :], lambda c, h: wo[:, h, c, :]).then_inc(o_ps, 1)

                    def body(it, first):
                        for k in range(BPT):
                            b = BPT * it + k
                            begin = first and k == 0
                            pe.wait_ge(ctx_lo, b + 1)
                            for dc in range(DC):
                                if dc < 2 and not begin:
                                    pe.wait_ge(v_lo, 2 * b - 1 + dc)
                                products(nc, bank[K_BANK[dc]][:, 0:SKE], range(DC), lambda c, h: wk[:, h, c, dc * P:(dc + 1) * P],
                                         lambda c, h: ctx[k % 2][:, h, c, :]).then_inc(k_ps, 1)

                            def value(kt):
                                pe.wait_ge(k_lo, DC * b + 1 + kt)
                                products(nc, bank[kt][:, :], range(DC), lambda c, h: ctx[k % 2][:, h, c, kt * P:(kt + 1) * P],
                                         lambda c, h: wv[:, h, c, :]).then_inc(v_ps, 1)
                            value(0)
                            if k == 1 and not first:
                                project(it - 1)
                            if not begin:
                                pe.wait_ge(k_lo, DC * b + DC)
                                turn(b - 1)
                            score(b, (0, 1), begin)
                            value(1)
                            score(b, (2, 3), begin)
                            if not begin:
                                if not (first and k == 1):
                                    pe.wait_ge(oT_ok, HPC * (b - 1))
                                attend(k - 1, b - 1, it if k == 1 and not first else None)
                    body(0, True)
                    with pe.Fori(1, NT) as it:
                        body(it, False)
                    turn(NB - 1)
                    pe.wait_ge(oT_ok, HPC * (NB - 1))
                    attend(BPT - 1, NB - 1, None)
                    project(NT - 1)


def retention_layers(nc, a, whole, holder, sem, bank, X, A, ident, vec, mhalf):
    with ExitStack() as phase:
        sb = holder(phase)
        gn_bc = sb("gn_bc", [P, 2, D])
        lnv = sb("lnv", [P, 2, 2, DC])
        rot = sb("rot", [P, 4, E // 2])
        decay = sb("decay", [P, 2, DC, P])
        mv = sb("r_mv", [P, NT, 2])
        stats = sb("r_stats", [P, NT, 6])
        veps = sb("r_veps", [P, NT])
        rstd = sb("r_rstd", [P, NT])
        xh = [sb(f"r_xh{i}", [P, D]) for i in range(2)]
        xf = [sb(f"xf{i}", [P, DC, P]) for i in range(2)]
        att = ExitStack()
        sba = holder(att)
        wq, wk = (sba(n, [P, 2, DC, D], F32R) for n in ("r_wq", "r_wk"))
        wraw = [sba(f"wraw{i}", [P, DC, 256]) for i in range(WS)]
        wv, wg, wo = (sba(n, [P, 2, DC, D], F32R) for n in ("r_wv", "r_wg", "r_wo"))
        matrices = (wq, wk, wv, wg, wo)
        xn = [sba(f"xn{i}", [P, 2, DC, P], F32R) for i in range(2)]
        rc = sba("rc", [P, 2, D])
        rs = sba("rs", [P, 2, D])
        qk = sba("qk", [P, 2, D])
        qkT = sba("qkT", [P, 2, 2, DC, P], F32R)
        vv = sba("vv", [P, 2, D], F32R)
        sw = sba("sw", [P, D])
        sws = sba("sws", [P, 2, D])
        pf = sba("pf", [P, 2, DC, P])
        p_hl = sba("p_hl", [P, 2, 2, DC, P], F32R)
        gst = sba("gst", [P, H, 6])
        gmv = sba("gmv", [P, H, 2])
        gve = sba("gve", [P, H])
        grs = sba("grs", [P, H])
        y = sba("y", [P, D])
        yT = sba("yT", [P, 2, DC, P], F32R)
        att.close()
        ff = ExitStack()
        sbf = holder(ff)
        x2T = sbf("x2T", [P, 2, DC, TOK], F32R)
        fraw = [sbf(f"fraw{i}", [P, 2 * D]) for i in range(FS)]
        fw = [sbf(f"fw{i}", [P, 2, 2 * D], F32R) for i in range(FS)]
        hf32 = [sbf(f"hf32_{i}", [P, 512]) for i in range(2)]
        hh = [sbf(f"hh{i}", [P, 2, 512], F32R) for i in range(2)]
        ff.close()

        names = """tab_in gn_in w_hi w_lo a0_ok st_ok ag_ok ve_ok rs_ok xh_ok x_turned xf_ok xn_hi xn_lo
            q_ps k_ps v_ps g_ps rc_ok qk_ok qk_turned qkT_hi qkT_lo v_hi v_lo sw_ok sws_ok s_ps pf_ok p_hi p_lo o_ps
            gst_ok gmv_ok gve_ok grs_ok cen_ok hn_ok ya_ok y_ok y_turned yT_hi yT_lo wo_ps res_ok
            st2_ok ag2_ok ve2_ok rs2_ok xh2_ok x2_turned xf2_ok x2_hi x2_lo
            f_hi f_lo up_ps h_ok h_hi h_lo down_ps ffn_ok ln0_st ln0_ag ln0_ve ln0_rs""".split()
        m = {n: sem("r_" + n) for n in names}
        w_in = [sem(f"r_w_in{i}") for i in range(WS)]
        f_in = [sem(f"r_f_in{i}") for i in range(FS)]

        def tile_of(tensor, t):
            if isinstance(t, int):
                return tensor[:, t, :]
            return tensor[:, bass.ds(t, 1), :].rearrange("p o d -> p (o d)")

        def pairs(eng, body):
            body(0, True, False)
            with eng.Fori(1, NT // 2 - 1) as it:
                body(it, False, False)
            body(NT // 2 - 1, False, True)

        halves = [slice(0, 32), slice(32, 64)]

        def split_halves(ap):
            return ap.rearrange("p (h two e) -> p h two e", two=2, e=E // 2)

        with nc.Block() as block:
            @block.sync
            def _(sp):
                sp.dma_start(rot[:, :, :], a["rot"]).then_inc(m["tab_in"], 16)
                sp.dma_start(decay[:, :, :, :], a["decay"]).then_inc(m["tab_in"], 16)
                with sp.Fori(0, L) as layer:
                    sp.wait_ge(m["ffn_ok"], 8 * layer + 1)
                    sp.dma_start(gn_bc[:, :, :], a["gn"][bass.ds(layer, 1), :, :, :].rearrange("o p k d -> p (o k) d")).then_inc(m["gn_in"], 16)
                    sp.dma_start(lnv[:, :, :, :], a["lnv"][bass.ds(layer, 1), :, :].rearrange("o p n -> p (o n)")).then_inc(m["gn_in"], 16)
                    for j in range(10):
                        if j >= WS:
                            sp.wait_ge(m["w_hi"], 10 * layer + j - WS + 1)
                            sp.wait_ge(m["w_lo"], 10 * layer + j - WS + 1)
                        sp.dma_start(wraw[j % WS][:, :, :], a["wa"][bass.ds(layer, 1), j, :, :].rearrange("o p (c n) -> p (o c) n", c=DC)).then_inc(w_in[j % WS], 16)
                    wait_alone(sp, m["w_hi"], 10 * layer + 10)
                    sp.wait_ge(m["w_lo"], 10 * layer + 10)
                    with sp.Fori(0, 2) as half:
                        with sp.Fori(0, FC // FS) as it:
                            for k in range(FS):
                                n = 32 * layer + 16 * half + FS * it + k
                                sp.wait_ge(m["f_hi"], n + 1)
                                sp.wait_ge(m["f_lo"], n + 1)
                                sp.dma_start(fraw[k][:, :], a["wf"][bass.ds(layer, 1), bass.ds(FS * it + k, 1), :, :].rearrange("o q p n -> p (o q n)")).then_inc(f_in[k], 16)

            @block.gpsimd
            def _(pool):
                def root(src, dst, n, ok, value, done):
                    pool.wait_ge(ok, value)
                    nc.gpsimd.tensor_tensor(dst, src, mhalf[:, 0:n], ALU.pow).then_inc(done, 1)
                root(veps[:, :], rstd[:, :], NT, m["ln0_ve"], 1, m["ln0_rs"])
                with pool.Fori(0, L) as layer:
                    n0 = 8 * layer

                    def combine(n, j):
                        pool.wait_ge(m["rc_ok"], 4 * n + 2 * j + 2)
                        c4, s4, o4 = (split_halves(z[:, j, :]) for z in (rc, rs, qk))
                        nc.gpsimd.tensor_tensor(o4[:, :, 0, :], c4[:, :, 0, :], s4[:, :, 1, :], ALU.subtract).then_inc(m["qk_ok"], 1)
                        nc.gpsimd.tensor_tensor(o4[:, :, 1, :], c4[:, :, 1, :], s4[:, :, 0, :], ALU.add).then_inc(m["qk_ok"], 1)

                    def norm_root(n):
                        root(veps[:, 0:1], rstd[:, 0:1], 1, m["ve_ok"], n + 1, m["rs_ok"])
                    norm_root(n0)
                    pool.wait_ge(m["gn_in"], 32 * layer + 32)

                    def body(it, first, last):
                        for k in range(2):
                            n = n0 + 2 * it + k
                            begin, end = first and k == 0, last and k == 1
                            if not end:
                                norm_root(n + 1)
                            combine(n, 0)
                            combine(n, 1)
                            if not begin:
                                root(gve[:, :], grs[:, :], H, m["gve_ok"], n, m["grs_ok"])
                                pool.wait_ge(m["ya_ok"], n)
                                pool.wait_ge(m["y_ok"], n)
                            pool.wait_ge(m["sw_ok"], n + 1)
                            for j in range(2):
                                nc.gpsimd.tensor_tensor(sws[:, j, :], sw[:, :], gn_bc[:, j, :], ALU.mult).then_inc(m["sws_ok"], 1)
                            for j in range(2):
                                pool.wait_ge(m["p_hi"], 2 * n + j + 1)
                                nc.gpsimd.tensor_tensor(p_hl[:, 1, j, :, :], pf[:, j, :, :], r(p_hl[:, 0, j, :, :]), ALU.subtract).then_inc(m["p_lo"], 1)
                    pairs(pool, body)
                    root(veps[:, 0:EARLY], rstd[:, 0:EARLY], EARLY, m["ve2_ok"], 2 * layer + 1, m["rs2_ok"])
                    root(gve[:, :], grs[:, :], H, m["gve_ok"], n0 + 8, m["grs_ok"])
                    root(veps[:, EARLY:], rstd[:, EARLY:], NT - EARLY, m["ve2_ok"], 2 * layer + 2, m["rs2_ok"])

            @block.scalar
            def _(act):
                for _ in range(FS):
                    act.sem_inc(m["f_hi"], 1)
                    act.sem_inc(m["down_ps"], 1)
                with act.Fori(0, L) as layer:
                    n0 = 8 * layer

                    def weights_hi(j):
                        act.wait_ge(w_in[j % WS], 16 * len(range(j % WS, 10, WS)) * layer + 16 * (j // WS) + 16)
                        nc.scalar.activation(matrices[j // 2][:, 0, :, j % 2 * 256:(j % 2 + 1) * 256], wraw[j % WS][:, :, :], ACT.Copy).then_inc(m["w_hi"], 1)

                    def scale_columns(dst, name, bk, turned, value, done):
                        act.wait_ge(turned, value)
                        for c in range(DC):
                            nc.scalar.activation(dst[:, c, :], bk[:, c * P:(c + 1) * P], ACT.Identity, scale=lnv[:, name, 0, c:c + 1],
                                                 bias=lnv[:, name, 1, c:c + 1]).then_inc(done, 1)

                    def norm_hi(n, k):
                        scale_columns(xf[0], 0, bank[6], m["x_turned"], n + 1, m["xf_ok"])
                        act.wait_ge(m["xf_ok"], DC * (n + 1))
                        nc.scalar.activation(xn[k][:, 0, :, :], xf[0][:, :, :], ACT.Copy).then_inc(m["xn_hi"], 1)

                    weights_hi(0)
                    act.wait_ge(m["gn_in"], 32 * layer + 32)
                    norm_hi(n0, 0)

                    def turned_hi(dst, bk):
                        return nc.scalar.activation(dst, bk[:, :].rearrange("p (c n) -> p c n", c=DC), ACT.Copy)

                    def body(it, first, last):
                        for k in range(2):
                            n = n0 + 2 * it + k
                            begin, end = first and k == 0, last and k == 1
                            if begin:
                                for j in range(1, 8):
                                    weights_hi(j)
                            if not end:
                                norm_hi(n + 1, 1 - k)
                            if begin:
                                for j in range(8, 10):
                                    weights_hi(j)
                            act.wait_ge(m["v_ps"], n + 1)
                            nc.scalar.activation(vv[:, 0, :], bank[2][:, :], ACT.Copy).then_inc(m["v_hi"], 1)
                            act.wait_ge(m["g_ps"], n + 1)
                            if not begin:
                                act.wait_ge(m["sws_ok"], 2 * n)
                            nc.scalar.activation(sw[:, :], bank[3][:, :], ACT.Silu).then_inc(m["sw_ok"], 1)
                            for j in range(2):
                                act.wait_ge(m["qk_turned"], 2 * n + j + 1)
                                turned_hi(qkT[:, j, 0, :, :], bank[4 + j]).then_inc(m["qkT_hi"], 1)
                            if not begin:
                                act.wait_ge(m["y_turned"], n)
                                turned_hi(yT[:, 0, :, :], bank[6]).then_inc(m["yT_hi"], 1)
                            for j in range(2):
                                act.wait_ge(m["pf_ok"], 2 * n + j + 1)
                                nc.scalar.activation(p_hl[:, 0, j, :, :], pf[:, j, :, :], ACT.Copy).then_inc(m["p_hi"], 1)
                    pairs(act, body)
                    def weights2_hi(k, n):
                        act.wait_ge(m["down_ps"], n + 1)
                        act.wait_ge(f_in[k], 16 // FS * (n - k) + 16)
                        nc.scalar.activation(fw[k][:, 0, :], fraw[k][:, :], ACT.Copy).then_inc(m["f_hi"], 1)

                    def norm2_hi(t):
                        n = n0 + t
                        if t >= 2:
                            act.wait_ge(m["x2_lo"], n - 1)
                        scale_columns(xf[t % 2], 1, bank[X2_BANK[t]], m["x2_turned"], n + 1, m["xf2_ok"])
                        act.wait_ge(m["xf2_ok"], DC * (n + 1))
                        nc.scalar.activation(x2T[:, 0, :, t * P:(t + 1) * P], xf[t % 2][:, :, :], ACT.Copy).then_inc(m["x2_hi"], 1)
                    norm2_hi(0)
                    norm2_hi(1)
                    act.wait_ge(m["y_turned"], n0 + 8)
                    turned_hi(yT[:, 0, :, :], bank[6]).then_inc(m["yT_hi"], 1)
                    norm2_hi(2)
                    norm2_hi(3)
                    act.wait_ge(m["g_ps"], n0 + 8)
                    weights2_hi(0, 2 * FC * layer)
                    norm2_hi(4)
                    weights2_hi(1, 2 * FC * layer + 1)
                    for t in range(5, NT):
                        norm2_hi(t)

                    def hidden_hi(k, n):
                        act.wait_ge(m["up_ps"], n + 1)
                        nc.scalar.activation(hh[k % 2][:, 0, :], bank[k % 2][:, :], ACT.Gelu_apprx_tanh).then_inc(m["h_hi"], 1)
                        nc.scalar.activation(hf32[k % 2][:, :], bank[k % 2][:, :], ACT.Gelu_apprx_tanh).then_inc(m["h_ok"], 1)
                    with act.Fori(0, 2 * FC // FS - 1) as it:
                        for k in range(FS):
                            n = 2 * FC * layer + FS * it + k
                            hidden_hi(k, n)
                            weights2_hi((k + 2) % FS, n + 2)
                    for k in range(FS):
                        n = 2 * FC * layer + 2 * FC - FS + k
                        hidden_hi(k, n)
                        if k < 2:
                            weights2_hi(k + 2, n + 2)

            @block.vector
            def _(dve):
                dve.sem_inc(m["ffn_ok"], 1)
                dve.sem_inc(m["res_ok"], 1)
                for _ in range(FS):
                    dve.sem_inc(m["f_lo"], 1)
                for t in range(NT):
                    nc.vector.bn_stats(stats[:, t, :], X[:, t, :]).then_inc(m["ln0_st"], 1)
                for t in range(NT):
                    dve.wait_ge(m["ln0_st"], t + 1)
                    nc.vector.bn_aggr(mv[:, t, :], stats[:, t, :]).then_inc(m["ln0_ag"], 1)
                dve.wait_ge(m["ln0_ag"], NT)
                nc.vector.tensor_scalar(veps[:, :], mv[:, :, 1], 1e-5, None, ALU.add).then_inc(m["ln0_ve"], 1)
                dve.wait_ge(m["ln0_rs"], 1)
                for t in range(NT):
                    nc.vector.tensor_scalar(A[:, t, :], X[:, t, :], mv[:, t, 0:1], rstd[:, t:t + 1], ALU.subtract, ALU.mult).then_inc(m["a0_ok"], 1)
                dve.wait_ge(m["a0_ok"], NT)
                dve.wait_ge(m["tab_in"], 32)
                with dve.Fori(0, L) as layer:
                    n0 = 8 * layer

                    def weights_lo(j):
                        dve.wait_ge(m["w_hi"], 10 * layer + j + 1)
                        w, cols = matrices[j // 2], slice(j % 2 * 256, (j % 2 + 1) * 256)
                        nc.vector.tensor_tensor(w[:, 1, :, cols], wraw[j % WS][:, :, :], r(w[:, 0, :, cols]), ALU.subtract).then_inc(m["w_lo"], 1)

                    def norm_stats(n, t):
                        nc.vector.bn_stats(stats[:, 0, :], tile_of(A, t)).then_inc(m["st_ok"], 1)
                        wait_alone(dve, m["st_ok"], n + 1)
                        nc.vector.bn_aggr(mv[:, 0, :], stats[:, 0, :]).then_inc(m["ag_ok"], 1)
                        dve.wait_ge(m["ag_ok"], n + 1)
                        nc.vector.tensor_scalar(veps[:, 0:1], mv[:, 0, 1:2], 1e-6, None, ALU.add).then_inc(m["ve_ok"], 1)

                    def norm_apply(n, t):
                        dve.wait_ge(m["rs_ok"], n + 1)
                        nc.vector.tensor_scalar(xh[0][:, :], tile_of(A, t), mv[:, 0, 0:1], rstd[:, 0:1], ALU.subtract, ALU.mult).then_inc(m["xh_ok"], 1)

                    def norm_lo(n, k):
                        dve.wait_ge(m["xn_hi"], n + 1)
                        nc.vector.tensor_tensor(xn[k][:, 1, :, :], xf[0][:, :, :], r(xn[k][:, 0, :, :]), ALU.subtract).then_inc(m["xn_lo"], 1)

                    norm_stats(n0, 0)
                    norm_apply(n0, 0)
                    weights_lo(0)
                    norm_lo(n0, 0)

                    def rotate(n, j):
                        dve.wait_ge(m["q_ps" if j == 0 else "k_ps"], n + 1)
                        src = bank[j][:, :].rearrange("p (g e) -> p g e", e=E // 2)
                        for z, w in ((rc, 2 * j), (rs, 2 * j + 1)):
                            nc.vector.tensor_tensor(z[:, j, :].rearrange("p (g e) -> p g e", e=E // 2), src,
                                                    rot[:, w:w + 1, :].broadcast_to([P, 2 * H, E // 2]), ALU.mult).then_inc(m["rc_ok"], 1)

                    def group_norm(n):
                        dve.wait_ge(m["o_ps"], n)
                        for h in range(H):
                            nc.vector.bn_stats(gst[:, h, :], bank[7][:, h * E:(h + 1) * E]).then_inc(m["gst_ok"], 1)
                        wait_alone(dve, m["gst_ok"], H * n)
                        for h in range(H):
                            nc.vector.bn_aggr(gmv[:, h, :], gst[:, h, :]).then_inc(m["gmv_ok"], 1)
                        dve.wait_ge(m["gmv_ok"], H * n)
                        nc.vector.tensor_scalar(gve[:, :], gmv[:, :, 1], 1e-6, None, ALU.add).then_inc(m["gve_ok"], 1)
                        heads = lambda z: z.rearrange("p (h e) -> p h e", e=E)
                        nc.vector.tensor_tensor(heads(y[:, :]), heads(bank[7][:, :]), gmv[:, :, 0:1].broadcast_to([P, H, E]), ALU.subtract).then_inc(m["cen_ok"], 1)
                        dve.wait_ge(m["grs_ok"], n)
                        dve.wait_ge(m["cen_ok"], n)
                        nc.vector.tensor_tensor(heads(y[:, :]), heads(y[:, :]), grs[:, :].unsqueeze(2).broadcast_to([P, H, E]), ALU.mult).then_inc(m["hn_ok"], 1)
                        dve.wait_ge(m["sws_ok"], 2 * n)
                        dve.wait_ge(m["hn_ok"], n)
                        nc.vector.tensor_tensor(y[:, :], y[:, :], sws[:, 0, :], ALU.mult).then_inc(m["ya_ok"], 1)
                        dve.wait_ge(m["ya_ok"], n)
                        nc.vector.tensor_tensor(y[:, :], y[:, :], sws[:, 1, :], ALU.add).then_inc(m["y_ok"], 1)

                    def turned_lo(dst, bk, hi):
                        return nc.vector.tensor_tensor(dst, bk[:, :].rearrange("p (c n) -> p c n", c=DC), r(hi), ALU.subtract)

                    def residual(n, t):
                        dve.wait_ge(m["wo_ps"], n + 1)
                        nc.vector.tensor_tensor(tile_of(A, t), bank[0][:, :], tile_of(A, t), ALU.add).then_inc(m["res_ok"], 1)

                    def body(it, first, last):
                        for k in range(2):
                            t = 2 * it + k
                            n = n0 + t
                            begin, end = first and k == 0, last and k == 1
                            if begin:
                                for j in range(1, 4):
                                    weights_lo(j)
                            if not end:
                                norm_stats(n + 1, t + 1)
                            rotate(n, 0)
                            rotate(n, 1)
                            if not end:
                                norm_apply(n + 1, t + 1)
                            if begin:
                                for j in range(4, 8):
                                    weights_lo(j)
                                norm_lo(n + 1, 1 - k)
                                for j in range(8, 10):
                                    weights_lo(j)
                            if not begin:
                                group_norm(n)
                            dve.wait_ge(m["v_hi"], n + 1)
                            nc.vector.tensor_tensor(vv[:, 1, :], bank[2][:, :], r(vv[:, 0, :]), ALU.subtract).then_inc(m["v_lo"], 1)
                            if not (begin or end):
                                norm_lo(n + 1, 1 - k)
                            for j in range(2):
                                dve.wait_ge(m["qkT_hi"], 2 * n + j + 1)
                                turned_lo(qkT[:, j, 1, :, :], bank[4 + j], qkT[:, j, 0, :, :]).then_inc(m["qkT_lo"], 1)
                            if not first:
                                residual(n - 2, t - 2)
                            if not begin:
                                dve.wait_ge(m["yT_hi"], n)
                                turned_lo(yT[:, 1, :, :], bank[6], yT[:, 0, :, :]).then_inc(m["yT_lo"], 1)
                            dve.wait_ge(m["s_ps"], n + 1)
                            if not begin:
                                dve.wait_ge(m["p_lo"], 2 * n)
                            for j in range(2):
                                nc.vector.tensor_tensor(pf[:, j, :, :], bank[2 + j][:, :].rearrange("p (c n) -> p c n", c=DC),
                                                        decay[:, j, :, :], ALU.mult).then_inc(m["pf_ok"], 1)
                    pairs(dve, body)

                    def norm2_stats(tiles):
                        for t in tiles:
                            nc.vector.bn_stats(stats[:, t, :], A[:, t, :]).then_inc(m["st2_ok"], 1)
                        wait_alone(dve, m["st2_ok"], n0 + tiles.stop)
                        for t in tiles:
                            nc.vector.bn_aggr(mv[:, t, :], stats[:, t, :]).then_inc(m["ag2_ok"], 1)
                        dve.wait_ge(m["ag2_ok"], n0 + tiles.stop)
                        nc.vector.tensor_scalar(veps[:, tiles.start:tiles.stop], mv[:, tiles.start:tiles.stop, 1], 1e-6, None, ALU.add).then_inc(m["ve2_ok"], 1)

                    def norm2_apply(t):
                        dve.wait_ge(m["rs2_ok"], 2 * layer + 1 + (t >= EARLY))
                        if t >= 2:
                            dve.wait_ge(m["x2_turned"], n0 + t - 1)
                        else:
                            dve.wait_ge(m["x_turned"], n0 + 8)
                        nc.vector.tensor_scalar(xh[t % 2][:, :], A[:, t, :], mv[:, t, 0:1], rstd[:, t:t + 1], ALU.subtract, ALU.mult).then_inc(m["xh2_ok"], 1)

                    def norm2_lo(t):
                        dve.wait_ge(m["x2_hi"], n0 + t + 1)
                        cols = slice(t * P, (t + 1) * P)
                        nc.vector.tensor_tensor(x2T[:, 1, :, cols], xf[t % 2][:, :, :], r(x2T[:, 0, :, cols]), ALU.subtract).then_inc(m["x2_lo"], 1)

                    def weights2_lo(k, n):
                        dve.wait_ge(m["f_hi"], n + FS + 1)
                        nc.vector.tensor_tensor(fw[k][:, 1, :], fraw[k][:, :], r(fw[k][:, 0, :]), ALU.subtract).then_inc(m["f_lo"], 1)

                    dve.wait_ge(m["res_ok"], n0 + EARLY + 1)
                    norm2_stats(range(0, EARLY))
                    norm2_apply(0)
                    norm2_apply(1)
                    group_norm(n0 + 8)
                    residual(n0 + 6, 6)
                    norm2_lo(0)
                    norm2_apply(2)
                    norm2_lo(1)
                    norm2_apply(3)
                    dve.wait_ge(m["yT_hi"], n0 + 8)
                    turned_lo(yT[:, 1, :, :], bank[6], yT[:, 0, :, :]).then_inc(m["yT_lo"], 1)
                    norm2_lo(2)
                    norm2_apply(4)
                    norm2_lo(3)
                    norm2_apply(5)
                    residual(n0 + 7, 7)
                    dve.wait_ge(m["res_ok"], n0 + NT + 1)
                    norm2_stats(range(EARLY, NT))
                    weights2_lo(0, 2 * FC * layer)
                    norm2_lo(4)
                    weights2_lo(1, 2 * FC * layer + 1)
                    norm2_apply(6)
                    norm2_lo(5)
                    norm2_apply(7)
                    norm2_lo(6)
                    norm2_lo(7)

                    def chunks(n, ahead=True):
                        for k in range(FS):
                            dve.wait_ge(m["h_ok"], n + k + 1)
                            nc.vector.tensor_tensor(hh[k % 2][:, 1, :], hf32[k % 2][:, :], r(hh[k % 2][:, 0, :]), ALU.subtract).then_inc(m["h_lo"], 1)
                            if ahead or k < 2:
                                weights2_lo((k + 2) % FS, n + k + 2)

                    for half in range(2):
                        b = 2 * FC * layer + FC * half
                        with dve.Fori(0, FC // FS - half) as it:
                            chunks(b + FS * it)
                        if half == 1:
                            chunks(b + FC - FS, False)
                        dve.wait_ge(m["down_ps"], b + FC + FS)
                        for j in range(4):
                            nc.vector.tensor_tensor(A[:, 4 * half + j, :], bank[4 + j][:, :], A[:, 4 * half + j, :], ALU.add).then_inc(m["ffn_ok"], 1)
                    dve.wait_ge(m["ffn_ok"], n0 + 9)

            @block.tensor
            def _(pe):
                with pe.Fori(0, L) as layer:
                    n0 = 8 * layer

                    def turn(src, bk):
                        for c in range(DC):
                            last = nc.tensor.transpose(bk[:, c * P:(c + 1) * P], src[:, c * P:(c + 1) * P], ident[:, :])
                        return last

                    def project(which, bk, k):
                        return products(nc, bk[:, :], range(DC), lambda c, h: xn[k][:, h, c, :],
                                        lambda c, h: matrices[which][:, h, c, :])

                    def apply_scores(n):
                        pe.wait_ge(m["p_lo"], 2 * n)
                        pe.wait_ge(m["v_lo"], n)
                        for h in range(H):
                            last = products(nc, bank[7][:, h * E:(h + 1) * E], range(1), lambda _, i: p_hl[:, i, h % 2, h // 2, :],
                                            lambda _, i: vv[:, i, h * E:(h + 1) * E])
                        last.then_inc(m["o_ps"], 1)

                    def project_out(n):
                        pe.wait_ge(m["yT_lo"], n)
                        products(nc, bank[0][:, :], range(DC), lambda c, h: yT[:, h, c, :],
                                 lambda c, h: wo[:, h, c, :]).then_inc(m["wo_ps"], 1)

                    pe.wait_ge(m["xh_ok"], n0 + 1)
                    turn(xh[0], bank[6]).then_inc(m["x_turned"], 1)

                    def body(it, first, last):
                        for k in range(2):
                            n = n0 + 2 * it + k
                            begin, end = first and k == 0, last and k == 1
                            pe.wait_ge(m["xn_lo"], n + 1)
                            if begin:
                                pe.wait_ge(m["w_lo"], 10 * layer + 2)
                            elif first:
                                pe.wait_ge(m["rc_ok"], 4 * n - 2)
                            else:
                                pe.wait_ge(m["res_ok"], n - 1)
                            project(0, bank[0], k).then_inc(m["q_ps"], 1)
                            if begin:
                                pe.wait_ge(m["w_lo"], 10 * layer + 4)
                            else:
                                pe.wait_ge(m["rc_ok"], 4 * n)
                            project(1, bank[1], k).then_inc(m["k_ps"], 1)
                            if not begin:
                                apply_scores(n)
                            if not end:
                                if not first:
                                    pe.wait_ge(m["yT_lo"], n - 1)
                                elif k == 1:
                                    pe.wait_ge(m["xf_ok"], DC * (n + 1))
                                pe.wait_ge(m["xh_ok"], n + 2)
                                turn(xh[0], bank[6]).then_inc(m["x_turned"], 1)
                            if not begin:
                                pe.wait_ge(m["pf_ok"], 2 * n)
                            else:
                                pe.wait_ge(m["w_lo"], 10 * layer + 6)
                            project(2, bank[2], k).then_inc(m["v_ps"], 1)
                            if begin:
                                pe.wait_ge(m["w_lo"], 10 * layer + 8)
                            project(3, bank[3], k).then_inc(m["g_ps"], 1)
                            for j in range(2):
                                pe.wait_ge(m["qk_ok"], 4 * n + 2 * j + 2)
                                turn(qk[:, j, :], bank[4 + j]).then_inc(m["qk_turned"], 1)
                            if not first:
                                pe.wait_ge(m["rc_ok"], 4 * n + 2)
                                project_out(n - 1)
                            if not begin:
                                pe.wait_ge(m["y_ok"], n)
                                if not end:
                                    pe.wait_ge(m["xf_ok"], DC * (n + 2))
                                turn(y, bank[6]).then_inc(m["y_turned"], 1)
                            if first and k == 1:
                                pe.wait_ge(m["w_lo"], 10 * layer + 10)
                            pe.wait_ge(m["qkT_lo"], 2 * n + 2)
                            pe.wait_ge(m["v_lo"], n + 1)
                            pe.wait_ge(m["sw_ok"], n + 1)
                            for h in range(H):
                                rows = slice((h % 2) * E, (h % 2 + 1) * E)
                                c = h // 2
                                last_mm = products(nc, bank[2 + h % 2][:, c * P:(c + 1) * P], range(1), lambda _, i: qkT[rows, 1, i, c, :],
                                                   lambda _, i: qkT[rows, 0, i, c, :])
                            last_mm.then_inc(m["s_ps"], 1)
                    pairs(pe, body)

                    def turn2(t):
                        pe.wait_ge(m["xh2_ok"], n0 + t + 1)
                        if t >= 5:
                            pe.wait_ge(m["xf2_ok"], DC * (n0 + t - 4))
                        turn(xh[t % 2], bank[X2_BANK[t]]).then_inc(m["x2_turned"], 1)
                    apply_scores(n0 + 8)
                    project_out(n0 + 7)
                    pe.wait_ge(m["pf_ok"], 2 * n0 + 16)
                    turn2(0)
                    turn2(1)
                    pe.wait_ge(m["y_ok"], n0 + 8)
                    turn(y, bank[6]).then_inc(m["y_turned"], 1)
                    turn2(2)
                    turn2(3)
                    pe.wait_ge(m["res_ok"], n0 + 8)
                    project_out(n0 + 8)
                    turn2(4)
                    turn2(5)

                    def up(n, k, half):
                        pe.wait_ge(m["f_lo"], n + FS + 1)
                        products(nc, bank[k % 2][:, :], range(DC), lambda c, h: fw[k][:, h, c * P:(c + 1) * P],
                                 lambda c, h: x2T[:, h, c, half * 512:(half + 1) * 512]).then_inc(m["up_ps"], 1)

                    def down(n, k, start, stop):
                        pe.wait_ge(m["h_lo"], n + 1)
                        for j in range(4):
                            for i, (x, w) in enumerate(PARTS):
                                last = nc.tensor.matmul(bank[4 + j][:, :], hh[k % 2][:, x, j * P:(j + 1) * P], fw[k][:, w, D:2 * D],
                                                        start=start and i == 0, stop=stop and i == 2)
                        last.then_inc(m["down_ps"], 1)

                    def chunks(n, half, begin=False, end=False):
                        for k in range(FS):
                            if not (end and k == FS - 1):
                                up(n + k + 1, (k + 1) % FS, half)
                            elif half == 0:
                                pe.wait_ge(m["x2_lo"], n0 + NT)
                                up(n + k + 1, 0, 1)
                            if begin and half == 1 and k == 0:
                                pe.wait_ge(m["ffn_ok"], n0 + 4 + 1)
                            down(n + k, k, begin and k == 0, end and k == FS - 1)

                    wait_alone(pe, m["x2_lo"], n0 + 4)
                    pe.wait_ge(m["res_ok"], n0 + 9)
                    up(2 * FC * layer, 0, 0)
                    turn2(6)
                    turn2(7)
                    pe.wait_ge(m["x2_lo"], n0 + 6)
                    for half in range(2):
                        b = 2 * FC * layer + FC * half
                        chunks(b, half, begin=True)
                        with pe.Fori(1, FC // FS - 1) as it:
                            chunks(b + FS * it, half)
                        chunks(b + FC - FS, half, end=True)


def mixture(nc, a, out, whole, holder, sem, bank, X, A, ident, mhalf, xg, yg):
    with ExitStack() as phase:
        sb = holder(phase)
        slot = sb("slot", [P, 2, NT], I32)
        gate = sb("gate", [P, 2, NT])
        group_expert = sb("group_expert", [1, NG], I32)

        with ExitStack() as inner:
            sbi = holder(inner)
            tab = sbi("tab", [P, 2 * P + NE + NE * NE + NG])
            upper, ones = tab[:, 0:P], tab[:, P:2 * P]
            iota_e = tab[:, 2 * P:2 * P + NE]
            before = tab[:, 2 * P + NE:2 * P + NE + NE * NE].rearrange("p (e f) -> p e f", f=NE)
            iota_g = tab[:, 2 * P + NE + NE * NE:]
            rw = sbi("rw", [P, DC, NE])
            rw_hl = sbi("rw_hl", [P, 2, DC, NE], F32R)
            stats = sbi("m_stats", [P, NT, 6])
            mv = sbi("m_mv", [P, NT, 2])
            veps = sbi("m_veps", [P, NT])
            rstd = sbi("m_rstd", [P, NT])
            xr = [sbi(f"xr{i}", [P, 2, DC, P], F32R) for i in range(2)]
            logits = sbi("logits", [P, NT, NE])
            top = sbi("top", [P, NT, NE])
            topi = sbi("topi", [P, NT, NE], U32)
            chosen = sbi("chosen", [P, 2, NT])
            diff = sbi("diff", [P, NT])
            odds = sbi("odds", [P, NT])
            sum1 = sbi("sum1", [P, NT])
            hot = sbi("hot", [P, 2, NT, NE])
            both = sbi("both", [P, NT, NE])
            cnt = sbi("cnt", [P, 2, NT, NE])
            cum = sbi("cum", [P, NT + 1, NE])
            groups = sbi("groups", [P, 5, NE])
            tri = sbi("tri", [P, NE, NE])
            gs = sbi("gs", [P, 3, NE])
            where = sbi("where", [P, 2, NT, NE])
            picked = sbi("picked", [P, 2, NT, NE])
            slotf = sbi("slotf", [P, 2, NT])
            ge = sbi("ge", [P, NG, NE])
            gsum = sbi("gsum", [P, NG])
            gmin = sbi("gmin", [P, NG])
            names = """tab_in x2_ok st_ok ag_ok ve_ok rs_ok xh_ok turned hi lo rw_hi rw_lo logit_ps logit_ok top_ok topi_ok
                route odds_ok both_ok cnt_ps cum_ok slot_ok scattered""".split()
            m = {n: sem("m_" + n) for n in names}
            with nc.Block() as block:
                @block.sync
                def _(sp):
                    sp.dma_start(tab[:, :], a["route_tab"]).then_inc(m["tab_in"], 16)
                    sp.dma_start(rw[:, :, :], a["rw"]).then_inc(m["tab_in"], 16)

                @block.gpsimd
                def _(pool):
                    pool.wait_ge(m["ve_ok"], 1)
                    nc.gpsimd.tensor_tensor(rstd[:, :], veps[:, :], mhalf[:, 0:NT], ALU.pow).then_inc(m["rs_ok"], 1)
                    pool.wait_ge(m["slot_ok"], 1)
                    for t in range(NT):
                        for k in range(2):
                            nc.gpsimd.indirect_dma_start(out=xg[:, :], out_offset=bass.IndirectOffsetOnAxis(ap=slot[:, k, t:t + 1], axis=0),
                                                         in_=A[:, t, :], in_offset=None).then_inc(m["scattered"], 16)
                    pool.wait_ge(m["scattered"], 16 * 2 * NT)

                @block.scalar
                def _(act):
                    act.wait_ge(m["tab_in"], 32)
                    nc.scalar.activation(rw_hl[:, 0, :, :], rw[:, :, :], ACT.Copy).then_inc(m["rw_hi"], 1)
                    for t in range(NT):
                        act.wait_ge(m["turned"], t + 1)
                        if t >= 2:
                            act.wait_ge(m["logit_ps"], t - 1)
                        nc.scalar.activation(xr[t % 2][:, 0, :, :], bank[t % 2][:, :].rearrange("p (c n) -> p c n", c=DC), ACT.Copy).then_inc(m["hi"], 1)
                    act.wait_ge(m["route"], 2)
                    nc.scalar.activation(odds[:, :], diff[:, :], ACT.Exp).then_inc(m["odds_ok"], 1)

                @block.vector
                def _(dve):
                    for t in range(NT):
                        nc.vector.tensor_tensor(X[:, t, :], X[:, t, :], A[:, t, :], ALU.add).then_inc(m["x2_ok"], 1)
                    for t in range(NT):
                        dve.wait_ge(m["x2_ok"], t + 1)
                        nc.vector.bn_stats(stats[:, t, :], X[:, t, :]).then_inc(m["st_ok"], 1)
                    for t in range(NT):
                        dve.wait_ge(m["st_ok"], t + 1)
                        nc.vector.bn_aggr(mv[:, t, :], stats[:, t, :]).then_inc(m["ag_ok"], 1)
                    dve.wait_ge(m["ag_ok"], NT)
                    nc.vector.tensor_scalar(veps[:, :], mv[:, :, 1], 1e-5, None, ALU.add).then_inc(m["ve_ok"], 1)
                    dve.wait_ge(m["rw_hi"], 1)
                    nc.vector.tensor_tensor(rw_hl[:, 1, :, :], rw[:, :, :], r(rw_hl[:, 0, :, :]), ALU.subtract).then_inc(m["rw_lo"], 1)
                    dve.wait_ge(m["rs_ok"], 1)

                    def lo(t):
                        dve.wait_ge(m["hi"], t + 1)
                        nc.vector.tensor_tensor(xr[t % 2][:, 1, :, :], bank[t % 2][:, :].rearrange("p (c n) -> p c n", c=DC),
                                                r(xr[t % 2][:, 0, :, :]), ALU.subtract).then_inc(m["lo"], 1)
                    for t in range(NT):
                        nc.vector.tensor_scalar(A[:, t, :], X[:, t, :], mv[:, t, 0:1], rstd[:, t:t + 1], ALU.subtract, ALU.mult).then_inc(m["xh_ok"], 1)
                        if t >= 1:
                            lo(t - 1)
                    lo(NT - 1)
                    dve.wait_ge(m["logit_ps"], NT)
                    nc.vector.tensor_copy(logits[:, :, :], bank[2][:, 0:NT * NE].rearrange("p (t e) -> p t e", e=NE)).then_inc(m["logit_ok"], 1)
                    dve.wait_ge(m["logit_ok"], 1)
                    for t in range(NT):
                        nc.vector.max(top[:, t, :], logits[:, t, :]).then_inc(m["top_ok"], 1)
                    for t in range(NT):
                        dve.wait_ge(m["top_ok"], t + 1)
                        nc.vector.max_index(topi[:, t, :], top[:, t, :], logits[:, t, :]).then_inc(m["topi_ok"], 1)
                    step = [0]

                    def link(ins):
                        step[0] += 1
                        ins.then_inc(m["route"], 1)
                        dve.wait_ge(m["route"], step[0])
                    dve.wait_ge(m["topi_ok"], NT)
                    link(nc.vector.tensor_copy(chosen[:, :, :].rearrange("p k t -> p t k"), topi[:, :, 0:2]))
                    link(nc.vector.tensor_tensor(diff[:, :], top[:, :, 1], top[:, :, 0], ALU.subtract))
                    for k in range(2):
                        link(nc.vector.tensor_tensor(hot[:, k, :, :], chosen[:, k, :].unsqueeze(2).broadcast_to([P, NT, NE]),
                                                     iota_e.unsqueeze(1).broadcast_to([P, NT, NE]), ALU.is_equal))
                    nc.vector.tensor_tensor(both[:, :, :], hot[:, 0, :, :], hot[:, 1, :, :], ALU.add).then_inc(m["both_ok"], 1)
                    dve.wait_ge(m["odds_ok"], 1)
                    link(nc.vector.tensor_scalar(sum1[:, :], odds[:, :], 1.0, None, ALU.add))
                    link(nc.vector.reciprocal(gate[:, 0, :], sum1[:, :]))
                    link(nc.vector.tensor_tensor(gate[:, 1, :], gate[:, 0, :], odds[:, :], ALU.mult))
                    dve.wait_ge(m["cnt_ps"], 1)
                    link(nc.vector.tensor_copy(cnt[:, :, :, :].rearrange("p a t e -> p (a t e)"), bank[3][:, 0:2 * NT * NE]))
                    link(nc.vector.memset(cum[:, 0, :], 0.0))
                    for t in range(NT):
                        link(nc.vector.tensor_tensor(cum[:, t + 1, :], cum[:, t, :], cnt[:, 1, t, :], ALU.add))
                    link(nc.vector.tensor_scalar(groups[:, 0, :], cum[:, NT, :], 0.0, None, ALU.is_gt))
                    for j in range(1, TOK // GT):
                        link(nc.vector.scalar_tensor_tensor(groups[:, j, :], cum[:, NT, :], float(j * GT), groups[:, j - 1, :], ALU.is_gt, ALU.add))
                    per_expert = groups[:, TOK // GT - 1, :]
                    link(nc.vector.tensor_tensor(tri[:, :, :], before, per_expert.unsqueeze(1).broadcast_to([P, NE, NE]), ALU.mult))
                    link(nc.vector.tensor_reduce(gs[:, 0, :], tri[:, :, :], AX.X, ALU.add))
                    link(nc.vector.tensor_tensor(gs[:, 1, :], gs[:, 0, :], per_expert, ALU.add))
                    link(nc.vector.tensor_scalar(gs[:, 2, :], gs[:, 0, :], float(GT), None, ALU.mult))
                    link(nc.vector.tensor_tensor(where[:, 0, :, :], cnt[:, 0, :, :], cum[:, 0:NT, :], ALU.add))
                    link(nc.vector.tensor_tensor(where[:, 1, :, :], where[:, 0, :, :], gs[:, 2, :].unsqueeze(1).broadcast_to([P, NT, NE]), ALU.add))
                    for k in range(2):
                        link(nc.vector.tensor_tensor(picked[:, k, :, :], hot[:, k, :, :], where[:, 1, :, :], ALU.mult))
                    link(nc.vector.tensor_reduce(slotf[:, :, :], picked[:, :, :, :], AX.X, ALU.add))
                    nc.vector.tensor_copy(slot[:, :, :], slotf[:, :, :]).then_inc(m["slot_ok"], 1)
                    link(nc.vector.tensor_tensor(ge[:, :, :], gs[:, 1, :].unsqueeze(1).broadcast_to([P, NG, NE]),
                                                 iota_g.unsqueeze(2).broadcast_to([P, NG, NE]), ALU.is_le))
                    link(nc.vector.tensor_reduce(gsum[:, :], ge[:, :, :], AX.X, ALU.add))
                    link(nc.vector.tensor_scalar(gmin[:, :], gsum[:, :], float(NE - 1), None, ALU.min))
                    link(nc.vector.tensor_copy(group_expert[:, :], gmin[0:1, :]))

                @block.tensor
                def _(pe):
                    def score(t):
                        pe.wait_ge(m["lo"], t + 1)
                        products(nc, bank[2][:, t * NE:(t + 1) * NE], range(DC), lambda c, h: xr[t % 2][:, h, c, :],
                                 lambda c, h: rw_hl[:, h, c, :]).then_inc(m["logit_ps"], 1)
                    pe.wait_ge(m["rw_lo"], 1)
                    for t in range(NT):
                        pe.wait_ge(m["xh_ok"], t + 1)
                        if t >= 2:
                            pe.wait_ge(m["lo"], t - 1)
                        for c in range(DC):
                            last = nc.tensor.transpose(bank[t % 2][:, c * P:(c + 1) * P], A[:, t, c * P:(c + 1) * P], ident[:, :])
                        last.then_inc(m["turned"], 1)
                        if t >= 1:
                            score(t - 1)
                    score(NT - 1)
                    pe.wait_ge(m["both_ok"], 1)
                    pe.wait_ge(m["tab_in"], 32)
                    flat = both[:, :, :].rearrange("p t e -> p (t e)")
                    nc.tensor.matmul(bank[3][:, 0:NT * NE], upper, flat, start=True, stop=True)
                    nc.tensor.matmul(bank[3][:, NT * NE:2 * NT * NE], ones, flat, start=True, stop=True).then_inc(m["cnt_ps"], 1)

        with ExitStack() as inner:
            sbi = holder(inner)
            xin = sbi("xin", [P, 2, D])
            xT = sbi("e_xT", [P, 2, 2, DC, P], F32R)
            raw = [sbi(f"e_raw{i}", [P, DC, 512]) for i in range(3)]
            w = [sbi(f"e_w{i}", [P, 2, DC, 512], F32R) for i in range(3)]
            si = sbi("si", [P, 2, 512])
            hid = sbi("hid", [P, 2, 512])
            hT = [sbi(f"e_hT{i}", [P, 2, 2, DC, P], F32R) for i in range(2)]
            yb = sbi("yb", [P, 2, D])
            names = """x_in x_turned x_hi x_lo w_hi w_lo step_ps si_ok hid_ok h_turned h_hi h_lo y_ok y_out""".split()
            m = {n: sem("e_" + n) for n in names}
            w_in = [sem(f"e_w_in{i}") for i in range(3)]
            G0, D1, U0, G1, U1, D0 = range(6)
            PIECE_AT = {G0: 0, U0: 1, G1: 2, U1: 3, D0: 4, D1: 5}

            def count(g, pos):
                if isinstance(g, int) and g == 0 and pos == G0:
                    return 1
                if isinstance(g, int) and g == NG:
                    return PIECES * NG
                return PIECES * g + pos

            def slot_before(g, pos):
                if isinstance(g, int) and g == 0:
                    return {G0: None, U0: None, G1: 1, U1: None, D0: 2}[pos]
                if isinstance(g, int) and g == NG:
                    return count(NG - 1, U1)
                return count(g, pos) - 3

            with nc.Block() as block:
                @block.sync
                def _(sp):
                    x_v = xg.rearrange("(g t p) d -> g p t d", p=P, t=2)

                    def load(g, pos, expert):
                        n = slot_before(g, pos)
                        if n is not None:
                            sp.wait_ge(m["w_hi"], n)
                            sp.wait_ge(m["w_lo"], n)
                        sp.dma_start(raw[pos % 3][:, :, :], a["we"][bass.ds(expert, 1), PIECE_AT[pos], :, :]
                                     .rearrange("o p (c n) -> p (o c) n", c=DC)).then_inc(w_in[pos % 3], 16)

                    def load_x(g):
                        sp.dma_start(xin[:, :, :], x_v[bass.ds(g, 1), :, :, :].rearrange("o p t d -> p (o t) d")).then_inc(m["x_in"], 16)

                    def body(g, first):
                        expert = sp.value_load(group_expert[0:1, bass.ds(g, 1)], min_val=0, max_val=NE - 1)
                        load(g, G0, expert)
                        if not first:
                            before = sp.value_load(group_expert[0:1, bass.ds(g - 1, 1)], min_val=0, max_val=NE - 1)
                            load(g, D1, before)
                        for pos in (U0, G1, U1, D0):
                            load(g, pos, expert)
                        return expert
                    load_x(0)
                    body(0, True)
                    with sp.Fori(1, NG) as g:
                        sp.wait_ge(m["x_turned"], g)
                        load_x(g)
                        body(g, False)
                    last = sp.value_load(group_expert[0:1, NG - 1:NG], min_val=0, max_val=NE - 1)
                    load(NG, D1, last)

                @block.scalar
                def _(act):
                    y_v = yg.rearrange("(g t p) d -> g p t d", p=P, t=2)

                    def split_hi(g, pos):
                        n = slot_before(g, pos)
                        if isinstance(g, int) and g == NG:
                            loads = 2 * NG
                        else:
                            loads = {G0: 2 * g + 1, G1: 2 * g + 2, U0: 2 * g + 1, D0: 2 * g + 2, D1: 2 * g, U1: 2 * g + 1}[pos]
                        act.wait_ge(w_in[pos % 3], 16 * loads)
                        if n is not None:
                            act.wait_ge(m["step_ps"], n)
                        nc.scalar.activation(w[pos % 3][:, 0, :, :], raw[pos % 3][:, :, :], ACT.Copy).then_inc(m["w_hi"], 1)

                    def silu(g, j):
                        act.wait_ge(m["step_ps"], count(g, G0 if j == 0 else G1))
                        if not (isinstance(g, int) and g == 0 and j == 0):
                            act.wait_ge(m["hid_ok"], 4 * g + 2 * j)
                        for t in range(2):
                            nc.scalar.activation(si[:, t, :], bank[t][:, :], ACT.Silu).then_inc(m["si_ok"], 1)

                    def hidden_hi(g, j):
                        for t in range(2):
                            act.wait_ge(m["h_turned"], 4 * g + 2 * j + t + 1)
                            nc.scalar.activation(hT[j][:, 0, t, :, :], bank[6 + t][:, :].rearrange("p (c n) -> p c n", c=DC), ACT.Copy).then_inc(m["h_hi"], 1)

                    def x_hi(g):
                        for t in range(2):
                            act.wait_ge(m["x_turned"], g + 1)
                            nc.scalar.activation(xT[:, 0, t, :, :], bank[6 + t][:, :].rearrange("p (c n) -> p c n", c=DC), ACT.Copy).then_inc(m["x_hi"], 1)

                    def store(g, n, first):
                        act.wait_ge(m["step_ps"], n)
                        if not first:
                            act.wait_ge(m["y_out"], 16 * g)
                        for t in range(2):
                            nc.scalar.activation(yb[:, t, :], bank[4 + t][:, :], ACT.Copy).then_inc(m["y_ok"], 1)
                        act.wait_ge(m["y_ok"], 2 * g + 2)
                        act.dma_start(y_v[bass.ds(g, 1), :, :, :].rearrange("o p t d -> p (o t) d"), yb[:, :, :]).then_inc(m["y_out"], 16)

                    def body(g, first, second=False):
                        if not first:
                            hidden_hi(g - 1, 1)
                        split_hi(g, U0)
                        silu(g, 0)
                        split_hi(g, G1)
                        if not first:
                            store(g - 1, count(g, D1), second)
                        split_hi(g, U1)
                        split_hi(g, D0)
                        hidden_hi(g, 0)
                        silu(g, 1)
                    def tail(g):
                        split_hi(g + 1, G0)
                        x_hi(g + 1)
                        split_hi(g + 1, D1)
                    x_hi(0)
                    split_hi(0, G0)
                    body(0, True)
                    tail(0)
                    body(1, False, True)
                    tail(1)
                    with act.Fori(2, NG - 1) as g:
                        body(g, False)
                        tail(g)
                    body(NG - 1, False)
                    split_hi(NG, D1)
                    hidden_hi(NG - 1, 1)
                    store(NG - 1, PIECES * NG, False)
                    act.wait_ge(m["y_out"], 16 * NG)

                @block.vector
                def _(dve):
                    def split_lo(g, pos):
                        dve.wait_ge(m["w_hi"], count(g, pos))
                        nc.vector.tensor_tensor(w[pos % 3][:, 1, :, :], raw[pos % 3][:, :, :], r(w[pos % 3][:, 0, :, :]), ALU.subtract).then_inc(m["w_lo"], 1)

                    def hidden(g, j):
                        dve.wait_ge(m["step_ps"], count(g, U0 if j == 0 else U1))
                        for t in range(2):
                            dve.wait_ge(m["si_ok"], 4 * g + 2 * j + t + 1)
                            nc.vector.tensor_tensor(hid[:, t, :], bank[2 + t][:, :], si[:, t, :], ALU.mult).then_inc(m["hid_ok"], 1)

                    def hidden_lo(g, j):
                        for t in range(2):
                            dve.wait_ge(m["h_hi"], 4 * g + 2 * j + t + 1)
                            nc.vector.tensor_tensor(hT[j][:, 1, t, :, :], bank[6 + t][:, :].rearrange("p (c n) -> p c n", c=DC),
                                                    r(hT[j][:, 0, t, :, :]), ALU.subtract).then_inc(m["h_lo"], 1)

                    def x_lo(g):
                        for t in range(2):
                            dve.wait_ge(m["x_hi"], 2 * g + t + 1)
                            nc.vector.tensor_tensor(xT[:, 1, t, :, :], bank[6 + t][:, :].rearrange("p (c n) -> p c n", c=DC),
                                                    r(xT[:, 0, t, :, :]), ALU.subtract).then_inc(m["x_lo"], 1)

                    def body(g, first):
                        if not first:
                            hidden_lo(g - 1, 1)
                        split_lo(g, U0)
                        split_lo(g, G1)
                        split_lo(g, U1)
                        hidden(g, 0)
                        split_lo(g, D0)
                        hidden_lo(g, 0)

                    def tail(g):
                        split_lo(g + 1, G0)
                        x_lo(g + 1)
                        hidden(g, 1)
                        split_lo(g + 1, D1)
                    x_lo(0)
                    split_lo(0, G0)
                    body(0, True)
                    tail(0)
                    with dve.Fori(1, NG - 1) as g:
                        body(g, False)
                        tail(g)
                    body(NG - 1, False)
                    hidden(NG - 1, 1)
                    split_lo(NG, D1)
                    hidden_lo(NG - 1, 1)

                @block.tensor
                def _(pe):
                    def wide(g, pos, banks):
                        pe.wait_ge(m["w_lo"], count(g, pos))
                        for t in range(2):
                            last = products(nc, bank[banks + t][:, :], range(DC), lambda c, h: xT[:, h, t, c, :], lambda c, h: w[pos % 3][:, h, c, :])
                        last.then_inc(m["step_ps"], 1)

                    def down(n, pos, j):
                        pe.wait_ge(m["w_lo"], n)
                        for t in range(2):
                            for c in range(DC):
                                for i, (x, y) in enumerate(PARTS):
                                    last = nc.tensor.matmul(bank[4 + t][:, :], hT[j][:, x, t, c, :], w[pos % 3][:, y, c, :],
                                                            start=j == 0 and c == 0 and i == 0, stop=j == 1 and c == DC - 1 and i == 2,
                                                            skip_group_check=False)
                        last.then_inc(m["step_ps"], 1)

                    def turn_hidden(g, j):
                        for t in range(2):
                            pe.wait_ge(m["hid_ok"], 4 * g + 2 * j + t + 1)
                            for c in range(DC):
                                last = nc.tensor.transpose(bank[6 + t][:, c * P:(c + 1) * P], hid[:, t, c * P:(c + 1) * P], ident[:, :])
                            last.then_inc(m["h_turned"], 1)

                    def turn_x(g):
                        pe.wait_ge(m["x_in"], 16 * g + 16)
                        for t in range(2):
                            for c in range(DC):
                                last = nc.tensor.transpose(bank[6 + t][:, c * P:(c + 1) * P], xin[:, t, c * P:(c + 1) * P], ident[:, :])
                        last.then_inc(m["x_turned"], 1)

                    def body(g, first, last=False):
                        pe.wait_ge(m["x_lo"], 2 * g + 2)
                        wide(g, G0, 0)
                        if not first:
                            pe.wait_ge(m["h_lo"], 4 * g)
                            down(count(g, D1), D1, 1)
                        wide(g, U0, 2)
                        pe.wait_ge(m["si_ok"], 4 * g + 2)
                        wide(g, G1, 0)
                        turn_hidden(g, 0)
                        wide(g, U1, 2)
                        pe.wait_ge(m["h_lo"], 4 * g + 2)
                        if not last:
                            turn_x(g + 1)
                        if not first:
                            pe.wait_ge(m["y_ok"], 2 * g)
                        down(count(g, D0), D0, 0)
                        if not last:
                            pe.wait_ge(m["x_lo"], 2 * g + 4)
                        pe.wait_ge(m["si_ok"], 4 * g + 4)
                        turn_hidden(g, 1)
                    turn_x(0)
                    body(0, True)
                    with pe.Fori(1, NG - 1) as g:
                        body(g, False)
                    body(NG - 1, False, True)
                    pe.wait_ge(m["h_lo"], 4 * NG)
                    down(PIECES * NG, D1, 1)

        with ExitStack() as inner:
            sbi = holder(inner)
            rows = sbi("rows", [P, NT, 2, D])
            got = [sem(f"c_got{t}") for t in range(NT)]
            part, summed, stored = sem("c_part"), sem("c_summed"), sem("c_stored")
            with nc.Block() as block:
                @block.gpsimd
                def _(pool):
                    for t in range(NT):
                        for k in range(2):
                            nc.gpsimd.indirect_dma_start(out=rows[:, t, k, :], out_offset=None, in_=yg[:, :],
                                                         in_offset=bass.IndirectOffsetOnAxis(ap=slot[:, k, t:t + 1], axis=0)).then_inc(got[t], 16)

                @block.vector
                def _(dve):
                    for t in range(NT):
                        dve.wait_ge(got[t], 32)
                        nc.vector.scalar_tensor_tensor(X[:, t, :], rows[:, t, 0, :], gate[:, 0, t:t + 1], X[:, t, :], ALU.mult, ALU.add).then_inc(part, 1)
                        dve.wait_ge(part, t + 1)
                        nc.vector.scalar_tensor_tensor(X[:, t, :], rows[:, t, 1, :], gate[:, 1, t:t + 1], X[:, t, :], ALU.mult, ALU.add).then_inc(summed, 1)

                @block.sync
                def _(sp):
                    out_v = out.rearrange("(t p) d -> t p d", p=P)
                    for t in range(NT):
                        sp.wait_ge(summed, t + 1)
                        sp.dma_start(out_v[t, :, :], X[:, t, :]).then_inc(stored, 16)
                    sp.wait_ge(stored, 16 * NT)


def chunked(w):
    return np.ascontiguousarray(np.asarray(w).reshape(-1, P, w.shape[-1]).transpose(1, 0, 2))


def by_partition(v):
    return np.asarray(v).reshape(-1, P).T


def position_tables():
    f = np.float32
    base = (np.arange(0, E, 2, dtype=f) + f(0.4 * E)) / f(1.4 * E)
    pos = np.arange(S, dtype=f)
    scale = base[None, :] ** (pos[:, None] / f(256))
    angle = pos[:, None] * (f(1.0) / f(10000.0) ** (np.arange(E // 2, dtype=f) / f(E // 2)))[None, :]
    sin, cos = np.sin(angle), np.cos(angle)
    rot = np.stack([cos * scale, sin * scale, cos * (f(1) / scale), sin * (f(1) / scale)], axis=1)
    gammas = f(1.0) - f(2.0) ** (f(-5.0) - np.arange(H, dtype=f))
    tok = np.arange(P)
    diff = (tok[None, :] % S - tok[:, None] % S).astype(f)
    same = (tok[None, :] // S == tok[:, None] // S) & (diff >= 0)
    d = np.where(same[None], gammas[:, None, None] ** np.maximum(diff, 0)[None], f(0))
    decay = d.reshape(DC, 2, P, P).transpose(2, 1, 0, 3)
    return np.tile(rot, (BPT, 1, 1)).astype(f), decay.astype(f)


def arrays_of(inputs):
    g = {k: np.asarray(v) for k, v in inputs.items()}
    out = {"x": g["x"].reshape(TOK, D)}
    ctx = g["ctx_1024"]
    cT = ctx.transpose(0, 2, 1).reshape(NB, DC, P, SK).transpose(0, 2, 1, 3)
    out["ctx"] = cT.reshape(NB, P, DC * SK)
    last = np.zeros((P, DC, P), np.float32)
    last[:, :, :NB] = ctx[:, SK - 1, :].T.reshape(DC, P, NB).transpose(1, 0, 2)
    out["ctx_last"] = last
    for n, k in (("xwq", "Wq"), ("xwk", "Wk"), ("xwv", "Wv"), ("xwo", "Wo")):
        out[n] = chunked(g["L0_xattn_" + k].T)
    thr = g["L0_xattn_raw_thresholds"].reshape(XH)
    vecs = [by_partition(g["L0_xattn_" + k]) for k in ("bq", "bk", "bv")]
    vecs.append(np.repeat(thr.reshape(DC, HPC), XD, axis=1).T)
    vecs.append(np.repeat(np.eye(HPC, dtype=np.float32), XD, axis=0))
    out["vec"] = np.concatenate(vecs, axis=1)
    out["bo_bc"] = np.broadcast_to(g["L0_xattn_bo"], (P, D))
    out["ident"] = np.eye(P, dtype=np.float32)
    out["eye32"] = np.broadcast_to(np.eye(NB, 32, dtype=np.float32), (P, NB, 32))
    split = lambda w: w.transpose(0, 2, 1, 3).reshape(L, D, H, E // 2, 2).transpose(0, 1, 2, 4, 3).reshape(L, D, D)
    wq, wk = split(g["L0_attn_Wq"]), split(g["L0_attn_Wk"])
    wv = g["L0_attn_Wv"].transpose(0, 2, 1, 3).reshape(L, D, D)
    wa = np.concatenate([wq, wk, wv, g["L0_attn_Wg"], g["L0_attn_Wo"]], axis=2)
    out["wa"] = wa.reshape(L, DC, P, 10, 256).transpose(0, 3, 2, 1, 4).reshape(L, 10, P, DC * 256)
    w1 = g["L0_attn_ffn_w1"].reshape(L, DC, P, FC, P).transpose(0, 3, 2, 1, 4).reshape(L, FC, P, D)
    w2 = g["L0_attn_ffn_w2"].reshape(L, FC, P, D)
    out["wf"] = np.concatenate([w1, w2], axis=3)
    out["gn"] = np.broadcast_to(np.stack([g["L0_attn_gn_scale"], g["L0_attn_gn_bias"]], 1)[:, None], (L, P, 2, D))
    out["rot"], out["decay"] = position_tables()
    up, gt, down = g["L0_ffn_w_up"], g["L0_ffn_w_gate"], g["L0_ffn_w_down"]
    pieces = []
    for j in range(2):
        for w in (gt, up):
            pieces.append(w[:, 512 * j:512 * (j + 1), :].transpose(0, 2, 1).reshape(NE, DC, P, 512).transpose(0, 2, 1, 3))
    for j in range(2):
        pieces.append(down[:, :, 512 * j:512 * (j + 1)].transpose(0, 2, 1).reshape(NE, DC, P, D).transpose(0, 2, 1, 3))
    out["we"] = np.stack(pieces, axis=1).reshape(NE, PIECES, P, DC * 512)
    lnv = np.stack([g["L0_attn_" + k].reshape(L, DC, P) for k in ("ln1_scale", "ln1_bias", "ln2_scale", "ln2_bias")], axis=1)
    out["lnv"] = lnv.transpose(0, 3, 1, 2).reshape(L, P, 4 * DC)
    out["rw"] = chunked(g["L0_ffn_router_w"].T)
    col = lambda v: np.broadcast_to(v.astype(np.float32).reshape(-1), (P, v.size))
    i, e = np.arange(P), np.arange(NE)
    out["route_tab"] = np.concatenate([(i[:, None] < i[None, :]).astype(np.float32), np.ones((P, P), np.float32), col(e),
                                       col(e[None, :] < e[:, None]), col(np.arange(NG))], axis=1)
    return {k: np.ascontiguousarray(v) for k, v in out.items()}


def kernel(**inputs):
    import concourse.bacc as bacc
    from concourse.bass_utils import run_bass_kernel_spmd

    nc = bacc.Bacc("TRN2", target_bir_lowering=False, num_devices=1)
    arrays = {f"in_{name}": value for name, value in arrays_of(inputs).items()}
    aps = {name[3:]: nc.dram_tensor(name, value.shape, mybir.dt.from_np(value.dtype), kind="ExternalInput").ap()
           for name, value in arrays.items()}
    out = nc.dram_tensor("out", (TOK, D), F32, kind="ExternalOutput").ap()
    build(nc, aps, out)
    result = run_bass_kernel_spmd(nc, [arrays], core_ids=[0])
    return result.results[0]["out"].reshape(NB, S, D)
```

```python
from contextlib import ExitStack

import numpy as np
import concourse.bass as bass
from concourse import mybir

F32 = mybir.dt.float32
F32R = mybir.dt.float32r
I32 = mybir.dt.int32
U32 = mybir.dt.uint32
ALU = mybir.AluOpType
ACT = mybir.ActivationFunctionType
AX = mybir.AxisListType

P = 128
D = 512
DC = D // P
NB, S = 32, 32
TOK = NB * S
NT = TOK // P
BPT = P // S
SK = 257
SKE = SK + 1
XH = 16
XD = D // XH
HPC = P // XD
L, H, E = 2, 8, 64
F = 2048
FC = F // P
FS = 4
PAIR = (slice(0, E), slice(E, 2 * E))
K_BANK = (0, 1, 4, 5)
EARLY = 6
X2_BANK = (1, 2, 3, 4, 5, 2, 3, 2)
WS = 4
NE, HID = 8, 1024
GT = 256
NG = (2 * TOK - NE) // GT + NE
SLOTS = NG * GT
PIECES = 6
NEG_HUGE = -3.0e38
INV_SQRT_XD = float(1.0 / np.sqrt(np.float32(XD)))

PARTS = [(0, 0), (0, 1), (1, 0)]

VEC = {"bq": 0, "bk": 4, "bv": 8, "thr": 12, "head": 16}
NVEC = 20


def r(ap):
    return ap.bitcast(F32)


def wait_alone(eng, semaphore, value):
    value = eng.compute_val(value)
    eng.wait_ge(semaphore, 1)
    eng.wait_ge(semaphore, value)


def products(nc, out, terms, lhs, rhs, start=True):
    steps = [(t, a, b) for t in terms for a, b in PARTS]
    for n, (t, a, b) in enumerate(steps):
        last = nc.tensor.matmul(out, lhs(t, a), rhs(t, b), start=start and n == 0, stop=n == len(steps) - 1)
    return last


def build(nc, a, out, dbg=None):
    with ExitStack() as whole:
        def holder(stack):
            def sb(name, shape, dt=F32):
                return stack.enter_context(nc.sbuf_tensor(name, shape, dt))
            return sb

        taken = []

        def sem(name):
            taken.append(nc.alloc_semaphore(name))
            return taken[-1]

        def end_phase():
            nc.clear_and_free_semaphores(list(taken))
            nc.all_engine_barrier()
            taken.clear()

        keep = holder(whole)
        bank = [whole.enter_context(nc.psum_tensor(f"bank{i}", [P, 512], F32)) for i in range(8)]
        X = keep("X", [P, NT, D])
        ident = keep("ident", [P, P])
        vec = keep("vec", [P, NVEC])
        mhalf = keep("mhalf", [P, 64])
        x1_stats = keep("x1_stats", [P, NT, 6])
        xg = nc.dram_tensor("xg", (SLOTS, D), F32).ap()
        cross_attention(nc, a, whole, holder, sem, bank, X, ident, vec, mhalf, x1_stats, xg)
        end_phase()
        A = keep("A", [P, NT, D])
        if dbg != "x1":
            yg = nc.dram_tensor("yg", (SLOTS, D), F32).ap()
            retention_layers(nc, a, whole, holder, sem, bank, X, A, ident, vec, mhalf, x1_stats)
            end_phase()
            if dbg is None or dbg == "x3":
                mixture(nc, a, out, whole, holder, sem, bank, X, A, ident, mhalf, xg, yg)
                return
            done = sem("dbg_done")
            with nc.Block() as block:
                @block.sync
                def _(sp):
                    sp.dma_start(out.rearrange("(t p) d -> p t d", p=P), A[:, :, :]).then_inc(done, 16)
                    sp.wait_ge(done, 16)
            return
        if dbg == "x1":
            done = sem("dbg_done")
            with nc.Block() as block:
                @block.sync
                def _(sp):
                    sp.dma_start(out.rearrange("(t p) d -> p t d", p=P), X[:, :, :]).then_inc(done, 16)
                    sp.wait_ge(done, 16)
            return


def cross_attention(nc, a, whole, holder, sem, bank, X, ident, vec, mhalf, x1_stats, xg):
    def col(name, c=0):
        return vec[:, VEC[name] + c:VEC[name] + c + 1]

    with ExitStack() as phase:
        sb = holder(phase)
        wk = sb("wk", [P, 2, DC, D], F32R)
        wv = sb("wv", [P, 2, DC, D], F32R)
        wo = sb("wo", [P, 2, DC, D], F32R)
        qT = sb("qT", [P, 2, DC, TOK], F32R)
        vlast = sb("vlast", [3 * NB, D], F32R)
        thr = sb("thr", [P, DC])
        bo_bc = sb("bo_bc", [P, D])
        eye32 = sb("eye32", [P, NB, 32])
        ctxraw = [sb("ctxraw0", [P, DC, SK])]
        ctx = [sb("ctx0", [P, 2, DC, SKE], F32R)]
        ctx_in = [sem("ctx_in0"), sem("ctx_in1")]
        ctx_hi, ctx_lo, zeroed = sem("ctx_hi"), sem("ctx_lo"), sem("zeroed")

        with ExitStack() as inner:
            sbi = holder(inner)
            xT = sbi("xT", [P, 2, DC, TOK], F32R)
            raw = [sbi(f"raw{i}", [P, DC, D]) for i in range(3)]
            wq = sbi("wq", [P, 2, DC, D], F32R)
            craw = sbi("craw", [P, DC, P])
            cl = sbi("cl", [P, 2, DC, P], F32R)
            stats = sbi("stats", [P, NT, 6])
            mv = sbi("mv", [P, NT, 2])
            veps = sbi("veps", [P, NT])
            rstd = sbi("rstd", [P, NT])
            xh = sbi("xh", [P, 2, D])
            th = sbi("th", [P, 5, DC])
            x_in = [sem(f"x_in{i}") for i in range(2)]
            vec_in, id_in, cl_in, misc_in = sem("vec_in"), sem("id_in"), sem("cl_in"), sem("misc_in")
            w_in = [sem(f"w_in{i}") for i in range(4)]
            half_set, x_stats, x_aggr, veps_ok, rstd_ok = sem("half_set"), sem("x_stats"), sem("x_aggr"), sem("veps_ok"), sem("rstd_ok")
            xh_ok, x_turned, xT_hi, xT_lo = sem("xh_ok"), sem("x_turned"), sem("xT_hi"), sem("xT_lo")
            w_hi, w_lo, cl_hi, cl_lo = sem("w_hi"), sem("w_lo"), sem("cl_hi"), sem("cl_lo")
            q_ps, q_hi, q_lo = sem("q_ps"), sem("q_hi"), sem("q_lo")
            vl_ps, vl_hi, vl_lo = sem("vl_ps"), sem("vl_hi"), sem("vl_lo")
            th_act, th_dve = sem("th_act"), sem("th_dve")
            weights = [(a["xwq"], wq), (a["xwv"], wv), (a["xwk"], wk), (a["xwo"], wo)]
            with nc.Block() as block:
                @block.sync
                def _(sp):
                    xv = a["x"].rearrange("(t p) d -> p t d", p=P)
                    sp.dma_start(X[:, 0:4, :], xv[:, 0:4, :]).then_inc(x_in[0], 16)
                    sp.dma_start(ident[:, :], a["ident"]).then_inc(id_in, 16)
                    sp.dma_start(X[:, 4:8, :], xv[:, 4:8, :]).then_inc(x_in[1], 16)
                    sp.dma_start(raw[0][:, :, :], weights[0][0]).then_inc(w_in[0], 16)
                    sp.dma_start(vec[:, :], a["vec"]).then_inc(vec_in, 16)
                    sp.dma_start(craw[:, :, :], a["ctx_last"]).then_inc(cl_in, 16)
                    for i in (1, 2):
                        sp.dma_start(raw[i][:, :, :], weights[i][0]).then_inc(w_in[i], 16)
                    sp.dma_start(ctxraw[0][:, :, :], a["ctx"][0].rearrange("p (c n) -> p c n", c=DC)).then_inc(ctx_in[0], 16)
                    sp.dma_start(bo_bc[:, :], a["bo_bc"]).then_inc(misc_in, 16)
                    sp.dma_start(eye32[:, :, :], a["eye32"]).then_inc(misc_in, 16)
                    sp.wait_ge(w_hi, 1)
                    sp.wait_ge(w_lo, 1)
                    sp.dma_start(raw[0][:, :, :], weights[3][0]).then_inc(w_in[3], 16)
                    sp.wait_ge(misc_in, 32)

                @block.gpsimd
                def _(pool):
                    nc.gpsimd.memset(mhalf[:, :], -0.5).then_inc(half_set, 1)
                    pool.wait_ge(half_set, 1)
                    for i in range(2):
                        pool.wait_ge(veps_ok, i + 1)
                        nc.gpsimd.tensor_tensor(rstd[:, 4 * i:4 * i + 4], veps[:, 4 * i:4 * i + 4], mhalf[:, 0:4], ALU.pow).then_inc(rstd_ok, 1)
                    nc.gpsimd.memset(r(ctx[0][:, :, :, SK:SKE]), 0.0).then_inc(zeroed, 1)
                    pool.wait_ge(ctx_hi, 1)
                    nc.gpsimd.tensor_tensor(ctx[0][:, 1, :, 0:SK], ctxraw[0][:, :, :], r(ctx[0][:, 0, :, 0:SK]), ALU.subtract).then_inc(ctx_lo, 1)

                @block.vector
                def _(dve):
                    for i in range(2):
                        tiles = range(4 * i, 4 * i + 4)
                        dve.wait_ge(x_in[i], 16)
                        for t in tiles:
                            nc.vector.bn_stats(stats[:, t, :], X[:, t, :]).then_inc(x_stats, 1)
                        for t in tiles:
                            dve.wait_ge(x_stats, t + 1)
                            nc.vector.bn_aggr(mv[:, t, :], stats[:, t, :]).then_inc(x_aggr, 1)
                        dve.wait_ge(x_aggr, 4 * i + 4)
                        nc.vector.tensor_scalar(veps[:, 4 * i:4 * i + 4], mv[:, 4 * i:4 * i + 4, 1], 1e-5, None, ALU.add).then_inc(veps_ok, 1)

                    def normalise(t):
                        dve.wait_ge(rstd_ok, t // 4 + 1)
                        if t >= 2:
                            dve.wait_ge(x_turned, t - 1)
                        nc.vector.tensor_scalar(xh[:, t % 2, :], X[:, t, :], mv[:, t, 0:1], rstd[:, t:t + 1],
                                                ALU.subtract, ALU.mult).then_inc(xh_ok, 1)

                    def turned_lo(t):
                        dve.wait_ge(xT_hi, t + 1)
                        nc.vector.tensor_tensor(xT[:, 1, :, t * P:(t + 1) * P], bank[t % 2][:, :].rearrange("p (c n) -> p c n", c=DC),
                                                r(xT[:, 0, :, t * P:(t + 1) * P]), ALU.subtract).then_inc(xT_lo, 1)

                    def weight_lo(i):
                        dve.wait_ge(w_hi, i + 1)
                        nc.vector.tensor_tensor(weights[i][1][:, 1, :, :], raw[i % 3][:, :, :], r(weights[i][1][:, 0, :, :]), ALU.subtract).then_inc(w_lo, 1)

                    def query_lo(n):
                        half, dc = n // 4, n % 4
                        dve.wait_ge(q_hi, n + 1)
                        hi = qT[:, 0, dc, half * 512:(half + 1) * 512]
                        nc.vector.scalar_tensor_tensor(qT[:, 1, dc, half * 512:(half + 1) * 512], bank[2 + n % 2][:, :], col("bq", dc),
                                                       r(hi), ALU.add, ALU.subtract).then_inc(q_lo, 1)
                    normalise(0)
                    normalise(1)
                    turned_lo(0)
                    normalise(2)
                    turned_lo(1)
                    normalise(3)
                    weight_lo(0)
                    turned_lo(2)
                    turned_lo(3)
                    dve.wait_ge(vec_in, 16)
                    for n in range(4):
                        normalise(4 + n)
                        query_lo(n)
                        turned_lo(4 + n)
                    weight_lo(1)
                    query_lo(4)
                    dve.wait_ge(cl_hi, 1)
                    nc.vector.tensor_tensor(cl[:, 1, :, :], craw[:, :, :], r(cl[:, 0, :, :]), ALU.subtract).then_inc(cl_lo, 1)
                    query_lo(5)
                    weight_lo(2)
                    query_lo(6)
                    query_lo(7)
                    weight_lo(3)
                    dve.wait_ge(vl_hi, 1)
                    nc.vector.tensor_tensor(vlast[2 * NB:, :], bank[4][2 * NB:3 * NB, :], r(vlast[2 * NB:, :]), ALU.subtract).then_inc(vl_lo, 1)
                    dve.wait_ge(vec_in, 16)
                    raw_thr = vec[:, VEC["thr"]:VEC["thr"] + DC]
                    nc.vector.scalar_tensor_tensor(th[:, 0, :], raw_thr, -1.0, raw_thr, ALU.mult, ALU.max).then_inc(th_dve, 1)
                    nc.vector.tensor_scalar(th[:, 1, :], raw_thr, 0.0, None, ALU.max).then_inc(th_dve, 1)
                    dve.wait_ge(th_act, 2)
                    dve.wait_ge(th_dve, 2)
                    nc.vector.tensor_tensor(th[:, 4, :], th[:, 1, :], th[:, 3, :], ALU.add).then_inc(th_dve, 1)
                    dve.wait_ge(th_dve, 3)
                    nc.vector.tensor_scalar(thr[:, :], th[:, 4, :], float(np.sqrt(np.float32(XD))), None, ALU.mult).then_inc(th_dve, 1)

                @block.scalar
                def _(act):
                    def weight_hi(i):
                        act.wait_ge(w_in[i], 16)
                        nc.scalar.activation(weights[i][1][:, 0, :, :], raw[i % 3][:, :, :], ACT.Copy).then_inc(w_hi, 1)

                    def turned_hi(t):
                        act.wait_ge(x_turned, t + 1)
                        nc.scalar.activation(xT[:, 0, :, t * P:(t + 1) * P], bank[t % 2][:, :].rearrange("p (c n) -> p c n", c=DC),
                                             ACT.Copy).then_inc(xT_hi, 1)

                    def query_hi(n):
                        half, dc = n // 4, n % 4
                        act.wait_ge(q_ps, n + 1)
                        nc.scalar.activation(qT[:, 0, dc, half * 512:(half + 1) * 512], bank[2 + n % 2][:, :], ACT.Identity,
                                             bias=col("bq", dc)).then_inc(q_hi, 1)
                    turned_hi(0)
                    turned_hi(1)
                    weight_hi(0)
                    turned_hi(2)
                    turned_hi(3)
                    act.wait_ge(vec_in, 16)
                    for n in range(4):
                        query_hi(n)
                        turned_hi(4 + n)
                        if n == 2:
                            act.wait_ge(cl_in, 16)
                            nc.scalar.activation(cl[:, 0, :, :], craw[:, :, :], ACT.Copy).then_inc(cl_hi, 1)
                    weight_hi(1)
                    query_hi(4)
                    weight_hi(2)
                    query_hi(5)
                    act.wait_ge(ctx_in[0], 16)
                    nc.scalar.activation(ctx[0][:, 0, :, 0:SK], ctxraw[0][:, :, :], ACT.Copy).then_inc(ctx_hi, 1)
                    query_hi(6)
                    query_hi(7)
                    weight_hi(3)
                    act.wait_ge(vl_ps, 1)
                    nc.scalar.activation(vlast[:, :], bank[4][0:3 * NB, :], ACT.Copy).then_inc(vl_hi, 1)
                    act.wait_ge(th_dve, 1)
                    nc.scalar.activation(th[:, 2, :], th[:, 0, :], ACT.Exp, scale=-1.0).then_inc(th_act, 1)
                    act.wait_ge(th_act, 1)
                    nc.scalar.activation(th[:, 3, :], th[:, 2, :], ACT.Ln, bias=1.0).then_inc(th_act, 1)

                @block.tensor
                def _(pe):
                    pe.wait_ge(id_in, 16)
                    def turn(t):
                        pe.wait_ge(xh_ok, t + 1)
                        if t >= 2:
                            pe.wait_ge(xT_hi, t - 1)
                            pe.wait_ge(xT_lo, t - 1)
                        for c in range(DC):
                            last = nc.tensor.transpose(bank[t % 2][:, c * P:(c + 1) * P], xh[:, t % 2, c * P:(c + 1) * P], ident[:, :])
                        last.then_inc(x_turned, 1)

                    def query(n):
                        half, dc = n // 4, n % 4
                        if n >= 2:
                            pe.wait_ge(q_lo, n - 1)
                        products(nc, bank[2 + n % 2][:, :], range(DC), lambda c, h: wq[:, h, c, dc * P:(dc + 1) * P],
                                 lambda c, h: xT[:, h, c, half * 512:(half + 1) * 512]).then_inc(q_ps, 1)
                    for t in range(4):
                        turn(t)
                    pe.wait_ge(w_lo, 1)
                    pe.wait_ge(xT_lo, 4)
                    for n in range(4):
                        query(n)
                        turn(4 + n)
                    pe.wait_ge(xT_lo, NT)
                    for n in range(4, 8):
                        query(n)
                    pe.wait_ge(w_lo, 2)
                    pe.wait_ge(cl_lo, 1)
                    products(nc, bank[4][:, :], range(DC), lambda c, h: cl[:, h, c, :], lambda c, h: wv[:, h, c, :]).then_inc(vl_ps, 1)

        with ExitStack() as inner:
            sbi = holder(inner)
            ctxraw.append(sbi("ctxraw1", [P, DC, SK]))
            ctx.append(sbi("ctx1", [P, 2, DC, SKE], F32R))
            kT = sbi("kT", [P, 2, DC, SKE], F32R)
            v = [sbi(f"v{i}", [P, 2, 2, D], F32R) for i in range(2)]
            qbd = sbi("qbd", [P, 2, DC, P], F32R)
            u = sbi("u", [P, DC, SKE])
            ex = sbi("ex", [P, DC, SKE])
            pr = sbi("pr", [P, DC, SKE])
            umax = sbi("umax", [P, DC])
            keepany = sbi("keepany", [P, DC])
            sc = sbi("sc", [P, DC])
            nb = sbi("nb", [P, DC])
            floor = sbi("floor", [P, DC])
            psums = sbi("psums", [P, DC])
            rsum = sbi("rsum", [P, DC])
            plast = sbi("plast", [P, DC, 3, NB])
            pT = sbi("pT", [P, 2, 2, DC, P], F32R)
            pTl = sbi("pTl", [3 * NB, DC, P], F32R)
            oT = sbi("oT", [P, DC, P])
            zero = sbi("zero", [P, D])
            oT_hl = sbi("oT_hl", [P, 2, DC, P], F32R)
            k_ps, v_ps, s_ps, p_turned, pv_ps, o_ps = (sem(n) for n in ("k_ps", "v_ps", "s_ps", "p_turned", "pv_ps", "o_ps"))
            k_hi, k_lo, v_hi, v_lo = (sem(n) for n in ("k_hi", "k_lo", "v_hi", "v_lo"))
            u_ok, soft_ok, ex_ok, pr_ok, rsum_ok, pn_ok, plast_ok = (
                sem(n) for n in ("u_ok", "soft_ok", "ex_ok", "pr_ok", "rsum_ok", "pn_ok", "plast_ok"))
            pT_hi, pT_lo, oT_ok, oT_hi, oT_lo, x1_sum, x1_ok = (
                sem(n) for n in ("pT_hi", "pT_lo", "oT_ok", "oT_hi", "oT_lo", "x1_sum", "x1_ok"))
            qbd_ok, filled, x1_measured = sem("qbd_ok"), sem("filled"), sem("x1_measured")
            ctx_view = a["ctx"]

            with nc.Block() as block:
                @block.sync
                def _(sp):
                    def load(it, k):
                        b = BPT * it + k
                        sp.dma_start(ctxraw[k % 2][:, :, :], ctx_view[bass.ds(b, 1), :, :].rearrange("o p (c n) -> p (o c) n", c=DC)).then_inc(ctx_in[k % 2], 16)
                    ZT = SLOTS // P // NT
                    xg_tiles = xg.rearrange("(n p) d -> p n d", p=P)
                    for k in range(1, BPT):
                        if k >= 2:
                            sp.wait_ge(ctx_hi, k - 1)
                            sp.wait_ge(ctx_lo, k - 1)
                        load(0, k)
                    sp.wait_ge(zeroed, 3)
                    with sp.Fori(1, NT) as it:
                        for k in range(BPT):
                            sp.wait_ge(ctx_hi, BPT * it + k - 1)
                            sp.wait_ge(ctx_lo, BPT * it + k - 1)
                            load(it, k)
                        sp.dma_start(xg_tiles[:, bass.ds(ZT * (it - 1), ZT), :], zero[:, :].unsqueeze(1).broadcast_to([P, ZT, D])).then_inc(filled, 16)
                    rest = ZT * (NT - 1)
                    sp.dma_start(xg_tiles[:, rest:, :], zero[:, :].unsqueeze(1).broadcast_to([P, SLOTS // P - rest, D])).then_inc(filled, 16)
                    sp.wait_ge(filled, 16 * NT)

                @block.gpsimd
                def _(pool):
                    nc.gpsimd.memset(r(ctx[1][:, :, :, SK:SKE]), 0.0).then_inc(zeroed, 1)
                    nc.gpsimd.memset(zero[:, :], 0.0).then_inc(zeroed, 1)

                    def context_lo(it, k, b):
                        pool.wait_ge(ctx_hi, b + 1)
                        nc.gpsimd.tensor_tensor(ctx[k % 2][:, 1, :, 0:SK], ctxraw[k % 2][:, :, :], r(ctx[k % 2][:, 0, :, 0:SK]),
                                                ALU.subtract).then_inc(ctx_lo, 1)

                    def spread_q(b):
                        src = r(qT[:, :, :, :]).rearrange("p h c n -> p (h c) n")[:, :, bass.ds(b * S, S)]
                        nc.gpsimd.tensor_tensor(qbd[:, :, :, :].rearrange("p h c (g n) -> p (h c) g n", g=HPC),
                                                src.unsqueeze(2).broadcast_to([P, 2 * DC, HPC, S]),
                                                vec[:, VEC["head"]:VEC["head"] + HPC].unsqueeze(1).unsqueeze(3).broadcast_to([P, 2 * DC, HPC, S]),
                                                ALU.mult).then_inc(qbd_ok, 1)

                    def normalise(b):
                        pool.wait_ge(rsum_ok, b + 1)
                        nc.gpsimd.tensor_tensor(pr[:, :, 0:SK], pr[:, :, 0:SK], rsum[:, :].unsqueeze(2).broadcast_to([P, DC, SK]),
                                                ALU.mult).then_inc(pn_ok, 1)
                        pool.wait_ge(pn_ok, b + 1)
                        nc.gpsimd.tensor_tensor(plast[:, :, :, :], pr[:, :, SK - 1:SK].unsqueeze(3).broadcast_to([P, DC, 3, NB]),
                                                eye32[:, bass.ds(b, 1), :].unsqueeze(1).broadcast_to([P, DC, 3, NB]), ALU.mult).then_inc(plast_ok, 1)

                    def body(it, first, last):
                        for k in range(BPT):
                            b = BPT * it + k
                            if not (first and k == 0):
                                pool.wait_ge(s_ps, DC * b)
                            spread_q(b)
                            if not (last and k == BPT - 1):
                                if not (first and k == 0):
                                    pool.wait_ge(v_ps, 2 * b)
                                context_lo(it, k + 1, b + 1)
                            if k == 2 and not first:
                                add_bias(it - 1)
                            normalise(b)

                    def add_bias(t):
                        pool.wait_ge(x1_sum, t + 1)
                        xt = X[:, bass.ds(t, 1), :].rearrange("p o d -> p (o d)")
                        nc.gpsimd.tensor_tensor(xt, xt, bo_bc[:, :], ALU.add).then_inc(x1_ok, 1)
                    body(0, True, False)
                    with pool.Fori(1, NT - 1) as it:
                        body(it, False, False)
                    body(NT - 1, False, True)
                    add_bias(NT - 1)

                @block.scalar
                def _(act):
                    def context_hi(k, use, b):
                        act.wait_ge(ctx_in[k % 2], 16 * use)
                        nc.scalar.activation(ctx[k % 2][:, 0, :, 0:SK], ctxraw[k % 2][:, :, :], ACT.Copy).then_inc(ctx_hi, 1)

                    def exps(b):
                        act.wait_ge(soft_ok, 5 * b + 5)
                        for c in range(DC):
                            nc.scalar.activation(ex[:, c, 0:SK], u[:, c, 0:SK], ACT.Exp, bias=nb[:, c:c + 1], scale=sc[:, c:c + 1]).then_inc(ex_ok, 1)

                    def turned(b):
                        for kt in range(2):
                            act.wait_ge(p_turned, 3 * b + kt + 1)
                            nc.scalar.activation(pT[:, 0, kt, :, :], bank[4 + kt][:, :].rearrange("p (c n) -> p c n", c=DC), ACT.Copy).then_inc(pT_hi, 1)
                        act.wait_ge(p_turned, 3 * b + 3)
                        nc.scalar.activation(pTl[:, :, :], bank[6][0:3 * NB, :].rearrange("p (c n) -> p c n", c=DC), ACT.Copy).then_inc(pT_hi, 1)

                    def heads_hi(t):
                        act.wait_ge(oT_ok, HPC * BPT * (t + 1))
                        nc.scalar.activation(oT_hl[:, 0, :, :], oT[:, :, :], ACT.Copy).then_inc(oT_hi, 1)

                    def body(it, first, last):
                        for k in range(BPT):
                            b = BPT * it + k
                            begin = first and k == 0
                            if begin:
                                act.wait_ge(zeroed, 3)
                            for dc in range(DC):
                                act.wait_ge(k_ps, DC * b + dc + 1)
                                nc.scalar.activation(kT[:, 0, dc, :], bank[K_BANK[dc]][:, 0:SKE], ACT.Identity, bias=col("bk", dc)).then_inc(k_hi, 1)
                                if dc == 1 and k == 1 and not first:
                                    heads_hi(it - 1)
                                if dc == 1 and not (last and k == BPT - 1):
                                    context_hi(k + 1, 2 * it + (k + 1) // 2 + 1, b + 1)
                            act.wait_ge(v_ps, 2 * b + 1)
                            nc.scalar.activation(v[k % 2][:, 0, 0, :], bank[0][:, :], ACT.Copy).then_inc(v_hi, 1)
                            if not begin:
                                turned(b - 1)
                            act.wait_ge(v_ps, 2 * b + 2)
                            nc.scalar.activation(v[k % 2][:, 0, 1, :], bank[1][:, :], ACT.Copy).then_inc(v_hi, 1)
                            exps(b)
                    body(0, True, False)
                    with act.Fori(1, NT - 1) as it:
                        body(it, False, False)
                    body(NT - 1, False, True)
                    turned(NB - 1)
                    heads_hi(NT - 1)

                @block.vector
                def _(dve):
                    def weigh(b):
                        for c in range(DC):
                            dve.wait_ge(ex_ok, DC * b + c + 1)
                            nc.vector.scalar_tensor_tensor(pr[:, c, 0:SK], u[:, c, 0:SK], floor[:, c:c + 1], ex[:, c, 0:SK],
                                                           ALU.is_gt, ALU.mult, accum_out=psums[:, c:c + 1]).then_inc(pr_ok, 1)

                    def reciprocal(b):
                        dve.wait_ge(pr_ok, DC * (b + 1))
                        nc.vector.reciprocal(rsum[:, :], psums[:, :]).then_inc(rsum_ok, 1)

                    def turned_lo(b):
                        for kt in range(2):
                            dve.wait_ge(pT_hi, 3 * b + kt + 1)
                            nc.vector.tensor_tensor(pT[:, 1, kt, :, :], bank[4 + kt][:, :].rearrange("p (c n) -> p c n", c=DC),
                                                    r(pT[:, 0, kt, :, :]), ALU.subtract).then_inc(pT_lo, 1)
                        dve.wait_ge(pT_hi, 3 * b + 3)
                        nc.vector.tensor_tensor(pTl[NB:2 * NB, :, :], bank[6][NB:2 * NB, :].rearrange("p (c n) -> p c n", c=DC),
                                                r(pTl[NB:2 * NB, :, :]), ALU.subtract).then_inc(pT_lo, 1)

                    def threshold(b, cs):
                        for c in cs:
                            dve.wait_ge(s_ps, DC * b + c + 1)
                            nc.vector.tensor_scalar(u[:, c, 0:SK], bank[2 + c % 2][:, 0:SK], thr[:, c:c + 1], None,
                                                    ALU.subtract, ALU.max, accum_out=umax[:, c:c + 1]).then_inc(u_ok, 1)

                    def heads(k, b):
                        dve.wait_ge(pv_ps, b + 1)
                        for g in range(HPC):
                            rows = slice(g * XD, (g + 1) * XD)
                            nc.vector.tensor_tensor(oT[rows, :, k * S:(k + 1) * S],
                                                    bank[7][rows, :].rearrange("p (c n) -> p c n", c=DC)[:, :, g * S:(g + 1) * S],
                                                    vec[rows, VEC["bv"]:VEC["bv"] + DC].unsqueeze(2).broadcast_to([XD, DC, S]),
                                                    ALU.add).then_inc(oT_ok, 1)

                    def softmax_terms(b):
                        n = 5 * b
                        dve.wait_ge(u_ok, DC * b + DC)
                        nc.vector.tensor_scalar(keepany[:, :], umax[:, :], 0.0, None, ALU.is_gt).then_inc(soft_ok, 1)
                        nc.vector.tensor_scalar(floor[:, :], umax[:, :], 0.0, NEG_HUGE, ALU.is_le, ALU.mult).then_inc(soft_ok, 1)
                        dve.wait_ge(soft_ok, n + 2)
                        nc.vector.tensor_scalar(sc[:, :], keepany[:, :], INV_SQRT_XD, None, ALU.mult).then_inc(soft_ok, 1)
                        dve.wait_ge(soft_ok, n + 3)
                        nc.vector.tensor_tensor(nb[:, :], sc[:, :], umax[:, :], ALU.mult).then_inc(soft_ok, 1)
                        dve.wait_ge(soft_ok, n + 4)
                        nc.vector.tensor_scalar(nb[:, :], nb[:, :], -1.0, None, ALU.mult).then_inc(soft_ok, 1)

                    def project_lo(t):
                        dve.wait_ge(oT_hi, t + 1)
                        nc.vector.tensor_tensor(oT_hl[:, 1, :, :], oT[:, :, :], r(oT_hl[:, 0, :, :]), ALU.subtract).then_inc(oT_lo, 1)

                    def add_x(t):
                        dve.wait_ge(o_ps, t + 1)
                        xt = X[:, bass.ds(t, 1), :].rearrange("p o d -> p (o d)")
                        nc.vector.tensor_tensor(xt, bank[7][:, :], xt, ALU.add).then_inc(x1_sum, 1)

                    def statistics(t):
                        dve.wait_ge(x1_ok, t + 1)
                        nc.vector.bn_stats(x1_stats[:, bass.ds(t, 1), :].rearrange("p o s -> p (o s)"),
                                           X[:, bass.ds(t, 1), :].rearrange("p o d -> p (o d)")).then_inc(x1_measured, 1)

                    def body(it, first):
                        for k in range(BPT):
                            b = BPT * it + k
                            begin = first and k == 0
                            if k == BPT - 1 and not first:
                                statistics(it - 1)
                            for dc in range(DC):
                                dve.wait_ge(k_hi, DC * b + dc + 1)
                                nc.vector.scalar_tensor_tensor(kT[:, 1, dc, :], bank[K_BANK[dc]][:, 0:SKE], col("bk", dc), r(kT[:, 0, dc, :]),
                                                               ALU.add, ALU.subtract).then_inc(k_lo, 1)
                                if dc == 1 and k == 1 and not first:
                                    project_lo(it - 1)

                            def value_lo(kt):
                                dve.wait_ge(v_hi, 2 * b + kt + 1)
                                nc.vector.tensor_tensor(v[k % 2][:, 1, kt, :], bank[kt][:, :], r(v[k % 2][:, 0, kt, :]), ALU.subtract).then_inc(v_lo, 1)
                            value_lo(0)
                            if k == 1 and not first:
                                add_x(it - 1)
                            threshold(b, (0, 1))
                            if not begin:
                                turned_lo(b - 1)
                            value_lo(1)
                            threshold(b, (2, 3))
                            softmax_terms(b)
                            weigh(b)
                            reciprocal(b)
                            if not begin:
                                heads((k - 1) % BPT, b - 1)
                    body(0, True)
                    with dve.Fori(1, NT) as it:
                        body(it, False)
                    turned_lo(NB - 1)
                    heads(BPT - 1, NB - 1)
                    project_lo(NT - 1)
                    add_x(NT - 1)
                    statistics(NT - 1)

                @block.tensor
                def _(pe):
                    def turn(b):
                        pe.wait_ge(pn_ok, b + 1)
                        for kt in range(2):
                            for c in range(DC):
                                last = nc.tensor.transpose(bank[4 + kt][:, c * P:(c + 1) * P], pr[:, c, kt * P:(kt + 1) * P], ident[:, :])
                            last.then_inc(p_turned, 1)
                        pe.wait_ge(plast_ok, b + 1)
                        for c in range(DC):
                            last = nc.tensor.transpose(bank[6][0:3 * NB, c * P:(c + 1) * P], plast[:, c, :, :].rearrange("p k n -> p (k n)"), ident[:, :])
                        last.then_inc(p_turned, 1)

                    def attend(k, b, t_sum):
                        pe.wait_ge(pT_lo, 3 * b + 3)
                        if t_sum is not None:
                            pe.wait_ge(x1_sum, t_sum)
                        for c in range(DC):
                            cols = slice(c * P, (c + 1) * P)
                            steps = [(lambda h, kt=kt: v[k % 2][:, h, kt, cols], lambda h, kt=kt: pT[:, h, kt, c, :]) for kt in range(2)]
                            nc.tensor.matmul(bank[7][:, cols], vlast[:, cols], pTl[:, c, :], start=True, stop=False)
                            last = products(nc, bank[7][:, cols], range(2), lambda s, h: steps[s][0](h), lambda s, h: steps[s][1](h), start=False)
                        last.then_inc(pv_ps, 1)

                    def score(b, cs, begin):
                        for c in cs:
                            pe.wait_ge(k_lo, DC * b + c + 1)
                            if not (begin and c < 2):
                                pe.wait_ge(u_ok, DC * b + c - 1)
                            if c == 0:
                                pe.wait_ge(qbd_ok, b + 1)
                            products(nc, bank[2 + c % 2][:, 0:SKE], range(1), lambda _, h: qbd[:, h, c, :],
                                     lambda _, h: kT[:, h, c, :]).then_inc(s_ps, 1)

                    def project(t):
                        pe.wait_ge(oT_lo, t + 1)
                        products(nc, bank[7][:, :], range(DC), lambda c, h: oT_hl[:, h, c, :], lambda c, h: wo[:, h, c, :]).then_inc(o_ps, 1)

                    def body(it, first):
                        for k in range(BPT):
                            b = BPT * it + k
                            begin = first and k == 0
                            pe.wait_ge(ctx_lo, b + 1)
                            for dc in range(DC):
                                if dc < 2 and not begin:
                                    pe.wait_ge(v_lo, 2 * b - 1 + dc)
                                products(nc, bank[K_BANK[dc]][:, 0:SKE], range(DC), lambda c, h: wk[:, h, c, dc * P:(dc + 1) * P],
                                         lambda c, h: ctx[k % 2][:, h, c, :]).then_inc(k_ps, 1)

                            def value(kt):
                                pe.wait_ge(k_lo, DC * b + 1 + kt)
                                products(nc, bank[kt][:, :], range(DC), lambda c, h: ctx[k % 2][:, h, c, kt * P:(kt + 1) * P],
                                         lambda c, h: wv[:, h, c, :]).then_inc(v_ps, 1)
                            value(0)
                            if k == 1 and not first:
                                project(it - 1)
                            if not begin:
                                pe.wait_ge(k_lo, DC * b + DC)
                                turn(b - 1)
                            score(b, (0, 1), begin)
                            value(1)
                            score(b, (2, 3), begin)
                            if not begin:
                                if not (first and k == 1):
                                    pe.wait_ge(oT_ok, HPC * (b - 1))
                                attend(k - 1, b - 1, it if k == 1 and not first else None)
                    body(0, True)
                    with pe.Fori(1, NT) as it:
                        body(it, False)
                    turn(NB - 1)
                    pe.wait_ge(oT_ok, HPC * (NB - 1))
                    attend(BPT - 1, NB - 1, None)
                    project(NT - 1)


def retention_layers(nc, a, whole, holder, sem, bank, X, A, ident, vec, mhalf, x1_stats):
    with ExitStack() as phase:
        sb = holder(phase)
        gn_bc = sb("gn_bc", [P, 2, D])
        lnv = sb("lnv", [P, 2, 2, DC])
        rot = sb("rot", [P, 4, E // 2])
        decay = sb("decay", [P, 2, DC, P])
        mv = sb("r_mv", [P, NT, 2])
        stats = sb("r_stats", [P, NT, 6])
        stats2 = sb("r_stats2", [P, NT, 6])
        veps = sb("r_veps", [P, NT])
        rstd = sb("r_rstd", [P, NT])
        xh = [sb(f"r_xh{i}", [P, D]) for i in range(2)]
        xf = [sb(f"xf{i}", [P, DC, P]) for i in range(2)]
        att = ExitStack()
        sba = holder(att)
        wq, wk = (sba(n, [P, 2, DC, D], F32R) for n in ("r_wq", "r_wk"))
        wraw = [sba(f"wraw{i}", [P, DC, 256]) for i in range(WS)]
        wv, wg, wo = (sba(n, [P, 2, DC, D], F32R) for n in ("r_wv", "r_wg", "r_wo"))
        matrices = (wq, wk, wv, wg, wo)
        xn = [sba(f"xn{i}", [P, 2, DC, P], F32R) for i in range(2)]
        rc = sba("rc", [P, 2, D])
        rs = sba("rs", [P, 2, D])
        qk = sba("qk", [P, 2, D])
        kT = sba("r_kT", [P, 2, DC, P], F32R)
        qd = sba("qd", [P, 2, DC, 2, P], F32R)
        vv = sba("vv", [P, 2, D], F32R)
        sw = sba("sw", [P, D])
        sws = sba("sws", [P, 2, D])
        pf = sba("pf", [P, 2, DC, P])
        p_hl = sba("p_hl", [P, 2, 2, DC, P], F32R)
        gst = sba("gst", [P, H, 6])
        gmv = sba("gmv", [P, H, 2])
        gve = sba("gve", [P, H])
        grs = sba("grs", [P, H])
        y = sba("y", [P, D])
        yT = sba("yT", [P, 2, DC, P], F32R)
        att.close()
        ff = ExitStack()
        sbf = holder(ff)
        x2T = sbf("x2T", [P, 2, DC, TOK], F32R)
        fraw = [sbf(f"fraw{i}", [P, 2 * D]) for i in range(FS)]
        fw = [sbf(f"fw{i}", [P, 2, 2 * D], F32R) for i in range(FS)]
        hf32 = [sbf(f"hf32_{i}", [P, 512]) for i in range(2)]
        hh = [sbf(f"hh{i}", [P, 2, 512], F32R) for i in range(2)]
        ff.close()

        names = """cleared tab_in gn_in w_hi w_lo a0_ok st_ok ag_ok ve_ok rs_ok xh_ok x_turned xf_ok xn_hi xn_lo
            q_ps k_ps v_ps g_ps rc_ok qk_ok qk_turned qkT_hi qkT_lo v_hi v_lo sw_ok sws_ok s_ps pf_ok p_hi p_lo o_ps
            gst_ok gmv_ok gve_ok grs_ok cen_ok hn_ok ya_ok y_ok y_turned yT_hi yT_lo wo_ps res_ok
            st2_ok ag2_ok ve2_ok rs2_ok xh2_ok x2_turned xf2_ok x2_hi x2_lo
            f_hi f_lo up_ps h_ok h_hi h_lo down_ps ffn_ok ln0_ag ln0_ve ln0_rs""".split()
        m = {n: sem("r_" + n) for n in names}
        w_in = [sem(f"r_w_in{i}") for i in range(WS)]
        f_in = [sem(f"r_f_in{i}") for i in range(FS)]

        def tile_of(tensor, t):
            if isinstance(t, int):
                return tensor[:, t, :]
            return tensor[:, bass.ds(t, 1), :].rearrange("p o d -> p (o d)")

        def pairs(eng, body):
            body(0, True, False)
            with eng.Fori(1, NT // 2 - 1) as it:
                body(it, False, False)
            body(NT // 2 - 1, False, True)

        halves = [slice(0, 32), slice(32, 64)]

        def split_halves(ap):
            return ap.rearrange("p (h two e) -> p h two e", two=2, e=E // 2)

        with nc.Block() as block:
            @block.sync
            def _(sp):
                sp.dma_start(rot[:, :, :], a["rot"]).then_inc(m["tab_in"], 16)
                sp.dma_start(decay[:, :, :, :], a["decay"]).then_inc(m["tab_in"], 16)
                with sp.Fori(0, L) as layer:
                    sp.wait_ge(m["f_hi"], 2 * FC * layer + FS)
                    sp.wait_ge(m["f_lo"], 2 * FC * layer + FS)
                    sp.dma_start(gn_bc[:, :, :], a["gn"][bass.ds(layer, 1), :, :, :].rearrange("o p k d -> p (o k) d")).then_inc(m["gn_in"], 16)
                    sp.dma_start(lnv[:, :, :, :], a["lnv"][bass.ds(layer, 1), :, :].rearrange("o p n -> p (o n)")).then_inc(m["gn_in"], 16)
                    for j in range(10):
                        if j >= WS:
                            sp.wait_ge(m["w_hi"], 10 * layer + j - WS + 1)
                            sp.wait_ge(m["w_lo"], 10 * layer + j - WS + 1)
                        sp.dma_start(wraw[j % WS][:, :, :], a["wa"][bass.ds(layer, 1), j, :, :].rearrange("o p (c n) -> p (o c) n", c=DC)).then_inc(w_in[j % WS], 16)
                    wait_alone(sp, m["w_hi"], 10 * layer + 10)
                    sp.wait_ge(m["w_lo"], 10 * layer + 10)
                    with sp.Fori(0, 2) as half:
                        with sp.Fori(0, FC // FS) as it:
                            for k in range(FS):
                                n = 32 * layer + 16 * half + FS * it + k
                                sp.wait_ge(m["f_hi"], n + 1)
                                sp.wait_ge(m["f_lo"], n + 1)
                                sp.dma_start(fraw[k][:, :], a["wf"][bass.ds(layer, 1), bass.ds(FS * it + k, 1), :, :].rearrange("o q p n -> p (o q n)")).then_inc(f_in[k], 16)

            @block.gpsimd
            def _(pool):
                def root(src, dst, n, ok, value, done):
                    pool.wait_ge(ok, value)
                    nc.gpsimd.tensor_tensor(dst, src, mhalf[:, 0:n], ALU.pow).then_inc(done, 1)
                nc.gpsimd.memset(r(qd[:, :, :, :, :]), 0.0).then_inc(m["cleared"], 1)
                root(veps[:, :], rstd[:, :], NT, m["ln0_ve"], 1, m["ln0_rs"])
                def norm_root(n):
                    root(veps[:, 0:1], rstd[:, 0:1], 1, m["ve_ok"], n + 1, m["rs_ok"])
                norm_root(0)
                with pool.Fori(0, L) as layer:
                    n0 = 8 * layer

                    def combine(n, j):
                        pool.wait_ge(m["rc_ok"], 4 * n + 2 * j + 2)
                        c4, s4, o4 = (split_halves(z[:, j, :]) for z in (rc, rs, qk))
                        nc.gpsimd.tensor_tensor(o4[:, :, 0, :], c4[:, :, 0, :], s4[:, :, 1, :], ALU.subtract).then_inc(m["qk_ok"], 1)
                        nc.gpsimd.tensor_tensor(o4[:, :, 1, :], c4[:, :, 1, :], s4[:, :, 0, :], ALU.add).then_inc(m["qk_ok"], 1)

                    pool.wait_ge(m["gn_in"], 32 * layer + 32)

                    def body(it, first, last):
                        for k in range(2):
                            n = n0 + 2 * it + k
                            begin, end = first and k == 0, last and k == 1
                            if not end:
                                norm_root(n + 1)
                            combine(n, 0)
                            combine(n, 1)
                            if not begin:
                                root(gve[:, :], grs[:, :], H, m["gve_ok"], n, m["grs_ok"])
                                pool.wait_ge(m["ya_ok"], n)
                                pool.wait_ge(m["y_ok"], n)
                            pool.wait_ge(m["sw_ok"], n + 1)
                            for j in range(2):
                                nc.gpsimd.tensor_tensor(sws[:, j, :], sw[:, :], gn_bc[:, j, :], ALU.mult).then_inc(m["sws_ok"], 1)
                            if end:
                                root(veps[:, 0:EARLY], rstd[:, 0:EARLY], EARLY, m["ve2_ok"], 2 * layer + 1, m["rs2_ok"])
                            for j in range(2):
                                pool.wait_ge(m["p_hi"], 2 * n + j + 1)
                                nc.gpsimd.tensor_tensor(p_hl[:, 1, j, :, :], pf[:, j, :, :], r(p_hl[:, 0, j, :, :]), ALU.subtract).then_inc(m["p_lo"], 1)
                    pairs(pool, body)
                    root(gve[:, :], grs[:, :], H, m["gve_ok"], n0 + 8, m["grs_ok"])
                    root(veps[:, EARLY:], rstd[:, EARLY:], NT - EARLY, m["ve2_ok"], 2 * layer + 2, m["rs2_ok"])
                    norm_root(n0 + 8)

            @block.scalar
            def _(act):
                for _ in range(FS):
                    act.sem_inc(m["f_hi"], 1)
                    act.sem_inc(m["down_ps"], 1)
                with act.Fori(0, L) as layer:
                    n0 = 8 * layer

                    def weights_hi(j):
                        if j == 4:
                            act.wait_ge(m["down_ps"], 2 * FC * layer + FS)
                        act.wait_ge(w_in[j % WS], 16 * len(range(j % WS, 10, WS)) * layer + 16 * (j // WS) + 16)
                        nc.scalar.activation(matrices[j // 2][:, 0, :, j % 2 * 256:(j % 2 + 1) * 256], wraw[j % WS][:, :, :], ACT.Copy).then_inc(m["w_hi"], 1)

                    def scale_columns(dst, name, bk, turned, value, done):
                        act.wait_ge(turned, value)
                        for c in range(DC):
                            nc.scalar.activation(dst[:, c, :], bk[:, c * P:(c + 1) * P], ACT.Identity, scale=lnv[:, name, 0, c:c + 1],
                                                 bias=lnv[:, name, 1, c:c + 1]).then_inc(done, 1)

                    def norm_hi(n, k, bk=bank[6]):
                        scale_columns(xf[0], 0, bk, m["x_turned"], n + 1, m["xf_ok"])
                        act.wait_ge(m["xf_ok"], DC * (n + 1))
                        nc.scalar.activation(xn[k][:, 0, :, :], xf[0][:, :, :], ACT.Copy).then_inc(m["xn_hi"], 1)

                    weights_hi(0)
                    weights_hi(1)
                    act.wait_ge(m["cleared"], 1)
                    act.wait_ge(m["gn_in"], 32 * layer + 32)
                    norm_hi(n0, 0, bank[2])

                    def turned_hi(dst, bk, rows=slice(0, P)):
                        return nc.scalar.activation(dst, bk[rows, :].rearrange("p (c n) -> p c n", c=DC), ACT.Copy)

                    def body(it, first, last):
                        for k in range(2):
                            n = n0 + 2 * it + k
                            begin, end = first and k == 0, last and k == 1
                            if begin:
                                for j in range(2, 8):
                                    weights_hi(j)
                            if not end:
                                norm_hi(n + 1, 1 - k)
                            if begin:
                                for j in range(8, 10):
                                    weights_hi(j)
                            act.wait_ge(m["v_ps"], n + 1)
                            nc.scalar.activation(vv[:, 0, :], bank[2][:, :], ACT.Copy).then_inc(m["v_hi"], 1)
                            act.wait_ge(m["g_ps"], n + 1)
                            if not begin:
                                act.wait_ge(m["sws_ok"], 2 * n)
                            nc.scalar.activation(sw[:, :], bank[3][:, :], ACT.Silu).then_inc(m["sw_ok"], 1)
                            act.wait_ge(m["qk_turned"], 2 * n + 1)
                            for i, rows in enumerate(PAIR):
                                turned_hi(qd[rows, 0, :, i, :], bank[4], rows).then_inc(m["qkT_hi"], 1)
                            act.wait_ge(m["qk_turned"], 2 * n + 2)
                            turned_hi(kT[:, 0, :, :], bank[5]).then_inc(m["qkT_hi"], 1)
                            if not begin:
                                act.wait_ge(m["y_turned"], n)
                                turned_hi(yT[:, 0, :, :], bank[6]).then_inc(m["yT_hi"], 1)
                            for j in range(2):
                                act.wait_ge(m["pf_ok"], 2 * n + j + 1)
                                nc.scalar.activation(p_hl[:, 0, j, :, :], pf[:, j, :, :], ACT.Copy).then_inc(m["p_hi"], 1)
                    pairs(act, body)
                    def weights2_hi(k, n):
                        act.wait_ge(m["down_ps"], n + 1)
                        act.wait_ge(f_in[k], 16 // FS * (n - k) + 16)
                        nc.scalar.activation(fw[k][:, 0, :], fraw[k][:, :], ACT.Copy).then_inc(m["f_hi"], 1)

                    def norm2_hi(t):
                        n = n0 + t
                        if t >= 2:
                            act.wait_ge(m["x2_lo"], n - 1)
                        scale_columns(xf[t % 2], 1, bank[X2_BANK[t]], m["x2_turned"], n + 1, m["xf2_ok"])
                        act.wait_ge(m["xf2_ok"], DC * (n + 1))
                        nc.scalar.activation(x2T[:, 0, :, t * P:(t + 1) * P], xf[t % 2][:, :, :], ACT.Copy).then_inc(m["x2_hi"], 1)
                    norm2_hi(0)
                    norm2_hi(1)
                    norm2_hi(2)
                    norm2_hi(3)
                    act.wait_ge(m["g_ps"], n0 + 8)
                    weights2_hi(0, 2 * FC * layer)
                    act.wait_ge(m["y_turned"], n0 + 8)
                    turned_hi(yT[:, 0, :, :], bank[6]).then_inc(m["yT_hi"], 1)
                    weights2_hi(1, 2 * FC * layer + 1)
                    norm2_hi(4)
                    norm2_hi(5)

                    def hidden_hi(k, n):
                        act.wait_ge(m["up_ps"], n + 1)
                        nc.scalar.activation(hh[k % 2][:, 0, :], bank[k % 2][:, :], ACT.Gelu_apprx_tanh).then_inc(m["h_hi"], 1)
                        nc.scalar.activation(hf32[k % 2][:, :], bank[k % 2][:, :], ACT.Gelu_apprx_tanh).then_inc(m["h_ok"], 1)
                    act.wait_ge(m["wo_ps"], n0 + 8)
                    for k in range(FS):
                        hidden_hi(k, 2 * FC * layer + k)
                        weights2_hi((k + 2) % FS, 2 * FC * layer + k + 2)
                        if k in (1, 2):
                            norm2_hi(5 + k)
                    with act.Fori(1, 2 * FC // FS - 1) as it:
                        for k in range(FS):
                            n = 2 * FC * layer + FS * it + k
                            hidden_hi(k, n)
                            weights2_hi((k + 2) % FS, n + 2)
                    for k in range(FS):
                        n = 2 * FC * layer + 2 * FC - FS + k
                        hidden_hi(k, n)
                        if k < 2:
                            weights2_hi(k + 2, n + 2)

            @block.vector
            def _(dve):
                dve.sem_inc(m["ffn_ok"], 1)
                dve.sem_inc(m["res_ok"], 1)
                for _ in range(FS):
                    dve.sem_inc(m["f_lo"], 1)
                for t in range(NT):
                    nc.vector.bn_aggr(mv[:, t, :], x1_stats[:, t, :]).then_inc(m["ln0_ag"], 1)
                dve.wait_ge(m["ln0_ag"], NT)
                nc.vector.tensor_scalar(veps[:, :], mv[:, :, 1], 1e-5, None, ALU.add).then_inc(m["ln0_ve"], 1)
                dve.wait_ge(m["ln0_rs"], 1)

                def normalise(t):
                    nc.vector.tensor_scalar(A[:, t, :], X[:, t, :], mv[:, t, 0:1], rstd[:, t:t + 1], ALU.subtract, ALU.mult).then_inc(m["a0_ok"], 1)

                def norm_stats(n, t):
                    nc.vector.bn_stats(stats[:, 0, :], tile_of(A, t)).then_inc(m["st_ok"], 1)
                    wait_alone(dve, m["st_ok"], n + 1)
                    nc.vector.bn_aggr(mv[:, 0, :], stats[:, 0, :]).then_inc(m["ag_ok"], 1)
                    dve.wait_ge(m["ag_ok"], n + 1)
                    nc.vector.tensor_scalar(veps[:, 0:1], mv[:, 0, 1:2], 1e-6, None, ALU.add).then_inc(m["ve_ok"], 1)

                def norm_apply(n, t):
                    dve.wait_ge(m["rs_ok"], n + 1)
                    nc.vector.tensor_scalar(xh[0][:, :], tile_of(A, t), mv[:, 0, 0:1], rstd[:, 0:1], ALU.subtract, ALU.mult).then_inc(m["xh_ok"], 1)

                normalise(0)
                dve.wait_ge(m["a0_ok"], 1)
                norm_stats(0, 0)
                for t in range(1, NT):
                    normalise(t)
                norm_apply(0, 0)
                dve.wait_ge(m["a0_ok"], NT)
                dve.wait_ge(m["tab_in"], 32)
                with dve.Fori(0, L) as layer:
                    n0 = 8 * layer

                    def weights_lo(j):
                        dve.wait_ge(m["w_hi"], 10 * layer + j + 1)
                        w, cols = matrices[j // 2], slice(j % 2 * 256, (j % 2 + 1) * 256)
                        nc.vector.tensor_tensor(w[:, 1, :, cols], wraw[j % WS][:, :, :], r(w[:, 0, :, cols]), ALU.subtract).then_inc(m["w_lo"], 1)

                    def norm_lo(n, k):
                        dve.wait_ge(m["xn_hi"], n + 1)
                        nc.vector.tensor_tensor(xn[k][:, 1, :, :], xf[0][:, :, :], r(xn[k][:, 0, :, :]), ALU.subtract).then_inc(m["xn_lo"], 1)

                    weights_lo(0)
                    norm_lo(n0, 0)
                    weights_lo(1)

                    def rotate(n, j):
                        dve.wait_ge(m["q_ps" if j == 0 else "k_ps"], n + 1)
                        src = bank[j][:, :].rearrange("p (g e) -> p g e", e=E // 2)
                        for z, w in ((rc, 2 * j), (rs, 2 * j + 1)):
                            nc.vector.tensor_tensor(z[:, j, :].rearrange("p (g e) -> p g e", e=E // 2), src,
                                                    rot[:, w:w + 1, :].broadcast_to([P, 2 * H, E // 2]), ALU.mult).then_inc(m["rc_ok"], 1)

                    def group_norm(n):
                        dve.wait_ge(m["o_ps"], n)
                        for h in range(H):
                            nc.vector.bn_stats(gst[:, h, :], bank[7][:, h * E:(h + 1) * E]).then_inc(m["gst_ok"], 1)
                        wait_alone(dve, m["gst_ok"], H * n)
                        for h in range(H):
                            nc.vector.bn_aggr(gmv[:, h, :], gst[:, h, :]).then_inc(m["gmv_ok"], 1)
                        dve.wait_ge(m["gmv_ok"], H * n)
                        nc.vector.tensor_scalar(gve[:, :], gmv[:, :, 1], 1e-6, None, ALU.add).then_inc(m["gve_ok"], 1)
                        heads = lambda z: z.rearrange("p (h e) -> p h e", e=E)
                        nc.vector.tensor_tensor(heads(y[:, :]), heads(bank[7][:, :]), gmv[:, :, 0:1].broadcast_to([P, H, E]), ALU.subtract).then_inc(m["cen_ok"], 1)
                        dve.wait_ge(m["grs_ok"], n)
                        dve.wait_ge(m["cen_ok"], n)
                        nc.vector.tensor_tensor(heads(y[:, :]), heads(y[:, :]), grs[:, :].unsqueeze(2).broadcast_to([P, H, E]), ALU.mult).then_inc(m["hn_ok"], 1)
                        dve.wait_ge(m["sws_ok"], 2 * n)
                        dve.wait_ge(m["hn_ok"], n)
                        nc.vector.tensor_tensor(y[:, :], y[:, :], sws[:, 0, :], ALU.mult).then_inc(m["ya_ok"], 1)
                        dve.wait_ge(m["ya_ok"], n)
                        nc.vector.tensor_tensor(y[:, :], y[:, :], sws[:, 1, :], ALU.add).then_inc(m["y_ok"], 1)

                    def turned_lo(dst, bk, hi, rows=slice(0, P)):
                        return nc.vector.tensor_tensor(dst, bk[rows, :].rearrange("p (c n) -> p c n", c=DC), r(hi), ALU.subtract)

                    def residual(n, t, bk=bank[0]):
                        dve.wait_ge(m["wo_ps"], n + 1)
                        nc.vector.tensor_tensor(tile_of(A, t), bk[:, :], tile_of(A, t), ALU.add).then_inc(m["res_ok"], 1)
                        wait_alone(dve, m["res_ok"], n + 2)
                        nc.vector.bn_stats(tile_of(stats2, t), tile_of(A, t)).then_inc(m["st2_ok"], 1)

                    def norm2_aggregate(tiles):
                        wait_alone(dve, m["st2_ok"], n0 + tiles.stop)
                        for t in tiles:
                            nc.vector.bn_aggr(mv[:, t, :], stats2[:, t, :]).then_inc(m["ag2_ok"], 1)
                        dve.wait_ge(m["ag2_ok"], n0 + tiles.stop)
                        nc.vector.tensor_scalar(veps[:, tiles.start:tiles.stop], mv[:, tiles.start:tiles.stop, 1], 1e-6, None, ALU.add).then_inc(m["ve2_ok"], 1)

                    def body(it, first, last):
                        for k in range(2):
                            t = 2 * it + k
                            n = n0 + t
                            begin, end = first and k == 0, last and k == 1
                            if begin:
                                for j in range(2, 4):
                                    weights_lo(j)
                            if not end:
                                norm_stats(n + 1, t + 1)
                            if begin:
                                weights_lo(4)
                                norm_apply(n + 1, t + 1)
                            rotate(n, 0)
                            if begin:
                                weights_lo(5)
                            rotate(n, 1)
                            if not (begin or end):
                                norm_apply(n + 1, t + 1)
                            if begin:
                                for j in range(6, 8):
                                    weights_lo(j)
                                norm_lo(n + 1, 1 - k)
                                for j in range(8, 10):
                                    weights_lo(j)
                            if not begin:
                                group_norm(n)
                            dve.wait_ge(m["v_hi"], n + 1)
                            nc.vector.tensor_tensor(vv[:, 1, :], bank[2][:, :], r(vv[:, 0, :]), ALU.subtract).then_inc(m["v_lo"], 1)
                            if not (begin or end):
                                norm_lo(n + 1, 1 - k)
                            for i, rows in enumerate(PAIR):
                                dve.wait_ge(m["qkT_hi"], 3 * n + i + 1)
                                turned_lo(qd[rows, 1, :, i, :], bank[4], qd[rows, 0, :, i, :], rows).then_inc(m["qkT_lo"], 1)
                            dve.wait_ge(m["qkT_hi"], 3 * n + 3)
                            turned_lo(kT[:, 1, :, :], bank[5], kT[:, 0, :, :]).then_inc(m["qkT_lo"], 1)
                            if not first:
                                residual(n - 2, t - 2)
                            if not begin:
                                dve.wait_ge(m["yT_hi"], n)
                                turned_lo(yT[:, 1, :, :], bank[6], yT[:, 0, :, :]).then_inc(m["yT_lo"], 1)
                            if end:
                                norm2_aggregate(range(0, EARLY))
                            dve.wait_ge(m["s_ps"], n + 1)
                            if not begin:
                                dve.wait_ge(m["p_lo"], 2 * n)
                            for j in range(2):
                                nc.vector.tensor_tensor(pf[:, j, :, :], bank[2 + j][:, :].rearrange("p (c n) -> p c n", c=DC),
                                                        decay[:, j, :, :], ALU.mult).then_inc(m["pf_ok"], 1)
                    pairs(dve, body)

                    def norm2_apply(t):
                        dve.wait_ge(m["rs2_ok"], 2 * layer + 1 + (t >= EARLY))
                        if t >= 2:
                            dve.wait_ge(m["x2_turned"], n0 + t - 1)
                        else:
                            dve.wait_ge(m["x_turned"], n0 + 8)
                        nc.vector.tensor_scalar(xh[t % 2][:, :], A[:, t, :], mv[:, t, 0:1], rstd[:, t:t + 1], ALU.subtract, ALU.mult).then_inc(m["xh2_ok"], 1)

                    def norm2_lo(t):
                        dve.wait_ge(m["x2_hi"], n0 + t + 1)
                        cols = slice(t * P, (t + 1) * P)
                        nc.vector.tensor_tensor(x2T[:, 1, :, cols], xf[t % 2][:, :, :], r(x2T[:, 0, :, cols]), ALU.subtract).then_inc(m["x2_lo"], 1)

                    def weights2_lo(k, n):
                        dve.wait_ge(m["f_hi"], n + FS + 1)
                        nc.vector.tensor_tensor(fw[k][:, 1, :], fraw[k][:, :], r(fw[k][:, 0, :]), ALU.subtract).then_inc(m["f_lo"], 1)

                    norm2_apply(0)
                    norm2_apply(1)
                    norm2_lo(0)
                    norm2_apply(2)
                    norm2_lo(1)
                    norm2_apply(3)
                    group_norm(n0 + 8)
                    residual(n0 + 6, 6)
                    norm2_lo(2)
                    norm2_lo(3)
                    weights2_lo(0, 2 * FC * layer)
                    norm2_apply(4)
                    norm2_apply(5)
                    dve.wait_ge(m["yT_hi"], n0 + 8)
                    turned_lo(yT[:, 1, :, :], bank[6], yT[:, 0, :, :]).then_inc(m["yT_lo"], 1)
                    weights2_lo(1, 2 * FC * layer + 1)
                    norm2_lo(4)
                    residual(n0 + 7, 7, bank[7])
                    norm2_aggregate(range(EARLY, NT))
                    norm2_lo(5)
                    norm2_apply(6)
                    norm2_apply(7)

                    def chunks(n, ahead=True, tiles=False):
                        for k in range(FS):
                            dve.wait_ge(m["h_ok"], n + k + 1)
                            nc.vector.tensor_tensor(hh[k % 2][:, 1, :], hf32[k % 2][:, :], r(hh[k % 2][:, 0, :]), ALU.subtract).then_inc(m["h_lo"], 1)
                            if ahead or k < 2:
                                weights2_lo((k + 2) % FS, n + k + 2)
                            if tiles and k in (1, 2):
                                norm2_lo(5 + k)

                    for half in range(2):
                        b = 2 * FC * layer + FC * half
                        if half == 0:
                            chunks(b, tiles=True)
                        with dve.Fori(1 - half, FC // FS - half) as it:
                            chunks(b + FS * it)
                        if half == 1:
                            chunks(b + FC - FS, False)
                            norm_stats(n0 + 8, 0)
                            dve.wait_ge(m["x2_turned"], n0 + 8)
                            norm_apply(n0 + 8, 0)
                        dve.wait_ge(m["down_ps"], b + FC + FS)
                        for j in range(4):
                            nc.vector.tensor_tensor(A[:, 4 * half + j, :], bank[4 + j][:, :], A[:, 4 * half + j, :], ALU.add).then_inc(m["ffn_ok"], 1)
                    dve.wait_ge(m["ffn_ok"], n0 + 9)

            @block.tensor
            def _(pe):
                with pe.Fori(0, L) as layer:
                    n0 = 8 * layer

                    def turn(src, bk):
                        for c in range(DC):
                            last = nc.tensor.transpose(bk[:, c * P:(c + 1) * P], src[:, c * P:(c + 1) * P], ident[:, :])
                        return last

                    def project(which, bk, k):
                        return products(nc, bk[:, :], range(DC), lambda c, h: xn[k][:, h, c, :],
                                        lambda c, h: matrices[which][:, h, c, :])

                    def apply_scores(n):
                        pe.wait_ge(m["p_lo"], 2 * n)
                        pe.wait_ge(m["v_lo"], n)
                        for h in range(H):
                            last = products(nc, bank[7][:, h * E:(h + 1) * E], range(1), lambda _, i: p_hl[:, i, h // 4, h % 4, :],
                                            lambda _, i: vv[:, i, h * E:(h + 1) * E])
                        last.then_inc(m["o_ps"], 1)

                    def project_out(n, bk=bank[0]):
                        pe.wait_ge(m["yT_lo"], n)
                        products(nc, bk[:, :], range(DC), lambda c, h: yT[:, h, c, :],
                                 lambda c, h: wo[:, h, c, :]).then_inc(m["wo_ps"], 1)

                    pe.wait_ge(m["xh_ok"], n0 + 1)
                    turn(xh[0], bank[2]).then_inc(m["x_turned"], 1)

                    def body(it, first, last):
                        for k in range(2):
                            n = n0 + 2 * it + k
                            begin, end = first and k == 0, last and k == 1
                            pe.wait_ge(m["xn_lo"], n + 1)
                            if begin:
                                pe.wait_ge(m["w_lo"], 10 * layer + 2)
                            elif first:
                                pe.wait_ge(m["rc_ok"], 4 * n - 2)
                            else:
                                pe.wait_ge(m["res_ok"], n - 1)
                            project(0, bank[0], k).then_inc(m["q_ps"], 1)
                            if begin:
                                pe.wait_ge(m["w_lo"], 10 * layer + 4)
                            else:
                                pe.wait_ge(m["rc_ok"], 4 * n)
                            project(1, bank[1], k).then_inc(m["k_ps"], 1)
                            if not begin:
                                apply_scores(n)
                            if not end:
                                if not first:
                                    pe.wait_ge(m["yT_lo"], n - 1)
                                elif k == 1:
                                    pe.wait_ge(m["xf_ok"], DC * (n + 1))
                                pe.wait_ge(m["xh_ok"], n + 2)
                                turn(xh[0], bank[6]).then_inc(m["x_turned"], 1)
                            if not begin:
                                pe.wait_ge(m["pf_ok"], 2 * n)
                            else:
                                pe.wait_ge(m["w_lo"], 10 * layer + 6)
                            project(2, bank[2], k).then_inc(m["v_ps"], 1)
                            if begin:
                                pe.wait_ge(m["w_lo"], 10 * layer + 8)
                            project(3, bank[3], k).then_inc(m["g_ps"], 1)
                            for j in range(2):
                                pe.wait_ge(m["qk_ok"], 4 * n + 2 * j + 2)
                                turn(qk[:, j, :], bank[4 + j]).then_inc(m["qk_turned"], 1)
                            if not first:
                                pe.wait_ge(m["rc_ok"], 4 * n + 2)
                                project_out(n - 1)
                            if not begin:
                                pe.wait_ge(m["y_ok"], n)
                                if not end:
                                    pe.wait_ge(m["xf_ok"], DC * (n + 2))
                                turn(y, bank[6]).then_inc(m["y_turned"], 1)
                            if first and k == 1:
                                pe.wait_ge(m["w_lo"], 10 * layer + 10)
                            pe.wait_ge(m["qkT_lo"], 3 * n + 3)
                            pe.wait_ge(m["v_lo"], n + 1)
                            pe.wait_ge(m["sw_ok"], n + 1)
                            for c in range(DC):
                                last_mm = products(nc, bank[2 + c // 2][:, c % 2 * 2 * P:(c % 2 + 1) * 2 * P], range(1), lambda _, i: kT[:, i, c, :],
                                                   lambda _, i: qd[:, i, c, :, :].rearrange("p h n -> p (h n)"))
                            last_mm.then_inc(m["s_ps"], 1)
                    pairs(pe, body)

                    def turn2(t):
                        pe.wait_ge(m["xh2_ok"], n0 + t + 1)
                        if t >= 5:
                            before = {5: 1, 6: 2, 7: 5}[t]
                            pe.wait_ge(m["xf2_ok"], DC * (n0 + before + 1))
                        turn(xh[t % 2], bank[X2_BANK[t]]).then_inc(m["x2_turned"], 1)
                    def up(n, k, half):
                        pe.wait_ge(m["f_lo"], n + FS + 1)
                        products(nc, bank[k % 2][:, :], range(DC), lambda c, h: fw[k][:, h, c * P:(c + 1) * P],
                                 lambda c, h: x2T[:, h, c, half * 512:(half + 1) * 512]).then_inc(m["up_ps"], 1)

                    def down(n, k, start, stop):
                        pe.wait_ge(m["h_lo"], n + 1)
                        for j in range(4):
                            for i, (x, w) in enumerate(PARTS):
                                last = nc.tensor.matmul(bank[4 + j][:, :], hh[k % 2][:, x, j * P:(j + 1) * P], fw[k][:, w, D:2 * D],
                                                        start=start and i == 0, stop=stop and i == 2)
                        last.then_inc(m["down_ps"], 1)

                    def chunks(n, half, begin=False, end=False):
                        for k in range(FS):
                            if begin and half == 0 and k == 0:
                                pass
                            elif not (end and k == FS - 1):
                                up(n + k + 1, (k + 1) % FS, half)
                            elif half == 0:
                                pe.wait_ge(m["x2_lo"], n0 + NT)
                                up(n + k + 1, 0, 1)
                            if begin and half == 0 and k in (1, 2):
                                turn2(5 + k)
                            if begin and half == 1 and k == 0:
                                pe.wait_ge(m["ffn_ok"], n0 + 4 + 1)
                            down(n + k, k, begin and k == 0, end and k == FS - 1)

                    turn2(0)
                    turn2(1)
                    apply_scores(n0 + 8)
                    turn2(2)
                    turn2(3)
                    project_out(n0 + 7)
                    pe.wait_ge(m["y_ok"], n0 + 8)
                    turn(y, bank[6]).then_inc(m["y_turned"], 1)
                    wait_alone(pe, m["x2_lo"], n0 + 4)
                    pe.wait_ge(m["res_ok"], n0 + 8)
                    up(2 * FC * layer, 0, 0)
                    turn2(4)
                    turn2(5)
                    project_out(n0 + 8, bank[7])
                    up(2 * FC * layer + 1, 1, 0)
                    pe.wait_ge(m["x2_lo"], n0 + 5)
                    pe.wait_ge(m["res_ok"], n0 + 9)
                    for half in range(2):
                        b = 2 * FC * layer + FC * half
                        chunks(b, half, begin=True)
                        with pe.Fori(1, FC // FS - 1) as it:
                            chunks(b + FS * it, half)
                        chunks(b + FC - FS, half, end=True)


def mixture(nc, a, out, whole, holder, sem, bank, X, A, ident, mhalf, xg, yg):
    with ExitStack() as phase:
        sb = holder(phase)
        slot = sb("slot", [P, 2, NT], I32)
        gate = sb("gate", [P, 2, NT])
        group_expert = sb("group_expert", [1, NG], I32)

        with ExitStack() as inner:
            sbi = holder(inner)
            tab = sbi("tab", [P, 2 * P + NE + NE * NE + NG])
            upper, ones = tab[:, 0:P], tab[:, P:2 * P]
            iota_e = tab[:, 2 * P:2 * P + NE]
            before = tab[:, 2 * P + NE:2 * P + NE + NE * NE].rearrange("p (e f) -> p e f", f=NE)
            iota_g = tab[:, 2 * P + NE + NE * NE:]
            rw = sbi("rw", [P, DC, NE])
            stats = sbi("m_stats", [P, NT, 6])
            mv = sbi("m_mv", [P, NT, 2])
            veps = sbi("m_veps", [P, NT])
            rstd = sbi("m_rstd", [P, NT])
            xr = [sbi(f"xr{i}", [P, D]) for i in range(3)]
            logits = sbi("logits", [P, NT, NE])
            top = sbi("top", [P, NT, NE])
            topi = sbi("topi", [P, NT, NE], U32)
            chosen = sbi("chosen", [P, 2, NT])
            diff = sbi("diff", [P, NT])
            odds = sbi("odds", [P, NT])
            sum1 = sbi("sum1", [P, NT])
            hot = sbi("hot", [P, 2, NT, NE])
            both = sbi("both", [P, NT, NE])
            cnt = sbi("cnt", [P, 2, NT, NE])
            cum = sbi("cum", [P, NT + 1, NE])
            groups = sbi("groups", [P, 5, NE])
            tri = sbi("tri", [P, NE, NE])
            gs = sbi("gs", [P, 3, NE])
            where = sbi("where", [P, 2, NT, NE])
            picked = sbi("picked", [P, 2, NT, NE])
            slotf = sbi("slotf", [P, 2, NT])
            ge = sbi("ge", [P, NG, NE])
            gsum = sbi("gsum", [P, NG])
            gmin = sbi("gmin", [P, NG])
            names = """tab_in x2_ok st_ok ag_ok ve_ok rs_ok xh_ok turned xr_ok logit_ps logit_ok top_ok topi_ok
                route odds_ok both_ok cnt_ps""".split()
            m = {n: sem("m_" + n) for n in names}
            with nc.Block() as block:
                @block.sync
                def _(sp):
                    sp.dma_start(tab[:, :], a["route_tab"]).then_inc(m["tab_in"], 16)
                    sp.dma_start(rw[:, :, :], a["rw"]).then_inc(m["tab_in"], 16)

                @block.gpsimd
                def _(pool):
                    for i in range(2):
                        pool.wait_ge(m["ve_ok"], i + 1)
                        half = slice(NT // 2 * i, NT // 2 * (i + 1))
                        nc.gpsimd.tensor_tensor(rstd[:, half], veps[:, half], mhalf[:, 0:NT // 2], ALU.pow).then_inc(m["rs_ok"], 1)

                @block.scalar
                def _(act):
                    for t in range(NT):
                        act.wait_ge(m["turned"], t + 1)
                        if t >= 3:
                            act.wait_ge(m["logit_ps"], t - 2)
                        nc.scalar.activation(xr[t % 3][:, :], bank[t % 3][:, :], ACT.Copy).then_inc(m["xr_ok"], 1)
                    act.wait_ge(m["route"], 2)
                    nc.scalar.activation(odds[:, :], diff[:, :], ACT.Exp).then_inc(m["odds_ok"], 1)

                @block.vector
                def _(dve):
                    tiles = (range(0, NT // 2), range(NT // 2, NT))

                    def add(i):
                        for t in tiles[i]:
                            nc.vector.tensor_tensor(X[:, t, :], X[:, t, :], A[:, t, :], ALU.add).then_inc(m["x2_ok"], 1)

                    def statistics(i):
                        for t in tiles[i]:
                            dve.wait_ge(m["x2_ok"], t + 1)
                            nc.vector.bn_stats(stats[:, t, :], X[:, t, :]).then_inc(m["st_ok"], 1)
                        for t in tiles[i]:
                            dve.wait_ge(m["st_ok"], t + 1)
                            nc.vector.bn_aggr(mv[:, t, :], stats[:, t, :]).then_inc(m["ag_ok"], 1)
                        dve.wait_ge(m["ag_ok"], tiles[i].stop)
                        half = slice(tiles[i].start, tiles[i].stop)
                        nc.vector.tensor_scalar(veps[:, half], mv[:, half, 1], 1e-5, None, ALU.add).then_inc(m["ve_ok"], 1)

                    def normalise(i):
                        dve.wait_ge(m["rs_ok"], i + 1)
                        for t in tiles[i]:
                            nc.vector.tensor_scalar(A[:, t, :], X[:, t, :], mv[:, t, 0:1], rstd[:, t:t + 1], ALU.subtract, ALU.mult).then_inc(m["xh_ok"], 1)
                    add(0)
                    statistics(0)
                    add(1)
                    normalise(0)
                    statistics(1)
                    normalise(1)
                    dve.wait_ge(m["logit_ps"], NT)
                    nc.vector.tensor_copy(logits[:, :, :], bank[4][:, 0:NT * NE].rearrange("p (t e) -> p t e", e=NE)).then_inc(m["logit_ok"], 1)
                    dve.wait_ge(m["logit_ok"], 1)
                    for t in range(NT):
                        nc.vector.max(top[:, t, :], logits[:, t, :]).then_inc(m["top_ok"], 1)
                    for t in range(NT):
                        dve.wait_ge(m["top_ok"], t + 1)
                        nc.vector.max_index(topi[:, t, :], top[:, t, :], logits[:, t, :]).then_inc(m["topi_ok"], 1)
                    step = [0]

                    def link(ins):
                        step[0] += 1
                        ins.then_inc(m["route"], 1)
                        dve.wait_ge(m["route"], step[0])
                    dve.wait_ge(m["topi_ok"], NT)
                    link(nc.vector.tensor_copy(chosen[:, :, :].rearrange("p k t -> p t k"), topi[:, :, 0:2]))
                    link(nc.vector.tensor_tensor(diff[:, :], top[:, :, 1], top[:, :, 0], ALU.subtract))
                    for k in range(2):
                        link(nc.vector.tensor_tensor(hot[:, k, :, :], chosen[:, k, :].unsqueeze(2).broadcast_to([P, NT, NE]),
                                                     iota_e.unsqueeze(1).broadcast_to([P, NT, NE]), ALU.is_equal))
                    nc.vector.tensor_tensor(both[:, :, :], hot[:, 0, :, :], hot[:, 1, :, :], ALU.add).then_inc(m["both_ok"], 1)
                    dve.wait_ge(m["odds_ok"], 1)
                    link(nc.vector.tensor_scalar(sum1[:, :], odds[:, :], 1.0, None, ALU.add))
                    link(nc.vector.reciprocal(gate[:, 0, :], sum1[:, :]))
                    link(nc.vector.tensor_tensor(gate[:, 1, :], gate[:, 0, :], odds[:, :], ALU.mult))
                    dve.wait_ge(m["cnt_ps"], 1)
                    link(nc.vector.tensor_copy(cnt[:, :, :, :].rearrange("p a t e -> p (a t e)"), bank[3][:, 0:2 * NT * NE]))
                    link(nc.vector.memset(cum[:, 0, :], 0.0))
                    for t in range(NT):
                        link(nc.vector.tensor_tensor(cum[:, t + 1, :], cum[:, t, :], cnt[:, 1, t, :], ALU.add))
                    link(nc.vector.tensor_scalar(groups[:, 0, :], cum[:, NT, :], 0.0, None, ALU.is_gt))
                    for j in range(1, TOK // GT):
                        link(nc.vector.scalar_tensor_tensor(groups[:, j, :], cum[:, NT, :], float(j * GT), groups[:, j - 1, :], ALU.is_gt, ALU.add))
                    per_expert = groups[:, TOK // GT - 1, :]
                    link(nc.vector.tensor_tensor(tri[:, :, :], before, per_expert.unsqueeze(1).broadcast_to([P, NE, NE]), ALU.mult))
                    link(nc.vector.tensor_reduce(gs[:, 0, :], tri[:, :, :], AX.X, ALU.add))
                    link(nc.vector.tensor_tensor(gs[:, 1, :], gs[:, 0, :], per_expert, ALU.add))
                    link(nc.vector.tensor_scalar(gs[:, 2, :], gs[:, 0, :], float(GT), None, ALU.mult))
                    link(nc.vector.tensor_tensor(where[:, 0, :, :], cnt[:, 0, :, :], cum[:, 0:NT, :], ALU.add))
                    link(nc.vector.tensor_tensor(where[:, 1, :, :], where[:, 0, :, :], gs[:, 2, :].unsqueeze(1).broadcast_to([P, NT, NE]), ALU.add))
                    for k in range(2):
                        link(nc.vector.tensor_tensor(picked[:, k, :, :], hot[:, k, :, :], where[:, 1, :, :], ALU.mult))
                    link(nc.vector.tensor_reduce(slotf[:, :, :], picked[:, :, :, :], AX.X, ALU.add))
                    link(nc.vector.tensor_copy(slot[:, :, :], slotf[:, :, :]))
                    link(nc.vector.tensor_tensor(ge[:, :, :], gs[:, 1, :].unsqueeze(1).broadcast_to([P, NG, NE]),
                                                 iota_g.unsqueeze(2).broadcast_to([P, NG, NE]), ALU.is_le))
                    link(nc.vector.tensor_reduce(gsum[:, :], ge[:, :, :], AX.X, ALU.add))
                    link(nc.vector.tensor_scalar(gmin[:, :], gsum[:, :], float(NE - 1), None, ALU.min))
                    link(nc.vector.tensor_copy(group_expert[:, :], gmin[0:1, :]))

                @block.tensor
                def _(pe):
                    def score(t):
                        pe.wait_ge(m["xr_ok"], t + 1)
                        for c in range(DC):
                            last = nc.tensor.matmul(bank[4][:, t * NE:(t + 1) * NE], xr[t % 3][:, c * P:(c + 1) * P], rw[:, c, :],
                                                    start=c == 0, stop=c == DC - 1)
                        last.then_inc(m["logit_ps"], 1)
                    pe.wait_ge(m["tab_in"], 32)
                    for t in range(NT):
                        pe.wait_ge(m["xh_ok"], t + 1)
                        if t >= 3:
                            pe.wait_ge(m["xr_ok"], t - 2)
                        for c in range(DC):
                            last = nc.tensor.transpose(bank[t % 3][:, c * P:(c + 1) * P], A[:, t, c * P:(c + 1) * P], ident[:, :])
                        last.then_inc(m["turned"], 1)
                        if t >= 2:
                            score(t - 2)
                    score(NT - 2)
                    score(NT - 1)
                    pe.wait_ge(m["both_ok"], 1)
                    flat = both[:, :, :].rearrange("p t e -> p (t e)")
                    nc.tensor.matmul(bank[3][:, 0:NT * NE], upper, flat, start=True, stop=True)
                    nc.tensor.matmul(bank[3][:, NT * NE:2 * NT * NE], ones, flat, start=True, stop=True).then_inc(m["cnt_ps"], 1)

        with ExitStack() as inner:
            sbi = holder(inner)
            xin = sbi("xin", [P, 2, D])
            xT = sbi("e_xT", [P, 2, DC, GT], F32R)
            raw = [sbi(f"e_raw{i}", [P, DC, 512]) for i in range(3)]
            w = [sbi(f"e_w{i}", [P, 2, DC, 512], F32R) for i in range(3)]
            si = sbi("si", [P, 2, 512])
            hid = sbi("hid", [P, 2, 512])
            hT = [sbi(f"e_hT{i}", [P, 2, DC, GT], F32R) for i in range(2)]
            yb = sbi("yb", [P, 2, D])
            names = """scattered x_in x_turned x_hi x_lo w_hi w_lo step_ps si_ok hid_ok h_hi h_lo y_ok y_out""".split()
            m = {n: sem("e_" + n) for n in names}
            w_in = [sem(f"e_w_in{i}") for i in range(3)]
            G0, D1, U0, G1, U1, D0 = range(6)
            PIECE_AT = {G0: 0, U0: 1, G1: 2, U1: 3, D0: 4, D1: 5}

            def count(g, pos):
                if isinstance(g, int) and g == 0 and pos == G0:
                    return 1
                if isinstance(g, int) and g == NG:
                    return PIECES * NG
                return PIECES * g + pos

            def slot_before(g, pos):
                if isinstance(g, int) and g == 0:
                    return {G0: None, U0: None, G1: 1, U1: None, D0: 2}[pos]
                if isinstance(g, int) and g == NG:
                    return count(NG - 1, U1)
                return count(g, pos) - 3

            with nc.Block() as block:
                @block.sync
                def _(sp):
                    x_v = xg.rearrange("(g t p) d -> g p t d", p=P, t=2)

                    def load(g, pos, expert):
                        n = slot_before(g, pos)
                        if n is not None:
                            sp.wait_ge(m["w_hi"], n)
                            sp.wait_ge(m["w_lo"], n)
                        sp.dma_start(raw[pos % 3][:, :, :], a["we"][bass.ds(expert, 1), PIECE_AT[pos], :, :]
                                     .rearrange("o p (c n) -> p (o c) n", c=DC)).then_inc(w_in[pos % 3], 16)

                    def load_x(g):
                        sp.dma_start(xin[:, :, :], x_v[bass.ds(g, 1), :, :, :].rearrange("o p t d -> p (o t) d")).then_inc(m["x_in"], 16)

                    def body(g, first):
                        expert = sp.value_load(group_expert[0:1, bass.ds(g, 1)], min_val=0, max_val=NE - 1)
                        load(g, G0, expert)
                        if first:
                            load(g, U0, expert)
                            sp.wait_ge(m["scattered"], 16 * 2 * NT)
                            load_x(0)
                            for pos in (G1, U1, D0):
                                load(g, pos, expert)
                            return
                        if not first:
                            before = sp.value_load(group_expert[0:1, bass.ds(g - 1, 1)], min_val=0, max_val=NE - 1)
                            load(g, D1, before)
                        for pos in (U0, G1, U1, D0):
                            load(g, pos, expert)
                    body(0, True)
                    with sp.Fori(1, NG) as g:
                        sp.wait_ge(m["x_turned"], g)
                        load_x(g)
                        body(g, False)
                    last = sp.value_load(group_expert[0:1, NG - 1:NG], min_val=0, max_val=NE - 1)
                    load(NG, D1, last)

                @block.gpsimd
                def _(pool):
                    for t in range(NT):
                        for k in range(2):
                            nc.gpsimd.indirect_dma_start(out=xg[:, :], out_offset=bass.IndirectOffsetOnAxis(ap=slot[:, k, t:t + 1], axis=0),
                                                         in_=A[:, t, :], in_offset=None).then_inc(m["scattered"], 16)
                    pool.wait_ge(m["scattered"], 16 * 2 * NT)

                @block.scalar
                def _(act):
                    y_v = yg.rearrange("(g t p) d -> g p t d", p=P, t=2)

                    def split_hi(g, pos):
                        n = slot_before(g, pos)
                        if isinstance(g, int) and g == NG:
                            loads = 2 * NG
                        else:
                            loads = {G0: 2 * g + 1, G1: 2 * g + 2, U0: 2 * g + 1, D0: 2 * g + 2, D1: 2 * g, U1: 2 * g + 1}[pos]
                        act.wait_ge(w_in[pos % 3], 16 * loads)
                        if n is not None:
                            act.wait_ge(m["step_ps"], n)
                        nc.scalar.activation(w[pos % 3][:, 0, :, :], raw[pos % 3][:, :, :], ACT.Copy).then_inc(m["w_hi"], 1)

                    def silu(g, j):
                        act.wait_ge(m["step_ps"], count(g, G0 if j == 0 else G1))
                        if not (isinstance(g, int) and g == 0 and j == 0):
                            act.wait_ge(m["hid_ok"], 4 * g + 2 * j)
                        for t in range(2):
                            nc.scalar.activation(si[:, t, :], bank[t][:, :], ACT.Silu).then_inc(m["si_ok"], 1)

                    def hidden_hi(g, j):
                        for t in range(2):
                            act.wait_ge(m["hid_ok"], 4 * g + 2 * j + t + 1)
                            nc.scalar.activation(hT[j][:, 0, 2 * t:2 * t + 2, :], hid[:, t, :].rearrange("p (c n) -> p c n", n=GT), ACT.Copy).then_inc(m["h_hi"], 1)

                    def x_hi(g):
                        for t in range(2):
                            act.wait_ge(m["x_turned"], g + 1)
                            nc.scalar.activation(xT[:, 0, :, t * P:(t + 1) * P], bank[6 + t][:, :].rearrange("p (c n) -> p c n", c=DC), ACT.Copy).then_inc(m["x_hi"], 1)

                    def store(g, n, first):
                        act.wait_ge(m["step_ps"], n)
                        if not first:
                            act.wait_ge(m["y_out"], 16 * g)
                        for t in range(2):
                            nc.scalar.activation(yb[:, t, :], bank[4 + t][:, :], ACT.Copy).then_inc(m["y_ok"], 1)
                        act.wait_ge(m["y_ok"], 2 * g + 2)
                        act.dma_start(y_v[bass.ds(g, 1), :, :, :].rearrange("o p t d -> p (o t) d"), yb[:, :, :]).then_inc(m["y_out"], 16)

                    def body(g, first, second=False):
                        if not first:
                            hidden_hi(g - 1, 1)
                        split_hi(g, U0)
                        silu(g, 0)
                        split_hi(g, G1)
                        if not first:
                            store(g - 1, count(g, D1), second)
                        split_hi(g, U1)
                        split_hi(g, D0)
                        hidden_hi(g, 0)
                        silu(g, 1)
                    def tail(g):
                        split_hi(g + 1, G0)
                        x_hi(g + 1)
                        split_hi(g + 1, D1)
                    split_hi(0, G0)
                    x_hi(0)
                    body(0, True)
                    tail(0)
                    body(1, False, True)
                    tail(1)
                    with act.Fori(2, NG - 1) as g:
                        body(g, False)
                        tail(g)
                    body(NG - 1, False)
                    split_hi(NG, D1)
                    hidden_hi(NG - 1, 1)
                    store(NG - 1, PIECES * NG, False)
                    act.wait_ge(m["y_out"], 16 * NG)

                @block.vector
                def _(dve):
                    def split_lo(g, pos):
                        dve.wait_ge(m["w_hi"], count(g, pos))
                        nc.vector.tensor_tensor(w[pos % 3][:, 1, :, :], raw[pos % 3][:, :, :], r(w[pos % 3][:, 0, :, :]), ALU.subtract).then_inc(m["w_lo"], 1)

                    def hidden(g, j):
                        if not (isinstance(g, int) and g == 0 and j == 0):
                            dve.wait_ge(m["h_lo"], 4 * g + 2 * j)
                        dve.wait_ge(m["step_ps"], count(g, U0 if j == 0 else U1))
                        for t in range(2):
                            dve.wait_ge(m["si_ok"], 4 * g + 2 * j + t + 1)
                            nc.vector.tensor_tensor(hid[:, t, :], bank[2 + t][:, :], si[:, t, :], ALU.mult).then_inc(m["hid_ok"], 1)

                    def hidden_lo(g, j):
                        for t in range(2):
                            dve.wait_ge(m["h_hi"], 4 * g + 2 * j + t + 1)
                            nc.vector.tensor_tensor(hT[j][:, 1, 2 * t:2 * t + 2, :], hid[:, t, :].rearrange("p (c n) -> p c n", n=GT),
                                                    r(hT[j][:, 0, 2 * t:2 * t + 2, :]), ALU.subtract).then_inc(m["h_lo"], 1)

                    def x_lo(g):
                        for t in range(2):
                            dve.wait_ge(m["x_hi"], 2 * g + t + 1)
                            nc.vector.tensor_tensor(xT[:, 1, :, t * P:(t + 1) * P], bank[6 + t][:, :].rearrange("p (c n) -> p c n", c=DC),
                                                    r(xT[:, 0, :, t * P:(t + 1) * P]), ALU.subtract).then_inc(m["x_lo"], 1)

                    def body(g, first):
                        if not first:
                            hidden_lo(g - 1, 1)
                        split_lo(g, U0)
                        split_lo(g, G1)
                        split_lo(g, U1)
                        hidden(g, 0)
                        split_lo(g, D0)
                        hidden_lo(g, 0)

                    def tail(g):
                        split_lo(g + 1, G0)
                        x_lo(g + 1)
                        hidden(g, 1)
                        split_lo(g + 1, D1)
                    split_lo(0, G0)
                    x_lo(0)
                    body(0, True)
                    tail(0)
                    with dve.Fori(1, NG - 1) as g:
                        body(g, False)
                        tail(g)
                    body(NG - 1, False)
                    hidden(NG - 1, 1)
                    split_lo(NG, D1)
                    hidden_lo(NG - 1, 1)

                @block.tensor
                def _(pe):
                    def wide(g, pos, banks):
                        pe.wait_ge(m["w_lo"], count(g, pos))
                        for n in range(DC):
                            last = products(nc, bank[banks + n // 2][:, n % 2 * GT:(n % 2 + 1) * GT], range(DC),
                                            lambda c, h: w[pos % 3][:, h, c, n * P:(n + 1) * P], lambda c, h: xT[:, h, c, :])
                        last.then_inc(m["step_ps"], 1)

                    def down(n, pos, j):
                        pe.wait_ge(m["w_lo"], n)
                        for t in range(2):
                            for c in range(DC):
                                for i, (x, y) in enumerate(PARTS):
                                    last = nc.tensor.matmul(bank[4 + t][:, :], hT[j][:, x, c, t * P:(t + 1) * P], w[pos % 3][:, y, c, :],
                                                            start=j == 0 and c == 0 and i == 0, stop=j == 1 and c == DC - 1 and i == 2,
                                                            skip_group_check=False)
                        last.then_inc(m["step_ps"], 1)

                    def turn_x(g):
                        pe.wait_ge(m["x_in"], 16 * g + 16)
                        for t in range(2):
                            for c in range(DC):
                                last = nc.tensor.transpose(bank[6 + t][:, c * P:(c + 1) * P], xin[:, t, c * P:(c + 1) * P], ident[:, :])
                        last.then_inc(m["x_turned"], 1)

                    def body(g, first, last=False):
                        pe.wait_ge(m["x_lo"], 2 * g + 2)
                        wide(g, G0, 0)
                        if not first:
                            pe.wait_ge(m["h_lo"], 4 * g)
                            down(count(g, D1), D1, 1)
                        wide(g, U0, 2)
                        pe.wait_ge(m["si_ok"], 4 * g + 2)
                        wide(g, G1, 0)
                        pe.wait_ge(m["hid_ok"], 4 * g + 2)
                        wide(g, U1, 2)
                        if not last:
                            turn_x(g + 1)
                        if not first:
                            pe.wait_ge(m["y_ok"], 2 * g)
                        pe.wait_ge(m["h_lo"], 4 * g + 2)
                        down(count(g, D0), D0, 0)
                        pe.wait_ge(m["si_ok"], 4 * g + 4)
                    turn_x(0)
                    body(0, True)
                    with pe.Fori(1, NG - 1) as g:
                        body(g, False)
                    body(NG - 1, False, True)
                    pe.wait_ge(m["h_lo"], 4 * NG)
                    down(PIECES * NG, D1, 1)

        with ExitStack() as inner:
            sbi = holder(inner)
            rows = sbi("rows", [P, NT, 2, D])
            got = [sem(f"c_got{t}") for t in range(NT)]
            part, summed, stored = sem("c_part"), sem("c_summed"), sem("c_stored")
            with nc.Block() as block:
                @block.gpsimd
                def _(pool):
                    for t in range(NT):
                        for k in range(2):
                            nc.gpsimd.indirect_dma_start(out=rows[:, t, k, :], out_offset=None, in_=yg[:, :],
                                                         in_offset=bass.IndirectOffsetOnAxis(ap=slot[:, k, t:t + 1], axis=0)).then_inc(got[t], 16)

                @block.vector
                def _(dve):
                    for t in range(NT):
                        dve.wait_ge(got[t], 32)
                        nc.vector.scalar_tensor_tensor(X[:, t, :], rows[:, t, 0, :], gate[:, 0, t:t + 1], X[:, t, :], ALU.mult, ALU.add).then_inc(part, 1)
                        dve.wait_ge(part, t + 1)
                        nc.vector.scalar_tensor_tensor(X[:, t, :], rows[:, t, 1, :], gate[:, 1, t:t + 1], X[:, t, :], ALU.mult, ALU.add).then_inc(summed, 1)

                @block.sync
                def _(sp):
                    out_v = out.rearrange("(t p) d -> t p d", p=P)
                    for t in range(NT):
                        sp.wait_ge(summed, t + 1)
                        sp.dma_start(out_v[t, :, :], X[:, t, :]).then_inc(stored, 16)
                    sp.wait_ge(stored, 16 * NT)


def chunked(w):
    return np.ascontiguousarray(np.asarray(w).reshape(-1, P, w.shape[-1]).transpose(1, 0, 2))


def by_partition(v):
    return np.asarray(v).reshape(-1, P).T


def position_tables():
    f = np.float32
    base = (np.arange(0, E, 2, dtype=f) + f(0.4 * E)) / f(1.4 * E)
    pos = np.arange(S, dtype=f)
    scale = base[None, :] ** (pos[:, None] / f(256))
    angle = pos[:, None] * (f(1.0) / f(10000.0) ** (np.arange(E // 2, dtype=f) / f(E // 2)))[None, :]
    sin, cos = np.sin(angle), np.cos(angle)
    rot = np.stack([cos * scale, sin * scale, cos * (f(1) / scale), sin * (f(1) / scale)], axis=1)
    gammas = f(1.0) - f(2.0) ** (f(-5.0) - np.arange(H, dtype=f))
    tok = np.arange(P)
    diff = (tok[None, :] % S - tok[:, None] % S).astype(f)
    same = (tok[None, :] // S == tok[:, None] // S) & (diff >= 0)
    d = np.where(same[None], gammas[:, None, None] ** np.maximum(diff, 0)[None], f(0))
    decay = d.reshape(2, DC, P, P).transpose(2, 0, 1, 3)
    return np.tile(rot, (BPT, 1, 1)).astype(f), decay.astype(f)


def arrays_of(inputs):
    g = {k: np.asarray(v) for k, v in inputs.items()}
    out = {"x": g["x"].reshape(TOK, D)}
    ctx = g["ctx_1024"]
    cT = ctx.transpose(0, 2, 1).reshape(NB, DC, P, SK).transpose(0, 2, 1, 3)
    out["ctx"] = cT.reshape(NB, P, DC * SK)
    last = np.zeros((P, DC, P), np.float32)
    for i in range(3):
        last[:, :, i * NB:(i + 1) * NB] = ctx[:, SK - 1, :].T.reshape(DC, P, NB).transpose(1, 0, 2)
    out["ctx_last"] = last
    for n, k in (("xwq", "Wq"), ("xwk", "Wk"), ("xwv", "Wv"), ("xwo", "Wo")):
        out[n] = chunked(g["L0_xattn_" + k].T)
    thr = g["L0_xattn_raw_thresholds"].reshape(XH)
    vecs = [by_partition(g["L0_xattn_" + k]) for k in ("bq", "bk", "bv")]
    vecs.append(np.repeat(thr.reshape(DC, HPC), XD, axis=1).T)
    vecs.append(np.repeat(np.eye(HPC, dtype=np.float32), XD, axis=0))
    out["vec"] = np.concatenate(vecs, axis=1)
    out["bo_bc"] = np.broadcast_to(g["L0_xattn_bo"], (P, D))
    out["ident"] = np.eye(P, dtype=np.float32)
    out["eye32"] = np.broadcast_to(np.eye(NB, 32, dtype=np.float32), (P, NB, 32))
    split = lambda w: w.transpose(0, 2, 1, 3).reshape(L, D, H, E // 2, 2).transpose(0, 1, 2, 4, 3).reshape(L, D, D)
    wq, wk = split(g["L0_attn_Wq"]), split(g["L0_attn_Wk"])
    wv = g["L0_attn_Wv"].transpose(0, 2, 1, 3).reshape(L, D, D)
    wa = np.concatenate([wq, wk, wv, g["L0_attn_Wg"], g["L0_attn_Wo"]], axis=2)
    out["wa"] = wa.reshape(L, DC, P, 10, 256).transpose(0, 3, 2, 1, 4).reshape(L, 10, P, DC * 256)
    w1 = g["L0_attn_ffn_w1"].reshape(L, DC, P, FC, P).transpose(0, 3, 2, 1, 4).reshape(L, FC, P, D)
    w2 = g["L0_attn_ffn_w2"].reshape(L, FC, P, D)
    out["wf"] = np.concatenate([w1, w2], axis=3)
    out["gn"] = np.broadcast_to(np.stack([g["L0_attn_gn_scale"], g["L0_attn_gn_bias"]], 1)[:, None], (L, P, 2, D))
    out["rot"], out["decay"] = position_tables()
    up, gt, down = g["L0_ffn_w_up"], g["L0_ffn_w_gate"], g["L0_ffn_w_down"]
    pieces = []
    for j in range(2):
        for w in (gt, up):
            pieces.append(w[:, 512 * j:512 * (j + 1), :].transpose(0, 2, 1).reshape(NE, DC, P, 512).transpose(0, 2, 1, 3))
    for j in range(2):
        pieces.append(down[:, :, 512 * j:512 * (j + 1)].transpose(0, 2, 1).reshape(NE, DC, P, D).transpose(0, 2, 1, 3))
    out["we"] = np.stack(pieces, axis=1).reshape(NE, PIECES, P, DC * 512)
    lnv = np.stack([g["L0_attn_" + k].reshape(L, DC, P) for k in ("ln1_scale", "ln1_bias", "ln2_scale", "ln2_bias")], axis=1)
    out["lnv"] = lnv.transpose(0, 3, 1, 2).reshape(L, P, 4 * DC)
    out["rw"] = chunked(g["L0_ffn_router_w"].T)
    col = lambda v: np.broadcast_to(v.astype(np.float32).reshape(-1), (P, v.size))
    i, e = np.arange(P), np.arange(NE)
    out["route_tab"] = np.concatenate([(i[:, None] < i[None, :]).astype(np.float32), np.ones((P, P), np.float32), col(e),
                                       col(e[None, :] < e[:, None]), col(np.arange(NG))], axis=1)
    return {k: np.ascontiguousarray(v) for k, v in out.items()}


def kernel(**inputs):
    import concourse.bacc as bacc
    from concourse.bass_utils import run_bass_kernel_spmd

    nc = bacc.Bacc("TRN2", target_bir_lowering=False, num_devices=1)
    arrays = {f"in_{name}": value for name, value in arrays_of(inputs).items()}
    aps = {name[3:]: nc.dram_tensor(name, value.shape, mybir.dt.from_np(value.dtype), kind="ExternalInput").ap()
           for name, value in arrays.items()}
    out = nc.dram_tensor("out", (TOK, D), F32, kind="ExternalOutput").ap()
    build(nc, aps, out)
    result = run_bass_kernel_spmd(nc, [arrays], core_ids=[0])
    return result.results[0]["out"].reshape(NB, S, D)
```
